# Optimizing a Trainium2 kernel written in Bass

```python
import numpy as np
import jax
import jax.numpy as jnp

def _softmax(x, axis=-1):
    return jax.nn.softmax(x, axis=axis)

def _gelu(x):
    return jax.nn.gelu(x, approximate=True)

def _silu(x):
    return jax.nn.silu(x)

def _sigmoid(x):
    return jax.nn.sigmoid(x)

def _layernorm(x, axis=-1, eps=1e-05):
    m = jnp.mean(x, axis=axis, keepdims=True)
    v = jnp.var(x, axis=axis, keepdims=True)
    return (x - m) / jnp.sqrt(v + eps)

def _scatter_add(tgt, idx, src, axis=0):
    return tgt.at[idx].add(src)

def _segment_sum(src, seg, n):
    return jax.ops.segment_sum(src, seg, n)
kernel_name = 'mk_flamingo_gated_d2_seqx_r8_6b66bd'

def setup_inputs(seed: int=0):
    np.random.seed(seed)
    _w = jnp.asarray

    def _rec_inputs():
        import jax
        import jax.numpy as jnp
        _rk = jax.random.key(seed)
        x = -0.0002928 + 1 * jax.random.normal(jax.random.fold_in(_rk, 1), (8, 56, 128), jnp.float32)
        _lenS = 56 - jax.random.randint(jax.random.fold_in(_rk, 7), (8,), 0, max(1, 56 // 4) + 1, jnp.int32)
        _lenS2 = 1500 - jax.random.randint(jax.random.fold_in(_rk, 8), (8,), 0, max(1, 1500 // 4) + 1, jnp.int32)
        _ctx_1024P = jax.random.normal(jax.random.fold_in(_rk, 11), (8, 16, 128), jnp.float32)
        _ctx_1024c = jax.random.dirichlet(jax.random.fold_in(_rk, 511), 0.3 * jnp.ones((16,), jnp.float32), (8, 1500))
        _ctx_1024t = jnp.einsum('bsk,bkd->bsd', _ctx_1024c, _ctx_1024P)
        _ctx_1024t = _ctx_1024t * jax.lax.rsqrt(jnp.mean(jnp.square(_ctx_1024t)) + 1e-12) * 0.953939
        ctx_1024 = -1.39393e-06 + 0.999914 * (_ctx_1024t + 0.3 * jax.random.normal(jax.random.fold_in(_rk, 611), (8, 1500, 128), jnp.float32))
        _g = jax.random.normal(jax.random.fold_in(_rk, 9001), (2, 2), jnp.float32)
        _g = jnp.sign(_g) * jnp.maximum(jnp.abs(_g), 1.0) + (_g == 0) * 1.0
        g_xattn = _g[0]
        g_ffn = _g[1]
        return (x, ctx_1024, g_xattn, g_ffn)
    x, ctx_1024, g_xattn, g_ffn = _rec_inputs()

    def _L0_xattn_setup():
        import jax, jax.numpy as jnp
        import numpy as np
        import math
        H = 16
        D_MODEL = 128
        D_K = D_MODEL // H

        def _split_heads(x):
            b, s, _ = x.shape
            return x.reshape(b, s, H, D_K).transpose(0, 2, 1, 3)
        key = jax.random.key(seed)
        ks = jax.random.split(key, 11)
        B, S = (2, 256)
        scale = 1.0 / math.sqrt(D_MODEL)
        inp = {'query': jax.random.normal(ks[0], (B, S, D_MODEL), dtype=jnp.float32), 'key': jax.random.normal(ks[1], (B, S, D_MODEL), dtype=jnp.float32), 'value': jax.random.normal(ks[2], (B, S, D_MODEL), dtype=jnp.float32), 'Wq': jax.random.normal(ks[3], (D_MODEL, D_MODEL), dtype=jnp.float32) * scale, 'bq': jnp.zeros((D_MODEL,), dtype=jnp.float32), 'Wk': jax.random.normal(ks[4], (D_MODEL, D_MODEL), dtype=jnp.float32) * scale, 'bk': jnp.zeros((D_MODEL,), dtype=jnp.float32), 'Wv': jax.random.normal(ks[5], (D_MODEL, D_MODEL), dtype=jnp.float32) * scale, 'bv': jnp.zeros((D_MODEL,), dtype=jnp.float32), 'Wo': jax.random.normal(ks[6], (D_MODEL, D_MODEL), dtype=jnp.float32) * scale, 'bo': jnp.zeros((D_MODEL,), dtype=jnp.float32)}
        return inp
    _L0_xattn_all = _L0_xattn_setup()
    _L0_xattn_in = {k: v for k, v in _L0_xattn_all.items() if k in ('Wq', 'bq', 'Wk', 'bk', 'Wv', 'bv', 'Wo', 'bo')}
    del _L0_xattn_all

    def _L0_ffn_setup():
        import jax, jax.numpy as jnp
        import numpy as np
        B, S, D, E, K = (4, 256, 128, 8, 2)
        H = 4 * D
        key = jax.random.key(seed)
        ks = jax.random.split(key, 4)
        sc = lambda n: 1.0 / np.sqrt(n)
        return {'x': jax.random.normal(ks[0], (B, S, D), jnp.float32), 'gate_w': jax.random.normal(ks[1], (D, E), jnp.float32) * sc(D), 'gate_b': jnp.zeros((E,), jnp.float32), 'w1': jax.random.normal(ks[2], (E, D, H), jnp.float32) * sc(D), 'b1': jnp.zeros((E, H), jnp.float32), 'w2': jax.random.normal(ks[3], (E, H, D), jnp.float32) * sc(H), 'b2': jnp.zeros((E, D), jnp.float32)}
    _L0_ffn_all = _L0_ffn_setup()
    _L0_ffn_in = {k: v for k, v in _L0_ffn_all.items() if k in ('gate_w', 'gate_b', 'w1', 'b1', 'w2', 'b2')}
    del _L0_ffn_all

    def _L1_xattn_setup():
        import jax, jax.numpy as jnp
        import numpy as np
        DIM = 128
        CTX_DIM = 128
        HEADS = 16
        DIM_HEAD = 64
        INNER = HEADS * DIM_HEAD
        FF_INNER = 4 * DIM
        EPS = 1e-05

        def layer_norm(x, g, b):
            mu = jnp.mean(x, axis=-1, keepdims=True)
            var = jnp.var(x, axis=-1, keepdims=True)
            return (x - mu) * jax.lax.rsqrt(var + EPS) * g + b
        key = jax.random.key(seed)
        ks = jax.random.split(key, 9)
        b, n, j = (4, 256, 128)
        inp = {'x': jax.random.normal(ks[0], (b, n, DIM), dtype=jnp.float32), 'context': jax.random.normal(ks[1], (b, j, CTX_DIM), dtype=jnp.float32), 'ln_g': jnp.ones((DIM,), jnp.float32), 'ln_b': jnp.zeros((DIM,), jnp.float32), 'cln_g': jnp.ones((CTX_DIM,), jnp.float32), 'cln_b': jnp.zeros((CTX_DIM,), jnp.float32), 'Wq': jax.random.normal(ks[2], (DIM, INNER), dtype=jnp.float32) * DIM ** (-0.5), 'Wkv': jax.random.normal(ks[3], (CTX_DIM, 2 * DIM_HEAD), dtype=jnp.float32) * CTX_DIM ** (-0.5), 'Wo': jax.random.normal(ks[4], (INNER, DIM), dtype=jnp.float32) * INNER ** (-0.5), 'Wff1': jax.random.normal(ks[5], (DIM, 2 * FF_INNER), dtype=jnp.float32) * DIM ** (-0.5), 'Wff2': jax.random.normal(ks[6], (FF_INNER, DIM), dtype=jnp.float32) * FF_INNER ** (-0.5)}
        return inp
    _L1_xattn_all = _L1_xattn_setup()
    _L1_xattn_in = {k: v for k, v in _L1_xattn_all.items() if k in ('ln_g', 'ln_b', 'cln_g', 'cln_b', 'Wq', 'Wkv', 'Wo', 'Wff1', 'Wff2')}
    del _L1_xattn_all

    def _L1_ffn_setup():
        import jax, jax.numpy as jnp
        import numpy as np
        B, S, D_MODEL, D_HIDDEN = (4, 256, 128, 512)

        def act_quant(x):
            scale = 127.0 / jnp.clip(jnp.max(jnp.abs(x), axis=-1, keepdims=True), 1e-05)
            return jnp.clip(jnp.round(x * scale), -128, 127) / scale

        def weight_quant(w):
            scale = 1.0 / jnp.clip(jnp.mean(jnp.abs(w)), 1e-05)
            return jnp.clip(jnp.round(w * scale), -1, 1) / scale

        def bit_linear(x, w):
            xq = x + jax.lax.stop_gradient(act_quant(x) - x)
            wq = w + jax.lax.stop_gradient(weight_quant(w) - w)
            return jnp.einsum('bsd,hd->bsh', xq, wq)

        def depthwise_conv1d(x_bcl, w, b):
            y = jax.lax.conv_general_dilated(x_bcl, w, window_strides=(1,), padding=[(1, 1)], dimension_numbers=('NCH', 'OIH', 'NCH'), feature_group_count=x_bcl.shape[1])
            return y + b[None, :, None]
        key = jax.random.key(seed)
        ks = jax.random.split(key, 5)
        lim1 = 1.0 / np.sqrt(D_MODEL)
        lim2 = 1.0 / np.sqrt(D_HIDDEN)
        limc = 1.0 / np.sqrt(3.0)
        return {'x': jax.random.normal(ks[0], (B, S, D_MODEL), dtype=jnp.float32), 'w1': jax.random.uniform(ks[1], (D_HIDDEN, D_MODEL), jnp.float32, -lim1, lim1), 'conv_w': jax.random.uniform(ks[2], (D_HIDDEN, 1, 3), jnp.float32, -limc, limc), 'conv_b': jax.random.uniform(ks[3], (D_HIDDEN,), jnp.float32, -limc, limc), 'w2': jax.random.uniform(ks[4], (D_MODEL, D_HIDDEN), jnp.float32, -lim2, lim2)}
    _L1_ffn_all = _L1_ffn_setup()
    _L1_ffn_in = {k: v for k, v in _L1_ffn_all.items() if k in ('w1', 'conv_w', 'conv_b', 'w2')}
    del _L1_ffn_all
    return {'x': x, 'ctx_1024': ctx_1024, 'g_xattn': g_xattn, 'g_ffn': g_ffn, 'L0_xattn_Wq': _L0_xattn_in['Wq'], 'L0_xattn_bq': _L0_xattn_in['bq'], 'L0_xattn_Wk': _L0_xattn_in['Wk'], 'L0_xattn_bk': _L0_xattn_in['bk'], 'L0_xattn_Wv': _L0_xattn_in['Wv'], 'L0_xattn_bv': _L0_xattn_in['bv'], 'L0_xattn_Wo': _L0_xattn_in['Wo'], 'L0_xattn_bo': _L0_xattn_in['bo'], 'L0_ffn_gate_w': _L0_ffn_in['gate_w'], 'L0_ffn_gate_b': _L0_ffn_in['gate_b'], 'L0_ffn_w1': _L0_ffn_in['w1'], 'L0_ffn_b1': _L0_ffn_in['b1'], 'L0_ffn_w2': _L0_ffn_in['w2'], 'L0_ffn_b2': _L0_ffn_in['b2'], 'L1_xattn_ln_g': _L1_xattn_in['ln_g'], 'L1_xattn_ln_b': _L1_xattn_in['ln_b'], 'L1_xattn_cln_g': _L1_xattn_in['cln_g'], 'L1_xattn_cln_b': _L1_xattn_in['cln_b'], 'L1_xattn_Wq': _L1_xattn_in['Wq'], 'L1_xattn_Wkv': _L1_xattn_in['Wkv'], 'L1_xattn_Wo': _L1_xattn_in['Wo'], 'L1_xattn_Wff1': _L1_xattn_in['Wff1'], 'L1_xattn_Wff2': _L1_xattn_in['Wff2'], 'L1_ffn_w1': _L1_ffn_in['w1'], 'L1_ffn_conv_w': _L1_ffn_in['conv_w'], 'L1_ffn_conv_b': _L1_ffn_in['conv_b'], 'L1_ffn_w2': _L1_ffn_in['w2']}

def reference(x, ctx_1024, g_xattn, g_ffn, L0_xattn_Wq, L0_xattn_bq, L0_xattn_Wk, L0_xattn_bk, L0_xattn_Wv, L0_xattn_bv, L0_xattn_Wo, L0_xattn_bo, L0_ffn_gate_w, L0_ffn_gate_b, L0_ffn_w1, L0_ffn_b1, L0_ffn_w2, L0_ffn_b2, L1_xattn_ln_g, L1_xattn_ln_b, L1_xattn_cln_g, L1_xattn_cln_b, L1_xattn_Wq, L1_xattn_Wkv, L1_xattn_Wo, L1_xattn_Wff1, L1_xattn_Wff2, L1_ffn_w1, L1_ffn_conv_w, L1_ffn_conv_b, L1_ffn_w2):
    import jax
    import jax.numpy as jnp

    def _L0_xattn_ref(query, key, value, Wq, bq, Wk, bk, Wv, bv, Wo, bo):
        import jax, jax.numpy as jnp
        import numpy as np
        import math
        H = 16
        D_MODEL = 128
        D_K = D_MODEL // H

        def _split_heads(x):
            b, s, _ = x.shape
            return x.reshape(b, s, H, D_K).transpose(0, 2, 1, 3)
        q = _split_heads(query @ Wq.T + bq)
        k = _split_heads(key @ Wk.T + bk)
        v = _split_heads(value @ Wv.T + bv)
        scores = jnp.einsum('bhqd,bhkd->bhqk', q, k) / math.sqrt(D_K)
        attn = jax.nn.softmax(scores, axis=-1)
        ctx = jnp.einsum('bhqk,bhkd->bhqd', attn, v)
        b, h, s, d = ctx.shape
        ctx = ctx.transpose(0, 2, 1, 3).reshape(b, s, h * d)
        return ctx @ Wo.T + bo

    def _L0_ffn_ref(x, gate_w, gate_b, w1, b1, w2, b2):
        import jax, jax.numpy as jnp
        import numpy as np
        B, S, D, E, K = (4, 256, 128, 8, 2)
        H = 4 * D
        Bx, Sx, Dx = x.shape
        n_exp = w1.shape[0]
        logits = jnp.einsum('bsd,de->bse', x, gate_w) + gate_b
        scores = jax.nn.softmax(logits, axis=-1)
        topk_s, topk_i = jax.lax.top_k(scores, K)
        onehot = jax.nn.one_hot(topk_i, n_exp, dtype=scores.dtype)
        dispatch = jnp.einsum('bske,bsk->bse', onehot, topk_s)
        xf = x.reshape(-1, Dx)
        wf = dispatch.reshape(-1, n_exp)
        out = jnp.zeros_like(xf)
        for i in range(n_exp):
            wi = wf[:, i:i + 1]
            h = jax.nn.relu(xf * wi @ w1[i] + b1[i])
            y = h @ w2[i] + b2[i]
            out = jnp.where(wi > 0, y, out)
        return out.reshape(Bx, Sx, Dx)

    def _L1_xattn_ref(x, context, ln_g, ln_b, cln_g, cln_b, Wq, Wkv, Wo, Wff1, Wff2):
        import jax, jax.numpy as jnp
        import numpy as np
        DIM = 128
        CTX_DIM = 128
        HEADS = 16
        DIM_HEAD = 64
        INNER = HEADS * DIM_HEAD
        FF_INNER = 4 * DIM
        EPS = 1e-05

        def layer_norm(x, g, b):
            mu = jnp.mean(x, axis=-1, keepdims=True)
            var = jnp.var(x, axis=-1, keepdims=True)
            return (x - mu) * jax.lax.rsqrt(var + EPS) * g + b
        scale = DIM_HEAD ** (-0.5)
        xn = layer_norm(x, ln_g, ln_b)
        cn = layer_norm(context, cln_g, cln_b)
        b, n, _ = xn.shape
        q = (xn @ Wq).reshape(b, n, HEADS, DIM_HEAD).transpose(0, 2, 1, 3) * scale
        kv = cn @ Wkv
        k, v = (kv[..., :DIM_HEAD], kv[..., DIM_HEAD:])
        sim = jnp.einsum('bhid,bjd->bhij', q, k)
        attn = jax.nn.softmax(sim, axis=-1)
        out = jnp.einsum('bhij,bjd->bhid', attn, v)
        out = out.transpose(0, 2, 1, 3).reshape(b, n, INNER) @ Wo
        ff = xn @ Wff1
        h, gate = (ff[..., :FF_INNER], ff[..., FF_INNER:])
        out = out + jax.nn.silu(gate) * h @ Wff2
        return out

    def _L1_ffn_ref(x, w1, conv_w, conv_b, w2):
        import jax, jax.numpy as jnp
        import numpy as np
        B, S, D_MODEL, D_HIDDEN = (4, 256, 128, 512)

        def act_quant(x):
            scale = 127.0 / jnp.clip(jnp.max(jnp.abs(x), axis=-1, keepdims=True), 1e-05)
            return jnp.clip(jnp.round(x * scale), -128, 127) / scale

        def weight_quant(w):
            scale = 1.0 / jnp.clip(jnp.mean(jnp.abs(w)), 1e-05)
            return jnp.clip(jnp.round(w * scale), -1, 1) / scale

        def bit_linear(x, w):
            xq = x + jax.lax.stop_gradient(act_quant(x) - x)
            wq = w + jax.lax.stop_gradient(weight_quant(w) - w)
            return jnp.einsum('bsd,hd->bsh', xq, wq)

        def depthwise_conv1d(x_bcl, w, b):
            y = jax.lax.conv_general_dilated(x_bcl, w, window_strides=(1,), padding=[(1, 1)], dimension_numbers=('NCH', 'OIH', 'NCH'), feature_group_count=x_bcl.shape[1])
            return y + b[None, :, None]
        h = bit_linear(x, w1)
        h = depthwise_conv1d(h.transpose(0, 2, 1), conv_w, conv_b)
        h = h.transpose(0, 2, 1)
        h = jax.nn.silu(h)
        return bit_linear(h, w2)
    x = x + jnp.tanh(g_xattn[0]) * _L0_xattn_ref(_layernorm(x, axis=-1), ctx_1024, ctx_1024, L0_xattn_Wq, L0_xattn_bq, L0_xattn_Wk, L0_xattn_bk, L0_xattn_Wv, L0_xattn_bv, L0_xattn_Wo, L0_xattn_bo)
    x = x + jnp.tanh(g_ffn[0]) * _L0_ffn_ref(_layernorm(x, axis=-1), L0_ffn_gate_w, L0_ffn_gate_b, L0_ffn_w1, L0_ffn_b1, L0_ffn_w2, L0_ffn_b2)
    x = x + jnp.tanh(g_xattn[1]) * _L1_xattn_ref(_layernorm(x, axis=-1), ctx_1024, L1_xattn_ln_g, L1_xattn_ln_b, L1_xattn_cln_g, L1_xattn_cln_b, L1_xattn_Wq, L1_xattn_Wkv, L1_xattn_Wo, L1_xattn_Wff1, L1_xattn_Wff2)
    x = x + jnp.tanh(g_ffn[1]) * _L1_ffn_ref(_layernorm(x, axis=-1), L1_ffn_w1, L1_ffn_conv_w, L1_ffn_conv_b, L1_ffn_w2)
    return x

_drawn_inputs = setup_inputs


def setup_inputs(seed=0):
    import zlib

    import numpy as np

    out = dict(_drawn_inputs(seed))
    spreads = {'g_ffn': (-1.0, 0.2),
     'L0_xattn_bq': (0.0, 0.1),
     'L0_xattn_bk': (0.0, 0.1),
     'L0_xattn_bv': (0.0, 0.1),
     'L0_xattn_bo': (0.0, 0.1),
     'L0_ffn_gate_b': (0.0, 0.1),
     'L0_ffn_b1': (0.0, 0.1),
     'L0_ffn_b2': (0.0, 0.1),
     'L1_xattn_ln_g': (1.0, 0.2),
     'L1_xattn_ln_b': (0.0, 0.1),
     'L1_xattn_cln_g': (1.0, 0.2),
     'L1_xattn_cln_b': (0.0, 0.1)}
    factors = {}
    for name, (base, spread) in spreads.items():
        noise = np.random.default_rng([zlib.crc32(name.encode()), seed]).standard_normal(out[name].shape)
        drawn = base * np.exp(spread * noise) if base else spread * noise
        out[name] = jnp.asarray(drawn.astype(out[name].dtype))
    for name, factor in factors.items():
        out[name] = (out[name] * factor).astype(out[name].dtype)
    return out
```

```python
import concourse.bass as bass
from concourse import mybir
from contextlib import ExitStack

B, S, D = 8, 56, 128
NK = 1500
H = 16
KT, NT = 125, 12
HS = H * S
HALF = HS // 2
RT = 2 * S
NRT = HS // RT
TOK = B * S
NTT = TOK // RT
CH, NCH = 500, 3
TPC = CH // KT
NMC = NRT * NCH
NH2 = 2 * NT
DK0, DK1 = 8, 64
NE, FF = 8, 512
FC = FF // 128
EPS = 1e-5
RING_S, RING_P = 3, 4
ROUND = 12582912.0

MAX_PLAN = [0, 0, 2, 3, 2, 3, 2, 2, 3, 2, 3, 2]
assert sum(MAX_PLAN) == NMC

fp32 = mybir.dt.float32
bf16 = mybir.dt.bfloat16
ALU = mybir.AluOpType
ACT = mybir.ActivationFunctionType
AX = mybir.AxisListType


def need(eng, sem, value):
    if isinstance(value, int) and value <= 0:
        return
    eng.wait_ge(sem, value)


def ctx_count(b, par):
    return 8 * (b - par) + 16


def build(nc, t, out):
    ctx = ExitStack()
    with ctx:
        ctx.enter_context(nc.allow_non_contiguous_dma(reason="biases, a few hundred values each"))
        def sb(name, shape, dt=fp32):
            return ctx.enter_context(nc.sbuf_tensor(name, shape, dt))

        def sem(name):
            return ctx.enter_context(nc.semaphore(name))

        bank = [ctx.enter_context(nc.psum_tensor(f"bank{i}", [128, 512], fp32)) for i in range(8)]
        prep_bank = [bank[0], bank[1], bank[7]]
        score_bank = [bank[2], bank[3], bank[4]]
        acc_bank = [bank[5], bank[6]]

        ident = sb("ident", [128, 128])
        identb = sb("identb", [128, 128], bf16)
        ones = sb("ones", [128, 128])
        qmask = sb("qmask", [128, 4])
        mmask0 = sb("mmask0", [RT, 2, 32])
        mmask1 = sb("mmask1", [RT, 32])
        sumsel = sb("sumsel", [128, 128])
        iota8 = sb("iota8", [RT, NTT, NE])
        iota1 = sb("iota1", [RT, NTT, NE])
        gates = sb("gates", [128, 4])
        tgates = sb("tgates", [128, 4])
        wkT = sb("wkT", [128, 128])
        wvT = sb("wvT", [128, 128])
        wq0 = sb("wq0", [128, 4, 4, 32])
        bq0 = sb("bq0", [128, 4])
        bk0 = sb("bk0", [128, 1])
        bv_bc = sb("bv_bc", [128, 128])
        bo_bc = sb("bo_bc", [128, 128])
        wo0 = sb("wo0", [128, 2, 2, 128])
        gate_w = sb("gate_w", [128, NE])
        gb_bc = sb("gb_bc", [128, NE])
        w1 = sb("w1", [128, NE, FF])
        b1 = sb("b1", [128, NE, FC])
        w2 = sb("w2", [128, NE, FC, 128])
        b2 = sb("b2", [NE, 128])
        wk1 = sb("wk1", [128, 2, DK1])
        wv1 = sb("wv1", [128, 128])
        wq1 = sb("wq1", [128, H, 2, DK1])
        wo1 = sb("wo1", [128, H // 2, 128])
        wff1 = sb("wff1", [128, 2 * FC, 128])
        wff2 = sb("wff2", [128, FC, 128])
        lng = sb("lng", [128, 4])
        bw1 = sb("bw1", [128, FF])
        bw2 = sb("bw2", [128, FC, 128])
        bw2t = sb("bw2t", [128, FC, 128], bf16)
        convw = sb("convw", [128, FC, 3])
        convb = sb("convb", [128, FC])
        ctxN = sb("ctxN", [KT, 2, NT, 128])
        xT = sb("xT", [128, NK])
        cn = w1[0:KT].rearrange("p e f -> p (e f)")[:, 0:2 * NT * 128].rearrange("p (a t d) -> p a t d", a=2, d=128)
        khi = sb("khi", [128, NK], bf16)
        klo = sb("klo", [128, NK], bf16)
        KS = sb("KS", [128, 2, 4, NK], bf16)
        VS = sb("VS", [KT, 2, NT, 256])
        QS = sb("QS", [128, B, HS], bf16)
        QB = sb("QB", [128, B, HS], bf16)
        P = sb("P", [KT, RING_P, HALF])
        O2 = sb("O2", [128, H // 2, TOK])
        mxc = sb("mxc", [RT, NMC])
        mx = sb("mx", [RT, NRT])
        MB = sb("MB", [RT, NRT, 32], bf16)
        rsum = sb("rsum", [64, 2, HALF])
        st6 = sb("st6", [128, NT, 6])
        st1 = sb("st1", [128, 12, NT])
        x = sb("x", [RT, NTT, 128])
        z = sb("z", [RT, NTT, 128])
        zT = sb("zT", [128, TOK])
        hT = QB[:].rearrange("p b n -> p (b n)").bitcast(fp32).rearrange("p (a c n) -> p a c n", a=2, c=FC)
        xw = P[0:RT].rearrange("p a n -> p (a n)")[:, 0:2 * NTT * 128].rearrange("p (a i d) -> p a i d", a=2, d=128)
        xwT = xT[:, 0:2 * TOK].rearrange("p (a n) -> p a n", a=2)
        uT = w2[:].rearrange("p e c d -> p (e c d)")[:, 0:2 * FC * TOK].rearrange("p (a c n) -> p a c n", a=2, c=FC)

        def sT(c):
            free = KS[:, c // 2, 2:4, :].rearrange("p a n -> p (a n)").bitcast(fp32)
            return free[:, c % 2 * TOK:c % 2 * TOK + TOK]

        sm = sb("sm", [RT, 12, NTT, NE])
        sm1 = sb("sm1", [128, 24, NTT])
        dispT = rsum[0:NE, 0, :]
        moe = sb("moe", [RT, NTT, 128])
        qsT = sb("qsT", [128, TOK], bf16)
        wqs = sb("wqs", [128, 8])

        const_in, w_in, moe_in, x_in, bc_in = sem("const_in"), sem("w_in"), sem("moe_in"), sem("x_in"), sem("bc_in")
        fill = sem("fill")
        E = {k: sem(k) for k in ("""tanh_ready acc_divided b2_done back_tr conv_done conv_exp dispT_ready disp_tr expert_added expert_out
                                 ff_exp ff_proj ff_silu final_done gate_exp hidden_ready hqT_ready hq_ready hq_tr
                                 identb_ready lin1_done lin2_done logit_ready logits_done out1_done q0_hi q0_proj
                                 q0_stacked q1_hi q1_lo q1_proj rstd_est silu_done sums_done tok_tr up_done var_log
                                 var_ready vector_chain wabs_ready winner_ready wmean_done wo0_done xq_ready xwT_ready
                                 xw_ready xw_tr zT_ready z_ready""").split()}
        out_done = sem("out_done")

        def attention_sems(n):
            names = ("stats_v", "stats_a", "rstd", "centred", "cn_ready", "tr_done", "tr_evac_a", "tr_evac_v",
                     "kproj", "khi_ready", "klo_ready", "khi_copied", "vproj", "v_ready", "stacked", "max_scores", "max_taken",
                     "max_final", "max_block", "max_row", "max_in_q", "scores", "exps", "pv", "acc_read",
                     "sum_rec", "normed")
            return {k: sem(f"{k}_{n}") for k in names} | {f"ctx_in{par}": sem(f"ctx_in{par}_{n}") for par in range(2)}

        A0, A1 = attention_sems(0), attention_sems(1)

        block = ctx.enter_context(nc.Block())
        ctx_h = t["ctx_1024"].rearrange("b (p t) d -> b p t d", t=NT)
        NCONST, NW, NMOE, NX, NBC = [0], [0], [0], [0], [0]
        counts = {"const_in": 0, "w_in": 0, "moe_in": 0, "x_in": 0}

        @block.sync
        def _(sp):
            def load(dst, src, s, key):
                sp.dma_start(dst, src).then_inc(s, 16)
                counts[key] += 16

            load(x[:], t["x"].rearrange("(n b) s d -> (b s) n d", b=2), x_in, "x_in")
            load(ident[:], t["c_ident"], x_in, "x_in")
            sp.dma_start(ctxN[:, 0], ctx_h[0]).then_inc(A0["ctx_in0"], 16)
            load(wkT[:], t["wkT"], w_in, "w_in")
            load(wvT[:], t["wvT"], w_in, "w_in")
            sp.wait_ge(fill, 1)
            for r in range(3):
                load(wq0[:, :, r, :], t["wqT"].rearrange("d (g n) -> d g n", g=4), w_in, "w_in")
                load(bq0[32 * r:32 * r + 32, :], t["L0_xattn_bq"].rearrange("(g p) -> p g", p=32), w_in, "w_in")
            load(bk0[:], t["L0_xattn_bk"].rearrange("(p o) -> p o", o=1), w_in, "w_in")
            load(qmask[:], t["c_qmask"], w_in, "w_in")
            load(mmask0[:], t["c_mmask0"], w_in, "w_in")
            load(mmask1[:], t["c_mmask1"], w_in, "w_in")
            load(sumsel[:], t["c_sumsel"], w_in, "w_in")
            load(iota8[:], t["c_iota8"], w_in, "w_in")
            load(iota1[:], t["c_iota1"], w_in, "w_in")
            load(bv_bc[:], t["L0_xattn_bv"].partition_broadcast(128), w_in, "w_in")
            load(gates[:, 0:2], t["g_xattn"].partition_broadcast(128), w_in, "w_in")
            load(gates[:, 2:4], t["g_ffn"].partition_broadcast(128), w_in, "w_in")
            sp.dma_start(ctxN[:, 1], ctx_h[1]).then_inc(A0["ctx_in1"], 16)

            def stack(b, par):
                need(sp, A0["khi_ready"], NCH * (b + 1))
                need(sp, A0["klo_ready"], NCH * (b + 1))
                for g in range(4):
                    rows = slice(32 * g, 32 * g + 32)
                    for r, src in enumerate((khi, khi, klo)):
                        sp.dma_start(KS[32 * r:32 * r + 32, par, g, :], src[rows, :]).then_inc(A0["stacked"], 16)

            def fetch(b, par):
                need(sp, A0["tr_done"], NCH * (b - 1))
                sp.dma_start(ctxN[:, par], ctx_h[bass.ds(b, 1)].rearrange("o p t d -> p (o t) d")).then_inc(A0[f"ctx_in{par}"], 16)

            stack(0, 0)
            fetch(2, 0)
            stack(1, 1)
            for dst, src in ((gate_w, t["L0_ffn_gate_w"]), (gb_bc, t["L0_ffn_gate_b"].partition_broadcast(128)),
                             (b2, t["L0_ffn_b2"]), (bo_bc, t["L0_xattn_bo"].partition_broadcast(128))):
                load(dst[:], src, moe_in, "moe_in")
            for half in range(2):
                for j in range(2):
                    for c in range(4):
                        h = 8 * half + 2 * c + j
                        load(wo0[32 * c + 8 * j:32 * c + 8 * j + 8, half, j, :], t["woT"][8 * h:8 * h + 8, :], moe_in, "moe_in")
            load(w1[:], t["L0_ffn_w1"].rearrange("e d h -> d e h"), moe_in, "moe_in")
            load(b1[:], t["L0_ffn_b1"].rearrange("e (c p) -> p e c", p=128), moe_in, "moe_in")
            load(w2[:], t["L0_ffn_w2"].rearrange("e (c p) d -> p e c d", p=128), moe_in, "moe_in")
            fetch(3, 1)
            with sp.Fori(1, B // 2 - 1) as pair:
                for j in range(2):
                    stack(2 * pair + j, j)
                    fetch(2 * pair + j + 2, j)
            stack(B - 2, 0)
            stack(B - 1, 1)
            for j in range(2):
                sp.dma_start(wk1[:, j, :], t["L1_xattn_Wkv"][:, 0:DK1]).then_inc(bc_in, 16)
                sp.dma_start(wq1[:, :, j, :], t["L1_xattn_Wq"].rearrange("d (h e) -> d h e", h=H)).then_inc(bc_in, 16)
            for dst, src in ((wv1, t["L1_xattn_Wkv"]), (wo1, t["L1_xattn_Wo"].rearrange("(a p) d -> p a d", p=128)),
                             (wff1, t["L1_xattn_Wff1"].rearrange("d (c n) -> d c n", n=128)),
                             (wff2, t["L1_xattn_Wff2"].rearrange("(c p) d -> p c d", p=128)),
                             (bw1, t["bw1T"]), (bw2, t["bw2T"].rearrange("(c p) d -> p c d", p=128)),
                             (convw, t["L1_ffn_conv_w"].rearrange("(c p) o k -> p c (o k)", p=128)),
                             (convb, t["L1_ffn_conv_b"].rearrange("(c p) -> p c", p=128))):
                sp.dma_start(dst[:], src).then_inc(bc_in, 16)
            for j, k in enumerate(("ln_g", "ln_b", "cln_g", "cln_b")):
                sp.dma_start(lng[:, j:j + 1], t["L1_xattn_" + k].rearrange("(p o) -> p o", o=1)).then_inc(bc_in, 16)
            sp.wait_ge(A0["tr_done"], NCH * B)
            for b in range(2):
                sp.dma_start(ctxN[:, b], ctx_h[b]).then_inc(A1[f"ctx_in{b}"], 16)

            def fetch1(b, par):
                need(sp, A1["cn_ready"], b - 1)
                sp.dma_start(ctxN[:, par], ctx_h[bass.ds(b, 1)].rearrange("o p t d -> p (o t) d")).then_inc(A1[f"ctx_in{par}"], 16)

            with sp.Fori(1, B // 2) as pair:
                for j in range(2):
                    fetch1(2 * pair + j, j)
            sp.wait_ge(E["final_done"], NTT)
            sp.dma_start(out.rearrange("(n b) s d -> (b s) n d", b=2), x[:]).then_inc(out_done, 16)
            sp.wait_ge(out_done, 16)

        BC_IN = 16 * (2 * 2 + 8 + 4)

        @block.gpsimd
        def _(pool):
            filled = [0]

            def put(dst, value):
                nc.gpsimd.memset(dst, value).then_inc(fill, 1)
                filled[0] += 1
                pool.wait_ge(fill, filled[0])

            put(wq0[:], 0.0)
            put(bq0[96:128, :], 0.0)
            put(ones[:], 1.0)
            put(KS[96:128], 0.0)
            put(VS[:], 0.0)
            put(wo0[:], 0.0)
            put(KS[96:100], 1.0)
            for par in range(2):
                put(VS[:, par].rearrange("p t (a n) -> p (t a) n", n=32)[:, :, 16:17], 1.0)
            pool.wait_ge(A0["pv"], NH2 * B)
            put(KS[64:128, :, 1, :], 0.0)
            put(VS[:, :, :, DK1:128], 1.0)
            pool.wait_ge(E["expert_out"], NE)
            put(QB[64:128], 0.0)
            put(KS[64:65, :, 1, :], 1.0)

            def normalise(b, par):
                need(pool, A1["rstd"], b + 1)
                need(pool, A1["tr_done"], NCH * (b - 1))
                mean = st1[0:KT, 6 * par, :, None].broadcast_to([KT, NT, 128])
                rstd = st1[0:KT, 6 * par + 5, :, None].broadcast_to([KT, NT, 128])
                nc.gpsimd.tensor_tensor(cn[:, par], ctxN[:, par], mean, ALU.subtract).then_inc(A1["centred"], 1)
                need(pool, A1["centred"], b + 1)
                nc.gpsimd.tensor_tensor(cn[:, par], cn[:, par], rstd, ALU.mult).then_inc(A1["cn_ready"], 1)

            pool.wait_ge(E["expert_out"], NE)
            for b in range(2):
                normalise(b, b)
            with pool.Fori(1, B // 2) as pair:
                for j in range(2):
                    normalise(2 * pair + j, j)

        @block.vector
        def _(v):
            count = {}

            def signal(ins, key="vector_chain"):
                count[key] = count.get(key, 0) + 1
                ins.then_inc(E[key], 1)

            def link(ins, key="vector_chain"):
                signal(ins, key)
                v.wait_ge(E[key], count[key])

            def layernorm(src, dst, k):
                for i in range(NTT):
                    last = nc.vector.bn_stats(st6[0:RT, i, :], src[:, i, :])
                link(last)
                for i in range(NTT):
                    last = nc.vector.bn_aggr(sm1[0:RT, 0:2, i], st6[0:RT, i, :])
                link(last)
                link(nc.vector.tensor_scalar(sm1[0:RT, 2, :], sm1[0:RT, 1, :], EPS, None, ALU.add), "var_ready")
                v.wait_ge(E["rstd_est"], k + 1)
                newton(sm1[0:RT, 2, :], sm1[0:RT, 4, :], sm1[0:RT, 5, :], link)
                for i in range(NTT):
                    last = nc.vector.tensor_scalar(dst[:, i, :], src[:, i, :], sm1[0:RT, 0, i:i + 1], sm1[0:RT, 4, i:i + 1],
                                                   ALU.subtract, ALU.mult)
                link(last, "z_ready")

            def newton(var, r, tmp, step):
                step(nc.vector.tensor_tensor(tmp, var, r, ALU.mult))
                step(nc.vector.tensor_tensor(tmp, tmp, r, ALU.mult))
                step(nc.vector.tensor_scalar(tmp, tmp, -0.5, 1.5, ALU.mult, ALU.add))
                step(nc.vector.tensor_tensor(r, r, tmp, ALU.mult))

            v.wait_ge(x_in, counts["x_in"])
            layernorm(x, z, 0)
            signal(nc.vector.tensor_copy(identb[:], ident[:]), "identb_ready")
            v.wait_ge(w_in, counts["w_in"])
            for g in range(4):
                v.wait_ge(E["q0_hi"], g + 1)
                src = prep_bank[g % 3]
                link(nc.vector.scalar_tensor_tensor(qsT[32:64, :], src[32:64, 0:TOK], bq0[32:64, g:g + 1], qsT[32:64, :],
                                                    ALU.add, ALU.subtract))
                for j in range(4):
                    dst = QS[:].rearrange("p b (g j q) -> p b g j q", g=4, j=4)[:, :, g, j, :]
                    last = nc.vector.tensor_scalar(dst, qsT[:].rearrange("p (b q) -> p b q", b=B), qmask[:, j:j + 1], None,
                                                   ALU.mult)
                link(last, "q0_stacked")

            def maxima(A, b, mask, rows):
                for c in range(NMC):
                    need(v, A["max_scores"], NMC * b + c + 1)
                    nc.vector.tensor_reduce(mxc[:, c:c + 1], bank[c % 2][0:RT, 0:CH], AX.X, ALU.max).then_inc(A["max_taken"], 1)
                need(v, A["max_taken"], NMC * (b + 1))
                nc.vector.tensor_reduce(mx[:], mxc[:].rearrange("p (r c) -> p r c", c=NCH), AX.X, ALU.max)\
                    .then_inc(A["max_final"], 1)
                need(v, A["max_final"], b + 1)
                need(v, A["max_row"], 2 * b)
                nc.vector.tensor_tensor(MB[:].rearrange("p (a c) n -> p a c n", c=2),
                                        mx[:].rearrange("p (a c) -> p a c", c=2)[:, :, :, None].broadcast_to([RT, NRT // 2, 2, 32]),
                                        mask, ALU.mult).then_inc(A["max_block"], 1)
                dst = QS if rows == 96 else QB
                for half in range(2):
                    need(v, A["max_row"], 2 * b + half + 1)
                    nc.vector.tensor_copy(dst[rows:rows + 32, bass.ds(b, 1), half * HALF:half * HALF + HALF]
                                          .rearrange("p o n -> p (o n)"),
                                          (bank[7], bank[0])[half][rows:rows + 32, 0:HALF]).then_inc(A["max_in_q"], 1)

            def prep0(b, par):
                A = A0
                need(v, A["tr_done"], NCH * b + 2)
                nc.vector.tensor_copy(xT[:, CH:2 * CH], prep_bank[1][:, 0:CH]).then_inc(A["tr_evac_v"], 1)
                for c in range(NCH):
                    need(v, A["khi_ready"], NCH * b + c + 1)
                    cols = slice(c * CH, c * CH + CH)
                    nc.vector.scalar_tensor_tensor(klo[:, cols], prep_bank[c][:, 0:CH], bk0[:, 0:1], khi[:, cols],
                                                   ALU.add, ALU.subtract).then_inc(A["klo_ready"], 1)
                for c in range(NCH):
                    need(v, A["vproj"], NCH * b + c + 1)
                    nc.vector.tensor_tensor(
                        VS[:, par, c * TPC:c * TPC + TPC, :].rearrange("p t (a n) -> p t a n", n=32)[:, :, :, 0:16],
                        prep_bank[c][0:KT, :].rearrange("p (t a n) -> p t a n", t=TPC, n=16),
                        bv_bc[0:KT, :].rearrange("p (a n) -> p a n", n=16)[:, None, :, :].broadcast_to([KT, TPC, 8, 16]),
                        ALU.add).then_inc(A["v_ready"], 1)

            mask0 = mmask0[:][:, None, :, :].broadcast_to([RT, NRT // 2, 2, 32])
            mask1 = mmask1[:][:, None, None, :].broadcast_to([RT, NRT // 2, 2, 32])
            v.wait_ge(fill, 9)
            for b in range(2):
                prep0(b, b)
                maxima(A0, b, mask0, 96)
            with v.Fori(1, B // 2) as pair:
                for j in range(2):
                    prep0(2 * pair + j, j)
                    maxima(A0, 2 * pair + j, mask0, 96)

            v.wait_ge(E["tanh_ready"], 1)
            v.wait_ge(moe_in, counts["moe_in"])
            for c in range(4):
                v.wait_ge(E["sums_done"], c + 1)
                r = hT[:, 0, c, :]
                link(nc.vector.reciprocal(r, prep_bank[c % 3][:, 0:448]))
                a = O2[:, c, :]
                link(nc.vector.tensor_tensor(a, a, r, ALU.mult), "acc_divided")
            v.wait_ge(E["wo0_done"], 1)
            ob = moe[:]
            link(nc.vector.tensor_tensor(ob, bank[2][0:RT, :].rearrange("p (i d) -> p i d", i=NTT),
                                         bo_bc[0:RT, None, :].broadcast_to([RT, NTT, 128]), ALU.add))
            link(nc.vector.scalar_tensor_tensor(x[:], ob, tgates[0:RT, 0:1], x[:], ALU.mult, ALU.add))

            layernorm(x, z, 1)
            v.wait_ge(E["logits_done"], 1)
            L, E_, s1, s2, o1, o2, w_, m_, t_ = (sm[:, k] for k in range(9))

            def col(k):
                return sm1[0:RT, 8 + k, :]

            def bc(a):
                return a[:, :, None].broadcast_to([RT, NTT, NE])

            link(nc.vector.tensor_tensor(L, bank[3][0:RT, 0:NTT * NE].rearrange("p (i e) -> p i e", e=NE),
                                         gb_bc[0:RT, None, :].broadcast_to([RT, NTT, NE]), ALU.add))
            link(nc.vector.tensor_reduce(col(0), L, AX.X, ALU.max))
            link(nc.vector.tensor_tensor(L, L, bc(col(0)), ALU.subtract), "logit_ready")
            v.wait_ge(E["gate_exp"], 1)
            link(nc.vector.tensor_reduce(col(1), E_, AX.X, ALU.add))
            link(nc.vector.reciprocal(col(2), col(1)))
            link(nc.vector.tensor_tensor(s1, E_, bc(col(2)), ALU.mult))

            def first_best(s, o):
                link(nc.vector.tensor_reduce(col(3), s, AX.X, ALU.max))
                link(nc.vector.tensor_tensor(t_, s, bc(col(3)), ALU.is_equal))
                link(nc.vector.tensor_tensor(t_, t_, iota8[:], ALU.mult))
                link(nc.vector.tensor_reduce(col(4), t_, AX.X, ALU.max))
                link(nc.vector.tensor_tensor(o, iota8[:], bc(col(4)), ALU.is_equal))

            first_best(s1, o1)
            link(nc.vector.scalar_tensor_tensor(s2, o1, -2.0, s1, ALU.mult, ALU.add))
            first_best(s2, o2)
            link(nc.vector.tensor_tensor(m_, o1, o2, ALU.add))
            link(nc.vector.tensor_tensor(w_, m_, s1, ALU.mult))
            link(nc.vector.scalar_tensor_tensor(t_, w_, 0.0, iota1[:], ALU.is_gt, ALU.mult))
            link(nc.vector.tensor_reduce(col(5), t_, AX.X, ALU.max))
            link(nc.vector.tensor_tensor(m_, iota1[:], bc(col(5)), ALU.is_equal), "winner_ready")

            def add_expert(e):
                v.wait_ge(E["expert_out"], e + 1)
                for i in range(NTT):
                    y = bank[6][0:RT, i * 128:i * 128 + 128]
                    if e == 0:
                        last = nc.vector.tensor_scalar(moe[:, i, :], y, m_[:, i, e:e + 1], None, ALU.mult)
                    else:
                        last = nc.vector.scalar_tensor_tensor(moe[:, i, :], y, m_[:, i, e:e + 1], moe[:, i, :],
                                                              ALU.mult, ALU.add)
                link(last, "expert_added")

            for e in range(NE):
                if e >= 2:
                    v.wait_ge(E["xw_tr"], e - 1)
                link(nc.vector.tensor_tensor(xw[:, e % 2], z[:], w_[:, :, e:e + 1].broadcast_to([RT, NTT, 128]), ALU.mult),
                     "xw_ready")
                if e >= 1:
                    add_expert(e - 1)
            add_expert(NE - 1)
            v.wait_ge(E["b2_done"], 1)
            link(nc.vector.tensor_tensor(moe[:], bank[2][0:RT, :].rearrange("p (i d) -> p i d", i=NTT), moe[:], ALU.add))
            link(nc.vector.scalar_tensor_tensor(x[:], moe[:], tgates[0:RT, 2:3], x[:], ALU.mult, ALU.add))

            layernorm(x, moe, 2)
            layernorm(moe, z, 3)
            v.wait_ge(fill, 12)
            for h in range(H):
                v.wait_ge(E["q1_hi"], h + 1)
                src = prep_bank[h % 3]
                q = slice(h * S, h * S + S)
                signal(nc.vector.tensor_tensor(QB[0:64, :, q], src[0:64, 0:TOK].rearrange("p (b q) -> p b q", b=B),
                                               QS[0:64, :, q], ALU.subtract), "q1_lo")
            for c in range(FC):
                v.wait_ge(E["ff_exp"], c + 1)
                e1, hb, gb = O2[:, c, :], bank[2 + 2 * (c % 2)][:, 0:TOK], bank[3 + 2 * (c % 2)][:, 0:TOK]
                link(nc.vector.tensor_scalar(e1, e1, 1.0, None, ALU.add))
                link(nc.vector.reciprocal(e1, e1))
                link(nc.vector.tensor_tensor(e1, e1, gb, ALU.mult))
                link(nc.vector.tensor_tensor(sT(c), e1, hb, ALU.mult), "ff_silu")

            v.wait_ge(bc_in, BC_IN)
            for k, w in enumerate((bw1[:], bw2[:].rearrange("p c d -> p (c d)"))):
                link(nc.vector.tensor_reduce(wqs[:, k:k + 1], w, AX.X, ALU.add, apply_absolute_value=True), "wabs_ready")
            v.wait_ge(E["wmean_done"], 1)
            link(nc.vector.tensor_scalar(wqs[:, 2:4], bank[3][:, 0:2], 1.0 / (D * FF), EPS, ALU.mult, ALU.max))
            link(nc.vector.reciprocal(wqs[:, 4:6], wqs[:, 2:4]))
            for k, w in enumerate((bw1[:], bw2[:].rearrange("p c d -> p (c d)"))):
                link(nc.vector.tensor_scalar(w, w, wqs[:, 4 + k:5 + k], ROUND, ALU.mult, ALU.add))
                link(nc.vector.tensor_scalar(w, w, ROUND, 1.0, ALU.subtract, ALU.min))
                if k == 0:
                    link(nc.vector.tensor_scalar(w, w, -1.0, wqs[:, 2:3], ALU.max, ALU.mult))
                else:
                    link(nc.vector.tensor_scalar(bw2t[:].rearrange("p c d -> p (c d)"), w, -1.0, None, ALU.max))

            A = A1

            def stats1(b, par):
                need(v, A[f"ctx_in{par}"], ctx_count(b, par))
                need(v, A["cn_ready"], b - 1)
                for k in range(NT):
                    last = nc.vector.bn_stats(st6[0:KT, k, :], ctxN[:, par, k, :])
                last.then_inc(A["stats_v"], 1)
                need(v, A["stats_v"], 8 * b + 1)
                f = [st6[0:KT, :, k] for k in range(6)]
                r = [st1[0:KT, 6 * par + k, :] for k in range(6)]
                steps = [0]

                def step(ins):
                    steps[0] += 1
                    ins.then_inc(A["stats_v"], 1)
                    need(v, A["stats_v"], 8 * b + 1 + steps[0])

                step(nc.vector.tensor_tensor(r[1], f[1], f[4], ALU.subtract))
                step(nc.vector.tensor_tensor(r[0], f[1], f[4], ALU.add))
                step(nc.vector.tensor_scalar(r[0], r[0], 0.5, None, ALU.mult))
                step(nc.vector.tensor_tensor(r[1], r[1], r[1], ALU.mult))
                step(nc.vector.tensor_tensor(r[2], f[2], f[5], ALU.add))
                step(nc.vector.tensor_scalar(r[2], r[2], 1.0 / D, EPS, ALU.mult, ALU.add))
                step(nc.vector.scalar_tensor_tensor(r[2], r[1], 0.25, r[2], ALU.mult, ALU.add))
                assert steps[0] == 7

            def rstd1(b, par):
                need(v, A["stats_a"], 2 * (b + 1))
                r = [st1[0:KT, 6 * par + k, :] for k in range(6)]
                steps = [0]

                def step(ins):
                    steps[0] += 1
                    ins.then_inc(A["sum_rec"], 1)
                    need(v, A["sum_rec"], 3 * b + steps[0])

                step(nc.vector.tensor_tensor(r[3], r[2], r[5], ALU.mult))
                step(nc.vector.tensor_tensor(r[3], r[3], r[5], ALU.mult))
                step(nc.vector.tensor_scalar(r[3], r[3], -0.5, 1.5, ALU.mult, ALU.add))
                nc.vector.tensor_tensor(r[5], r[5], r[3], ALU.mult).then_inc(A["rstd"], 1)

            def prep1(b, par):
                need(v, A["tr_done"], NCH * b + 2)
                nc.vector.tensor_scalar(xT[:, CH:2 * CH], prep_bank[1][:, 0:CH], lng[:, 2:3], lng[:, 3:4],
                                        ALU.mult, ALU.add).then_inc(A["tr_evac_v"], 1)
                for c in range(NCH):
                    need(v, A["khi_ready"], NCH * b + c + 1)
                    cols = slice(c * CH, c * CH + CH)
                    nc.vector.tensor_copy(KS[0:64, par, 1, cols], KS[0:64, par, 0, cols]).then_inc(A["khi_copied"], 1)
                    nc.vector.tensor_tensor(KS[64:128, par, 0, cols], prep_bank[c][64:128, 0:CH], KS[64:128, par, 0, cols],
                                            ALU.subtract).then_inc(A["klo_ready"], 1)

            def norm1(b):
                for half in range(2):
                    need(v, A["pv"], NH2 * (b + 1) - 1 + half)
                    nc.vector.reciprocal(rsum[:, half, :], acc_bank[half][64:128, 0:HALF]).then_inc(A["acc_read"], 1)
                for half in range(2):
                    need(v, A["acc_read"], 2 * b + half + 1)
                    for odd in range(2):
                        nc.vector.tensor_tensor(
                            O2[64 * odd:64 * odd + 64, 4 * half:4 * half + 4, bass.ds(b * S, S)],
                            acc_bank[half][0:64, 0:HALF].rearrange("p (a o q) -> p a o q", o=2, q=S)[:, :, odd, :],
                            rsum[:, half, :].rearrange("p (a o q) -> p a o q", o=2, q=S)[:, :, odd, :],
                            ALU.mult).then_inc(A["normed"], 1)

            v.wait_ge(fill, 13)
            for b in range(2):
                stats1(b, b)
                rstd1(b, b)
            prep1(0, 0)
            maxima(A1, 0, mask1, 64)

            def step1(s, par, prep=True, stats=True):
                if prep:
                    prep1(s + 1, 1 - par)
                if stats:
                    stats1(s + 2, par)
                if prep:
                    if stats:
                        rstd1(s + 2, par)
                    maxima(A1, s + 1, mask1, 64)
                norm1(s)

            step1(0, 0)
            with v.Fori(0, B // 2 - 2) as pair:
                for j in range(2):
                    step1(2 * pair + 1 + j, 1 - j)
            step1(B - 3, 1)
            step1(B - 2, 0, stats=False)
            step1(B - 1, 1, prep=False, stats=False)

            v.wait_ge(E["out1_done"], 1)
            link(nc.vector.scalar_tensor_tensor(x[:], bank[2][0:RT, :].rearrange("p (i d) -> p i d", i=NTT), tgates[0:RT, 1:2],
                                                x[:], ALU.mult, ALU.add))
            layernorm(x, z, 4)

            def quantise(src, dst, inv, ints, key):
                link(nc.vector.tensor_reduce(inv, src, AX.X, ALU.max, apply_absolute_value=True))
                link(nc.vector.tensor_scalar(inv, inv, EPS, 1.0 / 127.0, ALU.max, ALU.mult))
                sc = sm1[0:RT, 20, :]
                link(nc.vector.reciprocal(sc, inv))
                for i in range(NTT):
                    link(nc.vector.tensor_scalar(src[:, i], src[:, i], sc[:, i:i + 1], ROUND, ALU.mult, ALU.add))
                link(nc.vector.tensor_scalar(src, src, ROUND, 127.0, ALU.subtract, ALU.min))
                if ints:
                    link(nc.vector.tensor_scalar(dst, src, -128.0, None, ALU.max), key)
                else:
                    for i in range(NTT):
                        last = nc.vector.tensor_scalar(dst[:, i], src[:, i], -128.0, inv[:, i:i + 1], ALU.max, ALU.mult)
                    link(last, key)

            quantise(z[:], moe[:], sm1[0:RT, 21, :], False, "xq_ready")
            for c in range(FC):
                v.wait_ge(E["lin1_done"], c + 1)
                hb = bank[2 + c][:, 0:TOK].rearrange("p (b q) -> p b q", b=B)
                d = uT[:, 0, c, :].rearrange("p (b q) -> p b q", b=B)
                link(nc.vector.tensor_scalar(d, hb, convw[:, c, 1:2], convb[:, c:c + 1], ALU.mult, ALU.add))
                link(nc.vector.scalar_tensor_tensor(d[:, :, 1:S], hb[:, :, 0:S - 1], convw[:, c, 0:1], d[:, :, 1:S],
                                                    ALU.mult, ALU.add))
                link(nc.vector.scalar_tensor_tensor(d[:, :, 0:S - 1], hb[:, :, 1:S], convw[:, c, 2:3], d[:, :, 0:S - 1],
                                                    ALU.mult, ALU.add), "conv_done")
            for c in range(FC):
                v.wait_ge(E["conv_exp"], c + 1)
                e1 = uT[:, 1, c, :]
                link(nc.vector.tensor_scalar(e1, e1, 1.0, None, ALU.add))
                link(nc.vector.reciprocal(e1, e1))
                link(nc.vector.tensor_tensor(sT(c), e1, uT[:, 0, c, :], ALU.mult), "silu_done")
            h2 = O2[0:RT, 0:5, :].rearrange("p a n -> p (a n)")[:, 0:NTT * FF].rearrange("p (i f) -> p i f", i=NTT)
            q2 = QS[0:RT, 0:3, :].rearrange("p a n -> p (a n)")[:, 0:NTT * FF].rearrange("p (i f) -> p i f", i=NTT)
            for i in range(NTT):
                v.wait_ge(E["back_tr"], i + 1)
                link(nc.vector.tensor_copy(h2[:, i, :], bank[2 + i][0:RT, :]))
            quantise(h2, q2, sm1[0:RT, 22, :], True, "hq_ready")
            link(nc.vector.tensor_scalar(wqs[:, 6:7], wqs[:, 3:4], tgates[:, 3:4], None, ALU.mult))
            link(nc.vector.tensor_scalar(sm1[0:RT, 23, :], sm1[0:RT, 22, :], wqs[0:RT, 6:7], None, ALU.mult))
            v.wait_ge(E["lin2_done"], 1)
            for i in range(NTT):
                link(nc.vector.scalar_tensor_tensor(x[:, i, :], bank[7][0:RT, i * 128:i * 128 + 128], sm1[0:RT, 23, i:i + 1],
                                                    x[:, i, :], ALU.mult, ALU.add), "final_done")

        def hqT(c):
            return QB[:, 0:2, :].rearrange("p a n -> p (a n)")[:, c * TOK:c * TOK + TOK]

        def hq_bank(c):
            return bank[3 + c][:].bitcast(bf16)[:, 0:TOK]

        @block.scalar
        def _(a):
            def done(ins, key):
                ins.then_inc(E[key], 1)

            def rstd(k):
                a.wait_ge(E["var_ready"], k + 1)
                done(nc.scalar.activation(sm1[0:RT, 3, :], sm1[0:RT, 2, :], ACT.Ln), "var_log")
                a.wait_ge(E["var_log"], k + 1)
                done(nc.scalar.activation(sm1[0:RT, 4, :], sm1[0:RT, 3, :], ACT.Exp, scale=-0.5), "rstd_est")

            a.wait_ge(w_in, counts["w_in"])
            done(nc.scalar.activation(tgates[:], gates[:], ACT.Tanh), "tanh_ready")
            rstd(0)
            a.wait_ge(E["tok_tr"], 1)
            done(nc.scalar.copy(zT[:], bank[2][:, 0:TOK]), "zT_ready")
            for g in range(4):
                if g == 0:
                    a.wait_ge(w_in, counts["w_in"])
                    a.wait_ge(fill, 2)
                a.wait_ge(E["q0_proj"], g + 1)
                if g >= 1:
                    a.wait_ge(E["q0_stacked"], g)
                done(nc.scalar.activation(qsT[:], prep_bank[g % 3][:, 0:TOK], ACT.Identity, bias=bq0[:, g:g + 1]), "q0_hi")

            def transposed(A, b, affine):
                for c in (0, 2):
                    need(a, A["tr_done"], NCH * b + c + 1)
                    dst, src = xT[:, c * CH:c * CH + CH], prep_bank[c][:, 0:CH]
                    if affine:
                        ins = nc.scalar.activation(dst, src, ACT.Identity, bias=lng[:, 3:4], scale=lng[:, 2:3])
                    else:
                        ins = nc.scalar.copy(dst, src)
                    ins.then_inc(A["tr_evac_a"], 1)

            def exps(A, b, scale):
                for k in range(NH2):
                    need(a, A["scores"], NH2 * b + k + 1)
                    need(a, A["pv"], NH2 * b + k + 1 - RING_P)
                    nc.scalar.activation(P[:, k % RING_P, :], score_bank[k % RING_S][0:KT, 0:HALF], ACT.Exp, scale=scale)\
                        .then_inc(A["exps"], 1)

            def prep0(b):
                transposed(A0, b, False)
                for c in range(NCH):
                    need(a, A0["kproj"], NCH * b + c + 1)
                    if c == 0:
                        need(a, A0["stacked"], 192 * b)
                    nc.scalar.activation(khi[:, c * CH:c * CH + CH], prep_bank[c][:, 0:CH], ACT.Identity, bias=bk0[:, 0:1])\
                        .then_inc(A0["khi_ready"], 1)

            def collect0(b, par):
                need(a, A0["pv"], NH2 * (b + 1))
                nc.scalar.copy(O2[:, 0:4, bass.ds(b * S, S)], acc_bank[par][:, 0:2 * RT].rearrange("p (a q) -> p a q", q=S))\
                    .then_inc(A0["acc_read"], 1)

            prep0(0)

            def step0(s, par, prep=True):
                if prep:
                    prep0(s + 1)
                exps(A0, s, DK0 ** -0.5)
                collect0(s, par)

            step0(0, 0)
            with a.Fori(0, B // 2 - 1) as pair:
                for j in range(2):
                    step0(2 * pair + 1 + j, 1 - j)
            step0(B - 1, 1, prep=False)

            rstd(1)
            a.wait_ge(E["tok_tr"], 2)
            done(nc.scalar.copy(zT[:], bank[2][:, 0:TOK]), "zT_ready")
            a.wait_ge(E["logit_ready"], 1)
            done(nc.scalar.activation(sm[:, 1], sm[:, 0], ACT.Exp), "gate_exp")
            for e in range(NE):
                a.wait_ge(E["xw_tr"], e + 1)
                if e >= 2:
                    a.wait_ge(E["up_done"], FC * (e - 2) + FC)
                done(nc.scalar.copy(xwT[:, e % 2, :], bank[e % 2][:, 0:TOK]), "xwT_ready")
                for c in range(FC):
                    if c == 0 and e >= 2:
                        a.wait_ge(E["expert_out"], e - 1)
                    a.wait_ge(E["up_done"], FC * e + c + 1)
                    done(nc.scalar.activation(hT[:, e % 2, c, :], bank[2 + c][:, 0:TOK], ACT.Relu, bias=b1[:, e, c:c + 1]), "hidden_ready")
            a.wait_ge(E["disp_tr"], 1)
            done(nc.scalar.copy(dispT, bank[7][0:NE, 0:TOK]), "dispT_ready")
            rstd(2)
            rstd(3)
            a.wait_ge(bc_in, BC_IN)
            a.wait_ge(E["tok_tr"], 3)
            done(nc.scalar.activation(zT[:], bank[2][:, 0:TOK], ACT.Identity, bias=lng[:, 1:2], scale=lng[:, 0:1]), "zT_ready")
            for h in range(H):
                a.wait_ge(E["q1_proj"], h + 1)
                done(nc.scalar.copy(QS[:, :, h * S:h * S + S], prep_bank[h % 3][:, 0:TOK].rearrange("p (b q) -> p b q", b=B)), "q1_hi")
            for c in range(FC):
                a.wait_ge(E["ff_proj"], c + 1)
                done(nc.scalar.activation(O2[:, c, :], bank[3 + 2 * (c % 2)][:, 0:TOK], ACT.Exp, scale=-1.0), "ff_exp")

            A = A1

            def stats1(b, par):
                need(a, A["stats_v"], 8 * (b + 1))
                nc.scalar.activation(st1[0:KT, 6 * par + 4, :], st1[0:KT, 6 * par + 2, :], ACT.Ln).then_inc(A["stats_a"], 1)
                need(a, A["stats_a"], 2 * b + 1)
                nc.scalar.activation(st1[0:KT, 6 * par + 5, :], st1[0:KT, 6 * par + 4, :], ACT.Exp, scale=-0.5)\
                    .then_inc(A["stats_a"], 1)

            def prep1(b, par):
                transposed(A, b, True)
                for c in range(NCH):
                    need(a, A["kproj"], NCH * b + c + 1)
                    nc.scalar.copy(KS[:, par, 0, c * CH:c * CH + CH], prep_bank[c][:, 0:CH]).then_inc(A["khi_ready"], 1)
                for c in range(NCH):
                    need(a, A["vproj"], NCH * b + c + 1)
                    nc.scalar.copy(VS[:, par, c * TPC:c * TPC + TPC, 0:DK1],
                                   prep_bank[c][0:KT, :].rearrange("p (t n) -> p t n", t=TPC)[:, :, DK1:128])\
                        .then_inc(A["v_ready"], 1)

            for b in range(2):
                stats1(b, b)
            a.wait_ge(fill, 13)
            prep1(0, 0)

            def step1(s, par, prep=True, stats=True):
                if prep:
                    prep1(s + 1, 1 - par)
                if stats:
                    stats1(s + 2, par)
                exps(A1, s, DK1 ** -0.5)

            step1(0, 0)
            with a.Fori(0, B // 2 - 2) as pair:
                for j in range(2):
                    step1(2 * pair + 1 + j, 1 - j)
            step1(B - 3, 1)
            step1(B - 2, 0, stats=False)
            step1(B - 1, 1, prep=False, stats=False)

            rstd(4)
            a.wait_ge(E["tok_tr"], 4)
            done(nc.scalar.copy(zT[:], bank[0][:, 0:TOK]), "zT_ready")
            for c in range(FC):
                a.wait_ge(E["conv_done"], c + 1)
                done(nc.scalar.activation(uT[:, 1, c, :], uT[:, 0, c, :], ACT.Exp, scale=-1.0), "conv_exp")
            for c in range(FC):
                a.wait_ge(E["hq_tr"], c + 1)
                done(nc.scalar.copy(hqT(c), hq_bank(c)), "hqT_ready")

        @block.tensor
        def _(pe):
            def done(ins, key):
                ins.then_inc(E[key], 1)

            def tokens_transposed(src, dst):
                for i in range(NTT):
                    last = nc.tensor.transpose(dst[:, i * RT:i * RT + RT], src[:, i, :], ident[0:RT, 0:RT])
                return last

            pe.wait_ge(x_in, counts["x_in"])
            pe.wait_ge(E["z_ready"], 1)
            done(tokens_transposed(z, bank[2]), "tok_tr")
            pe.wait_ge(w_in, counts["w_in"])
            pe.wait_ge(E["zT_ready"], 1)
            for g in range(4):
                if g >= 3:
                    pe.wait_ge(E["q0_stacked"], g - 2)
                done(nc.tensor.matmul(prep_bank[g % 3][:, 0:TOK], wq0[:, g].rearrange("p r n -> p (r n)"), zT[:],
                                      start=True, stop=True), "q0_proj")
            pe.wait_ge(E["q0_stacked"], 4)
            pe.wait_ge(fill, 9)

            def transposes(A, src, b, par, layer):
                need(pe, A["max_in_q"], 2 * b)
                if layer == 0:
                    need(pe, A[f"ctx_in{par}"], ctx_count(b, par))
                else:
                    need(pe, A["cn_ready"], b + 1)
                for c in range(NCH):
                    for k in range(TPC):
                        last = nc.tensor.transpose(prep_bank[c][:, k * KT:k * KT + KT], src[:, par, c * TPC + k, :],
                                                   ident[0:KT, 0:KT])
                    last.then_inc(A["tr_done"], 1)

            def project(A, b, wk, wv):
                for c in range(NCH):
                    if c == 1:
                        need(pe, A["tr_evac_v"], b + 1)
                    else:
                        need(pe, A["tr_evac_a"], 2 * b + 1 + c // 2)
                    nc.tensor.matmul(prep_bank[c][:, 0:CH], wk, xT[:, c * CH:c * CH + CH], start=True, stop=True)\
                        .then_inc(A["kproj"], 1)
                for c in range(NCH):
                    need(pe, A["klo_ready"], NCH * b + c + 1)
                    for k in range(TPC):
                        kk = (c * TPC + k) * KT
                        last = nc.tensor.matmul(prep_bank[c][0:KT, k * 128:k * 128 + 128], xT[:, kk:kk + KT], wv,
                                                start=True, stop=True)
                    last.then_inc(A["vproj"], 1)

            def max_chunk(A, b, par, c, layer):
                rt, j = divmod(c, NCH)
                if c < 2:
                    need(pe, A["v_ready"], NCH * b + c + 1)
                else:
                    need(pe, A["max_taken"], NMC * b + c - 1)
                if c == 0 and layer == 0:
                    need(pe, A["stacked"], 192 * (b + 1))
                g = rt // 2 if layer == 0 else 0
                nc.tensor.matmul(bank[c % 2][0:RT, 0:CH], QS[:, bass.ds(b, 1), rt * RT:rt * RT + RT].rearrange("p o n -> p (o n)"),
                                 KS[:, par, g, j * CH:j * CH + CH], start=True, stop=True).then_inc(A["max_scores"], 1)

            def max_rows(A, b, layer):
                rows = 96 if layer == 0 else 64
                need(pe, A["v_ready"], NCH * (b + 1))
                need(pe, A["max_block"], b + 1)
                for half in range(2):
                    for k in range(NRT // 2):
                        last = nc.tensor.matmul((bank[7], bank[0])[half][rows:rows + 32, k * RT:k * RT + RT],
                                                MB[:, half * NRT // 2 + k, :], identb[0:RT, 0:RT], start=True, stop=True,
                                                tile_position=(0, rows))
                    last.then_inc(A["max_row"], 1)

            def scores0(b, par, k):
                t_, half = divmod(k, 2)
                need(pe, A0["exps"], NH2 * b + k + 1 - RING_S)
                if k == 0:
                    need(pe, A0["max_in_q"], 2 * (b + 1))
                for j in range(2):
                    g = 2 * half + j
                    last = nc.tensor.matmul(score_bank[k % RING_S][0:KT, j * 224:j * 224 + 224],
                                            KS[:, par, g, t_ * KT:t_ * KT + KT],
                                            QS[:, bass.ds(b, 1), g * 224:g * 224 + 224].rearrange("p o n -> p (o n)"),
                                            start=True, stop=True)
                last.then_inc(A0["scores"], 1)

            def values0(b, par, k):
                t_, half = divmod(k, 2)
                need(pe, A0["exps"], NH2 * b + k + 1)
                if k == 0:
                    need(pe, A0["acc_read"], b - 1)
                for c in range(4):
                    last = nc.tensor.matmul(acc_bank[par][32 * c:32 * c + 32, half * RT:half * RT + RT],
                                            VS[:, par, t_, (4 * half + c) * 32:(4 * half + c) * 32 + 32],
                                            P[:, k % RING_P, c * RT:c * RT + RT],
                                            start=(k == 0), stop=(t_ == NT - 1), tile_position=(0, 32 * c),
                                            skip_group_check=True)
                last.then_inc(A0["pv"], 1)

            def scores1(b, par, k):
                t_, half = divmod(k, 2)
                need(pe, A1["exps"], NH2 * b + k + 1 - RING_S)
                if k == 0:
                    need(pe, A1["max_in_q"], 2 * (b + 1))
                cols = slice(half * HALF, half * HALF + HALF)
                dst = score_bank[k % RING_S][0:KT, 0:HALF]
                keys = slice(t_ * KT, t_ * KT + KT)
                nc.tensor.matmul(dst, KS[:, par, 0, keys], QS[:, bass.ds(b, 1), cols].rearrange("p o n -> p (o n)"),
                                 start=True, stop=False)
                nc.tensor.matmul(dst, KS[:, par, 1, keys], QB[:, bass.ds(b, 1), cols].rearrange("p o n -> p (o n)"),
                                 start=False, stop=True).then_inc(A1["scores"], 1)

            def values1(b, par, k):
                t_, half = divmod(k, 2)
                need(pe, A1["exps"], NH2 * b + k + 1)
                if k == 0:
                    need(pe, A1["normed"], 4 * b)
                nc.tensor.matmul(acc_bank[half][:, 0:HALF], VS[:, par, t_, 0:128], P[:, k % RING_P, :],
                                 start=(t_ == 0), stop=(t_ == NT - 1)).then_inc(A1["pv"], 1)

            def attend(A, layer, s, par, prep=True):
                scores, values = (scores0, values0) if layer == 0 else (scores1, values1)
                b1 = s + 1
                if prep:
                    if layer == 0:
                        transposes(A, ctxN, b1, 1 - par, 0)
                        project(A, b1, wkT[:], wvT[:])
                    else:
                        transposes(A, cn, b1, 1 - par, 1)
                        project(A, b1, wk1[:].rearrange("p a n -> p (a n)"), wv1[:])
                scores(s, par, 0)
                scores(s, par, 1)
                c = 0
                for t_ in range(NT):
                    for half in range(2):
                        k = 2 * t_ + half
                        if k + 2 < NH2:
                            scores(s, par, k + 2)
                        if prep:
                            for _ in range((MAX_PLAN[t_] + 1 - half) // 2):
                                max_chunk(A, b1, 1 - par, c, layer)
                                c += 1
                        values(s, par, k)
                if prep:
                    assert c == NMC
                    max_rows(A, b1, layer)

            transposes(A0, ctxN, 0, 0, 0)
            project(A0, 0, wkT[:], wvT[:])
            pe.wait_ge(E["identb_ready"], 1)
            for c in range(NMC):
                max_chunk(A0, 0, 0, c, 0)
            max_rows(A0, 0, 0)
            attend(A0, 0, 0, 0)
            with pe.Fori(0, B // 2 - 1) as pair:
                for j in range(2):
                    attend(A0, 0, 2 * pair + 1 + j, 1 - j)
            attend(A0, 0, B - 1, 1, prep=False)

            pe.wait_ge(A0["acc_read"], B)
            pe.wait_ge(moe_in, counts["moe_in"])
            for c in range(4):
                if c >= 3:
                    pe.wait_ge(E["acc_divided"], c - 2)
                done(nc.tensor.matmul(prep_bank[c % 3][:, 0:448], sumsel[:], O2[:, c, :], start=True, stop=True), "sums_done")
            pe.wait_ge(E["acc_divided"], 4)
            for i in range(NTT):
                for half in range(2):
                    for j in range(2):
                        lhsT = O2[:, 2 * half + j, i * RT:i * RT + RT]
                        last = nc.tensor.matmul(bank[2][0:RT, i * 128:i * 128 + 128], lhsT, wo0[:, half, j, :],
                                                start=(i == 0 and half == 0 and j == 0), stop=(half == 1 and j == 1),
                                                skip_group_check=True)
            done(last, "wo0_done")

            pe.wait_ge(E["z_ready"], 2)
            done(tokens_transposed(z, bank[2]), "tok_tr")
            pe.wait_ge(E["zT_ready"], 2)
            for i in range(NTT):
                last = nc.tensor.matmul(bank[3][0:RT, i * NE:i * NE + NE], zT[:, i * RT:i * RT + RT], gate_w[:],
                                        start=True, stop=True)
            done(last, "logits_done")

            def down(e):
                if e >= 1:
                    pe.wait_ge(E["expert_added"], e)
                pe.wait_ge(E["hidden_ready"], FC * e + FC)
                for i in range(NTT):
                    for c in range(FC):
                        last = nc.tensor.matmul(bank[6][0:RT, i * 128:i * 128 + 128], hT[:, e % 2, c, i * RT:i * RT + RT],
                                                w2[:, e, c, :], start=(i == 0 and c == 0), stop=(c == FC - 1),
                                                skip_group_check=True)
                done(last, "expert_out")

            for e in range(NE):
                pe.wait_ge(E["xw_ready"], e + 1)
                if e >= 2:
                    pe.wait_ge(E["xwT_ready"], e - 1)
                done(tokens_transposed(xw[:, e % 2], bank[e % 2]), "xw_tr")
                pe.wait_ge(E["xwT_ready"], e + 1)
                for c in range(FC):
                    if e >= 1:
                        pe.wait_ge(E["hidden_ready"], FC * (e - 1) + c + 1)
                    done(nc.tensor.matmul(bank[2 + c][:, 0:TOK], w1[:, e, c * 128:c * 128 + 128], xwT[:, e % 2, :],
                                          start=True, stop=True), "up_done")
                if e >= 1:
                    down(e - 1)
            for i in range(NTT):
                last = nc.tensor.transpose(bank[7][0:NE, i * RT:i * RT + RT], sm[:, 7, i, :], ident[0:RT, 0:RT])
            done(last, "disp_tr")
            down(NE - 1)
            pe.wait_ge(E["dispT_ready"], 1)
            for i in range(NTT):
                last = nc.tensor.matmul(bank[2][0:RT, i * 128:i * 128 + 128], dispT[:, i * RT:i * RT + RT], b2[:],
                                        start=True, stop=True)
            done(last, "b2_done")

            pe.wait_ge(E["z_ready"], 4)
            done(tokens_transposed(z, bank[2]), "tok_tr")
            pe.wait_ge(bc_in, BC_IN)
            pe.wait_ge(E["zT_ready"], 3)
            for h in range(H):
                if h >= 3:
                    pe.wait_ge(E["q1_lo"], h - 2)
                done(nc.tensor.matmul(prep_bank[h % 3][:, 0:TOK], wq1[:, h].rearrange("p a n -> p (a n)"), zT[:],
                                      start=True, stop=True), "q1_proj")
            for c in range(FC):
                if c >= 2:
                    pe.wait_ge(E["ff_silu"], c - 1)
                nc.tensor.matmul(bank[2 + 2 * (c % 2)][:, 0:TOK], wff1[:, c, :], zT[:], start=True, stop=True)
                done(nc.tensor.matmul(bank[3 + 2 * (c % 2)][:, 0:TOK], wff1[:, FC + c, :], zT[:], start=True, stop=True), "ff_proj")
            pe.wait_ge(E["wabs_ready"], 2)
            done(nc.tensor.matmul(bank[3][:, 0:2], ones[:], wqs[:, 0:2], start=True, stop=True), "wmean_done")

            pe.wait_ge(E["q1_lo"], H)
            pe.wait_ge(fill, 13)
            transposes(A1, cn, 0, 0, 1)
            project(A1, 0, wk1[:].rearrange("p a n -> p (a n)"), wv1[:])
            for c in range(NMC):
                max_chunk(A1, 0, 0, c, 1)
            max_rows(A1, 0, 1)
            attend(A1, 1, 0, 0)
            with pe.Fori(0, B // 2 - 1) as pair:
                for j in range(2):
                    attend(A1, 1, 2 * pair + 1 + j, 1 - j)
            attend(A1, 1, B - 1, 1, prep=False)

            pe.wait_ge(A1["normed"], 4 * B)
            for i in range(NTT):
                for k in range(H // 2 + FC):
                    lhsT = O2[:, k, i * RT:i * RT + RT] if k < H // 2 else sT(k - H // 2)[:, i * RT:i * RT + RT]
                    rhs = wo1[:, k, :] if k < H // 2 else wff2[:, k - H // 2, :]
                    last = nc.tensor.matmul(bank[2][0:RT, i * 128:i * 128 + 128], lhsT, rhs, start=(i == 0 and k == 0),
                                            stop=(k == H // 2 + FC - 1), skip_group_check=True)
            done(last, "out1_done")

            pe.wait_ge(E["xq_ready"], 1)
            done(tokens_transposed(moe, bank[0]), "tok_tr")
            pe.wait_ge(E["zT_ready"], 4)
            for c in range(FC):
                done(nc.tensor.matmul(bank[2 + c][:, 0:TOK], bw1[:, c * 128:c * 128 + 128], zT[:], start=True, stop=True), "lin1_done")
            pe.wait_ge(E["silu_done"], FC)
            for i in range(NTT):
                for c in range(FC):
                    last = nc.tensor.transpose(bank[2 + i][0:RT, c * 128:c * 128 + 128], sT(c)[:, i * RT:i * RT + RT], ident[:])
                done(last, "back_tr")
            pe.wait_ge(E["hq_ready"], 1)
            q2 = QS[0:RT, 0:3, :].rearrange("p a n -> p (a n)")[:, 0:NTT * FF].rearrange("p (i f) -> p i f", i=NTT)
            for c in range(FC):
                for i in range(NTT):
                    last = nc.tensor.transpose(hq_bank(c)[:, i * RT:i * RT + RT], q2[:, i, c * 128:c * 128 + 128],
                                               identb[0:RT, 0:RT])
                done(last, "hq_tr")
            pe.wait_ge(E["hqT_ready"], FC)
            for i in range(NTT):
                for c in range(FC):
                    last = nc.tensor.matmul(bank[7][0:RT, i * 128:i * 128 + 128], hqT(c)[:, i * RT:i * RT + RT],
                                            bw2t[:, c, :], start=(i == 0 and c == 0), stop=(c == FC - 1), skip_group_check=True)
            done(last, "lin2_done")


def kernel(**inputs):
    import numpy as np
    import concourse.bacc as bacc
    from concourse.bass_utils import run_bass_kernel_spmd

    arrays = {k: np.ascontiguousarray(v) for k, v in inputs.items()}
    for new, old in (("wkT", "L0_xattn_Wk"), ("wvT", "L0_xattn_Wv"), ("wqT", "L0_xattn_Wq"), ("woT", "L0_xattn_Wo"),
                     ("bw1T", "L1_ffn_w1"), ("bw2T", "L1_ffn_w2")):
        arrays[new] = np.ascontiguousarray(arrays.pop(old).T)
    arrays["c_ident"] = np.eye(128, dtype=np.float32)
    p = np.arange(128)
    arrays["c_qmask"] = ((p[:, None] % 32) // DK0 == np.arange(4)).astype(np.float32)
    head = 2 * np.arange(2)[None, :] + np.arange(RT)[:, None] // S
    arrays["c_mmask0"] = -(head[:, :, None] == np.arange(32)).astype(np.float32)
    arrays["c_mmask1"] = -np.tile(np.arange(32) == 0, (RT, 1)).astype(np.float32)
    arrays["c_sumsel"] = (p[:, None] == (p[None, :] // 32) * 32 + 16).astype(np.float32)
    arrays["c_iota8"] = np.tile(np.arange(NE, 0, -1, dtype=np.float32), (RT, NTT, 1))
    arrays["c_iota1"] = np.tile(np.arange(1, NE + 1, dtype=np.float32), (RT, NTT, 1))

    nc = bacc.Bacc("TRN2", target_bir_lowering=False, num_devices=1)
    t = {k: nc.dram_tensor(f"in_{k}", a.shape, mybir.dt.from_np(a.dtype), kind="ExternalInput").ap()
         for k, a in arrays.items()}
    out = nc.dram_tensor("out", (B, S, D), fp32, kind="ExternalOutput").ap()
    build(nc, t, out)
    r = run_bass_kernel_spmd(nc, [{f"in_{k}": a for k, a in arrays.items()}], core_ids=[0])
    return r.results[0]["out"]
```

```python
import concourse.bass as bass
from concourse import mybir
from contextlib import ExitStack

B, S, D = 8, 56, 128
NK = 1500
H = 16
KT, NT = 125, 12
HS = H * S
HALF = HS // 2
RT = 2 * S
TOK = B * S
NTT = TOK // RT
CH, NCH = 500, 3
TPC = CH // KT
NH2 = 2 * NT
DK0, DK1 = 8, 64
NE, FF = 8, 512
FC = FF // 128
EPS = 1e-5
STACKED = 3 * 16
RSTD_TILE = 8
SUMS_AT = 1
ADD_LAG = 3
NORM_AT = 18
QUERIES_AT = 5
RING_S, RING_P = 3, 6
ROUND = 12582912.0


class Layer:

    def __init__(self, n, rows, spare, group, before, beside):
        self.n, self.rows, self.spare, self.group = n, rows, spare, group
        self.tiles = HS // rows
        self.nmax = self.tiles * NCH
        self.split = (self.tiles + 1) // 2 * rows
        self.before = self.scheduled(before, (6, 7), 2)
        self.beside = [self.scheduled(beside, (7,), ahead) for ahead in range(3)]

    def scheduled(self, places, banks, most):
        schedule, held, turn = [[] for _ in range(NH2)], {}, 0
        for p, kind, c, ahead in sorted(places):
            if ahead > most:
                continue
            bank = None
            if kind in "TKV":
                bank, turn = banks[turn % len(banks)], turn + 1
            elif kind == "R":
                bank = 7
            schedule[p].append((kind, c, ahead, bank, held.get(bank)))
            if bank is not None:
                held[bank] = (kind, c, ahead)
        return schedule

    def max_chunk(self, c):
        return divmod(c, NCH) if self.n == 0 else divmod(c, self.tiles)[::-1]

    def items(self, s):
        return self.beside[sum(exists(s, ahead) for ahead in (1, 2))]


def spread(kind, ahead, places, first=0):
    return [(p, kind, first + c, ahead) for c, p in enumerate(places)]


def evenly(lo, hi, n):
    return [lo + i * (hi - lo + 1) // n for i in range(n)]


L0 = Layer(0, 2 * S, 96, 32,
           spread("T", 0, (0, 0, 1)) + spread("K", 0, (1, 2, 2)) + spread("V", 0, (3, 3, 4))
           + spread("M", 0, evenly(5, 16, 24)) + spread("T", 1, (6, 9, 10)) + spread("K", 1, (12, 14, 16))
           + [(17, "R", 0, 0)],
           spread("V", 1, (2, 3, 4)) + spread("M", 1, evenly(4, 21, 24)) + spread("T", 2, (6, 8, 10))
           + spread("K", 2, (13, 14, 16)) + [(22, "R", 0, 1)])
L1 = Layer(1, 128, 64, 64,
           spread("T", 0, (0, 1, 2)) + spread("K", 0, (1, 2, 3)) + spread("M", 0, evenly(2, 12, 21))
           + spread("V", 0, (2, 4, 6)) + [(13, "R", 0, 0)],
           spread("T", 1, (3, 5, 7)) + spread("K", 1, (4, 6, 8)) + spread("V", 1, (9, 11, 13))
           + spread("M", 1, evenly(5, 20, 21)) + [(22, "R", 0, 1)])

fp32 = mybir.dt.float32
bf16 = mybir.dt.bfloat16
ALU = mybir.AluOpType
ACT = mybir.ActivationFunctionType
AX = mybir.AxisListType


def need(eng, sem, value):
    if isinstance(value, int) and value <= 0:
        return
    eng.wait_ge(sem, value)


def steps(eng, step):
    step(0, 0)
    with eng.Fori(0, (B - 4) // 2) as pair:
        for j in range(2):
            step(2 * pair + 1 + j, 1 - j)
    for s in range(B - 3, B):
        step(s, s % 2)


def exists(s, ahead):
    return not isinstance(s, int) or s + ahead < B


def released(A, item, b):
    kind, c = item[0], item[1]
    return {"T": (A["tr_evac"], NCH * b + c + 1), "K": (A["klo_ready"], NCH * b + c + 1),
            "V": (A["v_ready"], NCH * b + c + 1)}[kind]


def ctx_count(b, par):
    return 8 * (b - par) + 16


def build(nc, t, out):
    ctx = ExitStack()
    with ctx:
        ctx.enter_context(nc.allow_non_contiguous_dma(reason="biases, a few hundred values each"))
        def sb(name, shape, dt=fp32):
            return ctx.enter_context(nc.sbuf_tensor(name, shape, dt))

        def sem(name):
            return ctx.enter_context(nc.semaphore(name))

        bank = [ctx.enter_context(nc.psum_tensor(f"bank{i}", [128, 512], fp32)) for i in range(8)]
        prep_bank = [bank[0], bank[1], bank[7]]
        q0_bank = [bank[0], bank[1], bank[3], bank[4]]
        score_bank = [bank[2], bank[3], bank[4]]
        acc_bank = [bank[5], bank[6]]

        ident = sb("ident", [128, 128])
        identb = sb("identb", [128, 128], bf16)
        ones = sb("ones", [128, 128])
        qmask = sb("qmask", [128, 4])
        mmask0 = sb("mmask0", [RT, 2, 32])
        mmask1 = sb("mmask1", [128, 32])
        iota8 = sb("iota8", [RT, NTT, NE])
        iota1 = sb("iota1", [RT, NTT, NE])
        gates = sb("gates", [128, 4])
        tgates = sb("tgates", [128, 4])
        wkT = sb("wkT", [128, 128])
        wvT = sb("wvT", [128, 128])
        wq0 = sb("wq0", [128, 4, 4, 32])
        bq0 = sb("bq0", [128, 4])
        bk0 = sb("bk0", [128, 1])
        bv0 = sb("bv0", [128, 1])
        bo_bc = sb("bo_bc", [128, 128])
        wo0 = sb("wo0", [128, 4, 128])
        woT = sb("woT", [128, 128])
        gate_w = sb("gate_w", [128, NE])
        gb_bc = sb("gb_bc", [128, NE])
        w1 = sb("w1", [128, NE, FF])
        b1 = sb("b1", [128, NE, FC])
        w2 = sb("w2", [128, NE, FC, 128])
        b2 = sb("b2", [NE, 128])
        wk1 = sb("wk1", [128, 2, DK1])
        wv1 = sb("wv1", [128, 128])
        wq1 = sb("wq1", [128, H, 2, DK1])
        wo1 = sb("wo1", [128, H // 2, 128])
        wff1 = sb("wff1", [128, 2 * FC, 128])
        wff2 = sb("wff2", [128, FC, 128])
        lng = sb("lng", [128, 4])
        bw1 = sb("bw1", [128, FF])
        bw2 = sb("bw2", [128, FC, 128])
        bw2t = sb("bw2t", [128, FC, 128], bf16)
        convw = sb("convw", [128, FC, 3])
        convb = sb("convb", [128, FC])
        ctxN = sb("ctxN", [KT, 2, NT, 128])
        xT = sb("xT", [128, NK])
        cn = w1[0:KT].rearrange("p e f -> p (e f)")[:, 0:2 * NT * 128].rearrange("p (a t d) -> p a t d", a=2, d=128)
        khi = sb("khi", [128, NK], bf16)
        klo = sb("klo", [128, NK], bf16)
        KS = sb("KS", [128, 2, 4, NK], bf16)
        VS = sb("VS", [KT, 2, NT, 128])
        SP = sb("SP", [KT, 2, HALF])
        powers = sb("powers", [128, 3, NT])
        QS = sb("QS", [128, B, HS], bf16)
        QB = sb("QB", [128, B, HS], bf16)
        P = sb("P", [KT, RING_P, HALF])
        O2 = sb("O2", [128, H // 2, TOK])
        mxc = sb("mxc", [128, L0.nmax])
        mx = sb("mx", [128, L0.tiles])
        MB = sb("MB", [128, L0.tiles, 32], bf16)
        rsum = sb("rsum", [128, HALF])
        st6 = sb("st6", [128, NT, 6])
        st1 = sb("st1", [128, 12, NT])
        x = sb("x", [RT, NTT, 128])
        z = sb("z", [RT, NTT, 128])
        zT = sb("zT", [128, TOK])
        hT = QB[:].rearrange("p b n -> p (b n)").bitcast(fp32).rearrange("p (a c n) -> p a c n", a=2, c=FC)
        xw = P[0:RT].rearrange("p a n -> p (a n)")[:, 0:2 * NTT * 128].rearrange("p (a i d) -> p a i d", a=2, d=128)
        xwT = xT[:, 0:2 * TOK].rearrange("p (a n) -> p a n", a=2)
        uT = w2[:].rearrange("p e c d -> p (e c d)")[:, 0:2 * FC * TOK].rearrange("p (a c n) -> p a c n", a=2, c=FC)

        def q0(g):
            return QB[:, 0, g % 2 * TOK:g % 2 * TOK + TOK]

        def sT(c):
            free = KS[:, c // 2, 2:4, :].rearrange("p a n -> p (a n)").bitcast(fp32)
            return free[:, c % 2 * TOK:c % 2 * TOK + TOK]

        sm = sb("sm", [RT, 12, NTT, NE])
        sm1 = sb("sm1", [128, 24, NTT])
        dispT = rsum[0:NE, :]
        moe = sb("moe", [RT, NTT, 128])
        wqs = sb("wqs", [128, 8])

        k_in, w_in, moe_in, x_in, bc_in = sem("k_in"), sem("w_in"), sem("moe_in"), sem("x_in"), sem("bc_in")
        fill = sem("fill")
        E = {k: sem(k) for k in ("""tanh_ready acc_divided b2_done back_tr conv_done conv_exp dispT_ready disp_tr expert_added expert_out
                                 ff_exp ff_proj ff_silu final_done gate_exp hidden_ready hqT_ready hq_ready hq_tr
                                 identb_ready lin1_done lin2_done logit_ready logits_done out1_done q0_hi q0_proj
                                 q0_stacked q1_hi q1_lo q1_proj rstd_ready silu_done sums_done tok_tr up_done rstd_step
                                 var_ready vector_chain wabs_ready winner_ready wmean_done wo0_done xq_ready xwT_ready
                                 xw_ready xw_tr zT_ready z_ready""").split()}
        out_done = sem("out_done")

        def attention_sems(n):
            names = ("stats_v", "rstd", "shift", "cn_ready", "tr_done", "tr_evac",
                     "kproj", "khi_ready", "klo_ready", "khi_copied", "vproj", "v_ready", "max_scores", "max_taken",
                     "max_final", "max_block", "max_row", "max_in_q", "scores", "exps", "pv",
                     "sum0", "sum1", "sums_mm", "sum_rec", "normed")
            return {k: sem(f"{k}_{n}") for k in names} \
                | {f"ctx_in{par}": sem(f"ctx_in{par}_{n}") for par in range(2)} \
                | ({f"stacked{g}": sem(f"stacked{g}") for g in range(4)} if n == 0 else {})

        A0, A1 = attention_sems(0), attention_sems(1)

        block = ctx.enter_context(nc.Block())
        ctx_h = t["ctx_1024"].rearrange("b (p t) d -> b p t d", t=NT)
        NCONST, NW, NMOE, NX, NBC = [0], [0], [0], [0], [0]
        counts = {"k_in": 0, "w_in": 0, "moe_in": 0, "x_in": 0}

        def add_tile(unit, eng, A, b, half, t_):
            need(eng, A["exps"], NH2 * b + 2 * t_ + half + 1)
            if t_ == 1:
                need(eng, A["sums_mm"], b)
            else:
                need(eng, A[f"sum{half}"], (NT - 1) * b + t_ - 1)
            a = P[:, (2 * t_ + half) % RING_P, :]
            other = P[:, half, :] if t_ == 1 else SP[:, half, :]
            unit.tensor_tensor(SP[:, half, :], a, other, ALU.add).then_inc(A[f"sum{half}"], 1)

        @block.sync
        def _(sp):
            def load(dst, src, s, key):
                sp.dma_start(dst, src).then_inc(s, 16)
                counts[key] += 16

            load(x[:], t["x"].rearrange("(n b) s d -> (b s) n d", b=2), x_in, "x_in")
            load(ident[:], t["c_ident"], x_in, "x_in")
            sp.dma_start(ctxN[:, 0], ctx_h[0]).then_inc(A0["ctx_in0"], 16)
            load(wkT[:], t["wkT"], k_in, "k_in")
            load(wvT[:], t["wvT"], k_in, "k_in")
            load(bk0[:], t["L0_xattn_bk"].rearrange("(p o) -> p o", o=1), k_in, "k_in")
            for r in range(3):
                load(wq0[:, :, r, :], t["wqT"].rearrange("d (g n) -> d g n", g=4), w_in, "w_in")
                load(bq0[32 * r:32 * r + 32, :], t["L0_xattn_bq"].rearrange("(g p) -> p g", p=32), w_in, "w_in")
            load(qmask[:], t["c_qmask"], w_in, "w_in")
            load(mmask0[:], t["c_mmask0"], w_in, "w_in")
            sp.dma_start(ctxN[:, 1], ctx_h[1]).then_inc(A0["ctx_in1"], 16)

            def stack(b, par):
                need(sp, A0["klo_ready"], NCH * (b + 1))
                for g in range(4):
                    rows = slice(32 * g, 32 * g + 32)
                    for r, src in enumerate((khi, khi, klo)):
                        sp.dma_start(KS[32 * r:32 * r + 32, par, g, :], src[rows, :])\
                            .then_inc(A0[f"stacked{g}"], 16)

            def fetch(b, par):
                sp.dma_start(ctxN[:, par], ctx_h[bass.ds(b, 1)].rearrange("o p t d -> p (o t) d")).then_inc(A0[f"ctx_in{par}"], 16)

            def refill(b, par):
                need(sp, A0["scores"], NH2 * (b - 1))
                if exists(b, 2):
                    fetch(b + 2, par)
                stack(b, par)

            stack(0, 0)
            sp.wait_ge(A0["tr_done"], NCH)
            fetch(2, 0)
            stack(1, 1)
            fetch(3, 1)
            for dst, src in ((gate_w, t["L0_ffn_gate_w"]), (gb_bc, t["L0_ffn_gate_b"].partition_broadcast(128)),
                             (b2, t["L0_ffn_b2"]), (bo_bc, t["L0_xattn_bo"].partition_broadcast(128))):
                load(dst[:], src, moe_in, "moe_in")
            load(mmask1[:], t["c_mmask1"], moe_in, "moe_in")
            load(iota8[:], t["c_iota8"], moe_in, "moe_in")
            load(iota1[:], t["c_iota1"], moe_in, "moe_in")
            load(bv0[:], t["L0_xattn_bv"].rearrange("(p o) -> p o", o=1), moe_in, "moe_in")
            load(gates[:, 0:2], t["g_xattn"].partition_broadcast(128), moe_in, "moe_in")
            load(gates[:, 2:4], t["g_ffn"].partition_broadcast(128), moe_in, "moe_in")
            load(woT[:], t["woT"], moe_in, "moe_in")
            load(w1[:], t["L0_ffn_w1"].rearrange("e d h -> d e h"), moe_in, "moe_in")
            load(b1[:], t["L0_ffn_b1"].rearrange("e (c p) -> p e c", p=128), moe_in, "moe_in")
            load(w2[:], t["L0_ffn_w2"].rearrange("e (c p) d -> p e c d", p=128), moe_in, "moe_in")
            with sp.Fori(1, B // 2 - 1) as pair:
                for j in range(2):
                    refill(2 * pair + j, j)
            refill(B - 2, 0)
            refill(B - 1, 1)
            for j in range(2):
                sp.dma_start(wk1[:, j, :], t["L1_xattn_Wkv"][:, 0:DK1]).then_inc(bc_in, 16)
                sp.dma_start(wq1[:, :, j, :], t["L1_xattn_Wq"].rearrange("d (h e) -> d h e", h=H)).then_inc(bc_in, 16)
            for a in range(2):
                sp.dma_start(wo1[64 * a:64 * a + 64], t["L1_xattn_Wo"].rearrange("(a k p) d -> a p k d", a=2, k=8)[a])\
                    .then_inc(bc_in, 16)
            for dst, src in ((wv1, t["L1_xattn_Wkv"]),
                             (wff1, t["L1_xattn_Wff1"].rearrange("d (c n) -> d c n", n=128)),
                             (wff2, t["L1_xattn_Wff2"].rearrange("(c p) d -> p c d", p=128)),
                             (bw1, t["bw1T"]), (bw2, t["bw2T"].rearrange("(c p) d -> p c d", p=128)),
                             (convw, t["L1_ffn_conv_w"].rearrange("(c p) o k -> p c (o k)", p=128)),
                             (convb, t["L1_ffn_conv_b"].rearrange("(c p) -> p c", p=128))):
                sp.dma_start(dst[:], src).then_inc(bc_in, 16)
            for j, k in enumerate(("ln_g", "ln_b", "cln_g", "cln_b")):
                sp.dma_start(lng[:, j:j + 1], t["L1_xattn_" + k].rearrange("(p o) -> p o", o=1)).then_inc(bc_in, 16)
            sp.wait_ge(A0["tr_done"], NCH * B)
            for b in range(2):
                sp.dma_start(ctxN[:, b], ctx_h[b]).then_inc(A1[f"ctx_in{b}"], 16)

            def fetch1(b, par):
                need(sp, A1["cn_ready"], NT * (b - 1))
                sp.dma_start(ctxN[:, par], ctx_h[bass.ds(b, 1)].rearrange("o p t d -> p (o t) d")).then_inc(A1[f"ctx_in{par}"], 16)

            with sp.Fori(1, B // 2) as pair:
                for j in range(2):
                    fetch1(2 * pair + j, j)
            sp.wait_ge(E["final_done"], NTT)
            sp.dma_start(out.rearrange("(n b) s d -> (b s) n d", b=2), x[:]).then_inc(out_done, 16)
            sp.wait_ge(out_done, 16)

        BC_IN = 16 * (2 * 2 + 2 + 7 + 4)

        @block.gpsimd
        def _(pool):
            filled = [0]

            def put(dst, value):
                nc.gpsimd.memset(dst, value).then_inc(fill, 1)
                filled[0] += 1
                pool.wait_ge(fill, filled[0])

            put(wq0[:, :, 3, :], 0.0)
            put(bq0[96:128, :], 0.0)
            put(powers[:, 0], -0.5)
            put(powers[:, 1], 1.5)
            put(ones[:], 1.0)

            def estimate_rstd(var, r, tmp, n, width, done):
                p = slice(0, n)
                def step(ins):
                    ins.then_inc(done[0], 1)
                    done[1] += 1
                    need(pool, done[0], done[1])
                step(nc.gpsimd.tensor_tensor(r, var, powers[p, 0, 0:width], ALU.pow))
                step(nc.gpsimd.tensor_tensor(tmp, var, r, ALU.mult))
                step(nc.gpsimd.tensor_tensor(tmp, tmp, r, ALU.mult))
                step(nc.gpsimd.tensor_tensor(tmp, tmp, powers[p, 0, 0:width], ALU.mult))
                step(nc.gpsimd.tensor_tensor(tmp, tmp, powers[p, 1, 0:width], ALU.add))
                return nc.gpsimd.tensor_tensor(r, r, tmp, ALU.mult)

            def token_rstd(k):
                pool.wait_ge(E["var_ready"], k + 1)
                estimate_rstd(sm1[0:RT, 2, :], sm1[0:RT, 4, :], sm1[0:RT, 3, :], RT, NTT, [E["rstd_step"], 5 * k])\
                    .then_inc(E["rstd_ready"], 1)
                pool.wait_ge(E["rstd_ready"], k + 1)

            def context_rstd(b, par):
                r = [st1[0:KT, 6 * par + k, :] for k in range(6)]
                need(pool, A1["stats_v"], 8 * (b + 1))
                estimate_rstd(r[2], r[5], r[3], KT, NT, [A1["rstd"], 6 * b]).then_inc(A1["rstd"], 1)
                need(pool, A1["rstd"], 6 * (b + 1))
                nc.gpsimd.tensor_tensor(r[4], r[0], r[5], ALU.mult).then_inc(A1["shift"], 1)
                need(pool, A1["shift"], b + 1)

            def sum_tiles(A, s, first=1, end=NT):
                for t_ in range(first, end):
                    add_tile(nc.gpsimd, pool, A, s, 0, t_)
                need(pool, A["sum0"], (NT - 1) * s + end - 1)

            token_rstd(0)
            put(KS[96:128], 0.0)
            put(KS[96:100], 1.0)
            sum_tiles(A0, 0)
            with pool.Fori(1, B) as s:
                sum_tiles(A0, s)
            token_rstd(1)
            put(KS[64:128, :, 1, :], 0.0)
            put(KS[64:65, :, 1, :], 1.0)
            pool.wait_ge(E["expert_out"], NE)
            put(QB[64:128], 0.0)
            token_rstd(2)
            token_rstd(3)
            for b in range(2):
                context_rstd(b, b)

            def step1(s, par):
                sum_tiles(A1, s, 1, RSTD_TILE)
                if exists(s, 2):
                    context_rstd(s + 2, par)
                sum_tiles(A1, s, RSTD_TILE, NT)

            steps(pool, step1)
            token_rstd(4)

        @block.vector
        def _(v):
            count = {}

            def signal(ins, key="vector_chain"):
                count[key] = count.get(key, 0) + 1
                ins.then_inc(E[key], 1)

            def link(ins, key="vector_chain"):
                signal(ins, key)
                v.wait_ge(E[key], count[key])

            def layernorm(src, dst, k):
                for i in range(NTT):
                    last = nc.vector.bn_stats(st6[0:RT, i, :], src[:, i, :])
                link(last)
                for i in range(NTT):
                    last = nc.vector.bn_aggr(sm1[0:RT, 0:2, i], st6[0:RT, i, :])
                link(last)
                link(nc.vector.tensor_scalar(sm1[0:RT, 2, :], sm1[0:RT, 1, :], EPS, None, ALU.add), "var_ready")
                v.wait_ge(E["rstd_ready"], k + 1)
                for i in range(NTT):
                    last = nc.vector.tensor_scalar(dst[:, i, :], src[:, i, :], sm1[0:RT, 0, i:i + 1], sm1[0:RT, 4, i:i + 1],
                                                   ALU.subtract, ALU.mult)
                link(last, "z_ready")

            v.wait_ge(x_in, counts["x_in"])
            layernorm(x, z, 0)
            signal(nc.vector.tensor_copy(identb[:], ident[:]), "identb_ready")
            def item(A, L, mask, kind, c, bk, b, par):
                cols = slice(c * CH, c * CH + CH)
                if kind == "K":
                    need(v, A["khi_ready"], NCH * b + c + 1)
                    if L.n == 0:
                        nc.vector.scalar_tensor_tensor(klo[:, cols], bank[bk][:, 0:CH], bk0[:, 0:1], khi[:, cols],
                                                       ALU.add, ALU.subtract).then_inc(A["klo_ready"], 1)
                    else:
                        nc.vector.tensor_copy(KS[0:64, par, 1, cols], KS[0:64, par, 0, cols]).then_inc(A["khi_copied"], 1)
                        nc.vector.tensor_tensor(KS[64:128, par, 0, cols], bank[bk][64:128, 0:CH],
                                                KS[64:128, par, 0, cols], ALU.subtract).then_inc(A["klo_ready"], 1)
                elif kind == "M":
                    need(v, A["max_scores"], L.nmax * b + c + 1)
                    rt, j = L.max_chunk(c)
                    nc.vector.tensor_reduce(mxc[0:L.rows, rt * NCH + j:rt * NCH + j + 1], bank[c % 2][0:L.rows, 0:CH], AX.X, ALU.max)\
                        .then_inc(A["max_taken"], 1)
                    if c == L.nmax - 1:
                        need(v, A["max_taken"], L.nmax * (b + 1))
                        nc.vector.tensor_reduce(mx[0:L.rows, 0:L.tiles],
                                                mxc[0:L.rows, 0:L.nmax].rearrange("p (r c) -> p r c", c=NCH), AX.X, ALU.max)\
                            .then_inc(A["max_final"], 1)
                        need(v, A["max_final"], b + 1)
                        m, blk = mx[0:L.rows, 0:L.tiles], MB[0:L.rows, 0:L.tiles]
                        if L.n == 0:
                            m, blk = m.rearrange("p (a c) -> p a c", c=2), blk.rearrange("p (a c) n -> p a c n", c=2)
                        nc.vector.tensor_tensor(blk, m[..., None].broadcast_to(list(m.shape) + [32]), mask, ALU.mult)\
                            .then_inc(A["max_block"], 1)
                elif kind == "R":
                    dst = QS if L.n == 0 else QB
                    for half, (lo, hi) in enumerate(((0, L.split), (L.split, HS))):
                        need(v, A["max_row"], 2 * b + half + 1)
                        nc.vector.tensor_copy(dst[L.spare:L.spare + 32, bass.ds(b, 1), lo:hi].rearrange("p o n -> p (o n)"),
                                              (bank[7], bank[0])[half][L.spare:L.spare + 32, 0:hi - lo])\
                            .then_inc(A["max_in_q"], 1)

            def normalise(A, L, b, par):
                n_ = HS * L.group // 128
                need(v, A["sums_mm"], b + 1)
                nc.vector.reciprocal(rsum[:, 0:n_], bank[7][:, 0:n_]).then_inc(A["sum_rec"], 1)
                need(v, A["sum_rec"], b + 1)
                need(v, A["pv"], NT * (b + 1))
                nc.vector.tensor_tensor(O2[:, 0:n_ // S, bass.ds(b * S, S)],
                                        acc_bank[par][:, 0:n_].rearrange("p (a q) -> p a q", q=S),
                                        rsum[:, 0:n_].rearrange("p (a q) -> p a q", q=S), ALU.mult).then_inc(A["normed"], 1)

            def stats1(b, par, k):
                A = A1
                if k < NT:
                    if k == 0:
                        need(v, A[f"ctx_in{par}"], ctx_count(b, par))
                        need(v, A["cn_ready"], NT * (b - 1))
                    ins = nc.vector.bn_stats(st6[0:KT, k, :], ctxN[:, par, k, :])
                    if k == NT - 1:
                        ins.then_inc(A["stats_v"], 1)
                    return
                need(v, A["stats_v"], 8 * b + 1)
                f = [st6[0:KT, :, k] for k in range(6)]
                r = [st1[0:KT, 6 * par + k, :] for k in range(6)]
                steps = [0]

                def step(ins):
                    steps[0] += 1
                    ins.then_inc(A["stats_v"], 1)
                    need(v, A["stats_v"], 8 * b + 1 + steps[0])

                step(nc.vector.tensor_tensor(r[1], f[1], f[4], ALU.subtract))
                step(nc.vector.tensor_tensor(r[0], f[1], f[4], ALU.add))
                step(nc.vector.tensor_scalar(r[0], r[0], -0.5, None, ALU.mult))
                step(nc.vector.tensor_tensor(r[1], r[1], r[1], ALU.mult))
                step(nc.vector.tensor_tensor(r[2], f[2], f[5], ALU.add))
                step(nc.vector.tensor_scalar(r[2], r[2], 1.0 / D, EPS, ALU.mult, ALU.add))
                step(nc.vector.scalar_tensor_tensor(r[2], r[1], 0.25, r[2], ALU.mult, ALU.add))
                assert steps[0] == 7

            def step(A, L, mask, s, par):
                for p in range(NH2):
                    if p == SUMS_AT and not (isinstance(s, int) and s == 0):
                        normalise(A, L, s - 1, 1 - par)
                    for kind, c, ahead, bk, _ in L.items(s)[p]:
                        item(A, L, mask, kind, c, bk, s + ahead, (par + ahead) % 2)
                    if L.n == 1 and exists(s, 2) and p <= NT:
                        stats1(s + 2, par, p)
                    t_, odd = divmod(p - ADD_LAG, 2)
                    if odd == 0 and t_ >= 1:
                        add_tile(nc.vector, v, A, s, 1, t_)
                for t_ in range((NH2 - 1 - ADD_LAG) // 2 + 1, NT):
                    add_tile(nc.vector, v, A, s, 1, t_)

            mask0 = mmask0[:][:, None, :, :].broadcast_to([L0.rows, L0.tiles // 2, 2, 32])
            mask1 = mmask1[:][:, None, :].broadcast_to([L1.rows, L1.tiles, 32])
            def prepare(A, L, mask, places):
                for items in places:
                    for kind, c, b, bk, _ in items:
                        item(A, L, mask, kind, c, bk, b, b)

            prepare(A0, L0, mask0, L0.before[:QUERIES_AT])
            v.wait_ge(w_in, counts["w_in"])
            for g in range(4):
                v.wait_ge(E["q0_hi"], g + 1)
                link(nc.vector.scalar_tensor_tensor(q0(g)[32:64, :], q0_bank[g][32:64, 0:TOK], bq0[32:64, g:g + 1],
                                                    q0(g)[32:64, :], ALU.add, ALU.subtract))
                for j in range(4):
                    dst = QS[:].rearrange("p b (g j q) -> p b g j q", g=4, j=4)[:, :, g, j, :]
                    last = nc.vector.tensor_scalar(dst, q0(g).rearrange("p (b q) -> p b q", b=B), qmask[:, j:j + 1], None,
                                                   ALU.mult)
                link(last, "q0_stacked")
            prepare(A0, L0, mask0, L0.before[QUERIES_AT:])
            steps(v, lambda s, par: step(A0, L0, mask0, s, par))
            v.wait_ge(moe_in, counts["moe_in"])
            for j in range(4):
                last = nc.vector.tensor_scalar(wo0[:, j, :], woT[:], qmask[:, j:j + 1], None, ALU.mult)
            link(last)
            normalise(A0, L0, B - 1, 1)
            v.wait_ge(A0["normed"], B)
            link(nc.vector.tensor_scalar(O2[:, 0:4, :], O2[:, 0:4, :], bv0[:, 0:1], None, ALU.add), "acc_divided")

            v.wait_ge(E["tanh_ready"], 1)
            v.wait_ge(E["wo0_done"], 1)
            ob = moe[:]
            link(nc.vector.tensor_tensor(ob, bank[2][0:RT, :].rearrange("p (i d) -> p i d", i=NTT),
                                         bo_bc[0:RT, None, :].broadcast_to([RT, NTT, 128]), ALU.add))
            link(nc.vector.scalar_tensor_tensor(x[:], ob, tgates[0:RT, 0:1], x[:], ALU.mult, ALU.add))

            layernorm(x, z, 1)
            v.wait_ge(E["logits_done"], 1)
            L, E_, s1, s2, o1, o2, w_, m_, t_ = (sm[:, k] for k in range(9))

            def col(k):
                return sm1[0:RT, 8 + k, :]

            def bc(a):
                return a[:, :, None].broadcast_to([RT, NTT, NE])

            link(nc.vector.tensor_tensor(L, bank[3][0:RT, 0:NTT * NE].rearrange("p (i e) -> p i e", e=NE),
                                         gb_bc[0:RT, None, :].broadcast_to([RT, NTT, NE]), ALU.add))
            link(nc.vector.tensor_reduce(col(0), L, AX.X, ALU.max))
            link(nc.vector.tensor_tensor(L, L, bc(col(0)), ALU.subtract), "logit_ready")
            v.wait_ge(E["gate_exp"], 1)
            link(nc.vector.tensor_reduce(col(1), E_, AX.X, ALU.add))
            link(nc.vector.reciprocal(col(2), col(1)))
            link(nc.vector.tensor_tensor(s1, E_, bc(col(2)), ALU.mult))

            def first_best(s, o):
                link(nc.vector.tensor_reduce(col(3), s, AX.X, ALU.max))
                link(nc.vector.tensor_tensor(t_, s, bc(col(3)), ALU.is_equal))
                link(nc.vector.tensor_tensor(t_, t_, iota8[:], ALU.mult))
                link(nc.vector.tensor_reduce(col(4), t_, AX.X, ALU.max))
                link(nc.vector.tensor_tensor(o, iota8[:], bc(col(4)), ALU.is_equal))

            first_best(s1, o1)
            link(nc.vector.scalar_tensor_tensor(s2, o1, -2.0, s1, ALU.mult, ALU.add))
            first_best(s2, o2)
            link(nc.vector.tensor_tensor(m_, o1, o2, ALU.add))
            link(nc.vector.tensor_tensor(w_, m_, s1, ALU.mult))
            link(nc.vector.scalar_tensor_tensor(t_, w_, 0.0, iota1[:], ALU.is_gt, ALU.mult))
            link(nc.vector.tensor_reduce(col(5), t_, AX.X, ALU.max))
            link(nc.vector.tensor_tensor(m_, iota1[:], bc(col(5)), ALU.is_equal), "winner_ready")

            def add_expert(e):
                v.wait_ge(E["expert_out"], e + 1)
                for i in range(NTT):
                    y = bank[6][0:RT, i * 128:i * 128 + 128]
                    if e == 0:
                        last = nc.vector.tensor_scalar(moe[:, i, :], y, m_[:, i, e:e + 1], None, ALU.mult)
                    else:
                        last = nc.vector.scalar_tensor_tensor(moe[:, i, :], y, m_[:, i, e:e + 1], moe[:, i, :],
                                                              ALU.mult, ALU.add)
                link(last, "expert_added")

            for e in range(NE):
                if e >= 2:
                    v.wait_ge(E["xw_tr"], e - 1)
                link(nc.vector.tensor_tensor(xw[:, e % 2], z[:], w_[:, :, e:e + 1].broadcast_to([RT, NTT, 128]), ALU.mult),
                     "xw_ready")
                if e >= 1:
                    add_expert(e - 1)
            add_expert(NE - 1)
            v.wait_ge(E["b2_done"], 1)
            link(nc.vector.tensor_tensor(moe[:], bank[2][0:RT, :].rearrange("p (i d) -> p i d", i=NTT), moe[:], ALU.add))
            link(nc.vector.scalar_tensor_tensor(x[:], moe[:], tgates[0:RT, 2:3], x[:], ALU.mult, ALU.add))

            for b in range(2):
                for k in range(NT + 1):
                    stats1(b, b, k)
            layernorm(x, moe, 2)
            layernorm(moe, z, 3)
            v.wait_ge(fill, 10)
            for h in range(H):
                v.wait_ge(E["q1_hi"], h + 1)
                src = prep_bank[h % 3]
                q = slice(h * S, h * S + S)
                signal(nc.vector.tensor_tensor(QB[0:64, :, q], src[0:64, 0:TOK].rearrange("p (b q) -> p b q", b=B),
                                               QS[0:64, :, q], ALU.subtract), "q1_lo")
            for c in range(FC):
                v.wait_ge(E["ff_exp"], c + 1)
                e1, hb, gb = O2[:, c, :], bank[2 + 2 * (c % 2)][:, 0:TOK], bank[3 + 2 * (c % 2)][:, 0:TOK]
                link(nc.vector.tensor_scalar(e1, e1, 1.0, None, ALU.add))
                link(nc.vector.reciprocal(e1, e1))
                link(nc.vector.tensor_tensor(e1, e1, gb, ALU.mult))
                link(nc.vector.tensor_tensor(sT(c), e1, hb, ALU.mult), "ff_silu")

            v.wait_ge(bc_in, BC_IN)
            for k, w in enumerate((bw1[:], bw2[:].rearrange("p c d -> p (c d)"))):
                link(nc.vector.tensor_reduce(wqs[:, k:k + 1], w, AX.X, ALU.add, apply_absolute_value=True), "wabs_ready")
            v.wait_ge(E["wmean_done"], 1)
            link(nc.vector.tensor_scalar(wqs[:, 2:4], bank[3][:, 0:2], 1.0 / (D * FF), EPS, ALU.mult, ALU.max))
            link(nc.vector.reciprocal(wqs[:, 4:6], wqs[:, 2:4]))
            for k, w in enumerate((bw1[:], bw2[:].rearrange("p c d -> p (c d)"))):
                link(nc.vector.tensor_scalar(w, w, wqs[:, 4 + k:5 + k], ROUND, ALU.mult, ALU.add))
                link(nc.vector.tensor_scalar(w, w, ROUND, 1.0, ALU.subtract, ALU.min))
                if k == 0:
                    link(nc.vector.tensor_scalar(w, w, -1.0, wqs[:, 2:3], ALU.max, ALU.mult))
                else:
                    link(nc.vector.tensor_scalar(bw2t[:].rearrange("p c d -> p (c d)"), w, -1.0, None, ALU.max))

            v.wait_ge(fill, 10)
            prepare(A1, L1, mask1, L1.before)
            steps(v, lambda s, par: step(A1, L1, mask1, s, par))
            normalise(A1, L1, B - 1, 1)

            v.wait_ge(E["out1_done"], 1)
            link(nc.vector.scalar_tensor_tensor(x[:], bank[2][0:RT, :].rearrange("p (i d) -> p i d", i=NTT), tgates[0:RT, 1:2],
                                                x[:], ALU.mult, ALU.add))
            layernorm(x, z, 4)

            def quantise(src, dst, inv, ints, key):
                link(nc.vector.tensor_reduce(inv, src, AX.X, ALU.max, apply_absolute_value=True))
                link(nc.vector.tensor_scalar(inv, inv, EPS, 1.0 / 127.0, ALU.max, ALU.mult))
                sc = sm1[0:RT, 20, :]
                link(nc.vector.reciprocal(sc, inv))
                for i in range(NTT):
                    link(nc.vector.tensor_scalar(src[:, i], src[:, i], sc[:, i:i + 1], ROUND, ALU.mult, ALU.add))
                link(nc.vector.tensor_scalar(src, src, ROUND, 127.0, ALU.subtract, ALU.min))
                if ints:
                    link(nc.vector.tensor_scalar(dst, src, -128.0, None, ALU.max), key)
                else:
                    for i in range(NTT):
                        last = nc.vector.tensor_scalar(dst[:, i], src[:, i], -128.0, inv[:, i:i + 1], ALU.max, ALU.mult)
                    link(last, key)

            quantise(z[:], moe[:], sm1[0:RT, 21, :], False, "xq_ready")
            for c in range(FC):
                v.wait_ge(E["lin1_done"], c + 1)
                hb = bank[2 + c][:, 0:TOK].rearrange("p (b q) -> p b q", b=B)
                d = uT[:, 0, c, :].rearrange("p (b q) -> p b q", b=B)
                link(nc.vector.tensor_scalar(d, hb, convw[:, c, 1:2], convb[:, c:c + 1], ALU.mult, ALU.add))
                link(nc.vector.scalar_tensor_tensor(d[:, :, 1:S], hb[:, :, 0:S - 1], convw[:, c, 0:1], d[:, :, 1:S],
                                                    ALU.mult, ALU.add))
                link(nc.vector.scalar_tensor_tensor(d[:, :, 0:S - 1], hb[:, :, 1:S], convw[:, c, 2:3], d[:, :, 0:S - 1],
                                                    ALU.mult, ALU.add), "conv_done")
            for c in range(FC):
                v.wait_ge(E["conv_exp"], c + 1)
                e1 = uT[:, 1, c, :]
                link(nc.vector.tensor_scalar(e1, e1, 1.0, None, ALU.add))
                link(nc.vector.reciprocal(e1, e1))
                link(nc.vector.tensor_tensor(sT(c), e1, uT[:, 0, c, :], ALU.mult), "silu_done")
            h2 = O2[0:RT, 0:5, :].rearrange("p a n -> p (a n)")[:, 0:NTT * FF].rearrange("p (i f) -> p i f", i=NTT)
            q2 = QS[0:RT, 0:3, :].rearrange("p a n -> p (a n)")[:, 0:NTT * FF].rearrange("p (i f) -> p i f", i=NTT)
            for i in range(NTT):
                v.wait_ge(E["back_tr"], i + 1)
                link(nc.vector.tensor_copy(h2[:, i, :], bank[2 + i][0:RT, :]))
            quantise(h2, q2, sm1[0:RT, 22, :], True, "hq_ready")
            link(nc.vector.tensor_scalar(wqs[:, 6:7], wqs[:, 3:4], tgates[:, 3:4], None, ALU.mult))
            link(nc.vector.tensor_scalar(sm1[0:RT, 23, :], sm1[0:RT, 22, :], wqs[0:RT, 6:7], None, ALU.mult))
            v.wait_ge(E["lin2_done"], 1)
            for i in range(NTT):
                link(nc.vector.scalar_tensor_tensor(x[:, i, :], bank[7][0:RT, i * 128:i * 128 + 128], sm1[0:RT, 23, i:i + 1],
                                                    x[:, i, :], ALU.mult, ALU.add), "final_done")

        def hqT(c):
            return QB[:, 0:2, :].rearrange("p a n -> p (a n)")[:, c * TOK:c * TOK + TOK]

        def hq_bank(c):
            return bank[3 + c][:].bitcast(bf16)[:, 0:TOK]

        @block.scalar
        def _(a):
            def done(ins, key):
                ins.then_inc(E[key], 1)

            def item(A, L, kind, c, bk, b, par):
                cols = slice(c * CH, c * CH + CH)
                if kind == "T":
                    need(a, A["tr_done"], NCH * b + c + 1)
                    if L.n == 0:
                        ins = nc.scalar.copy(xT[:, cols], bank[bk][:, 0:CH])
                    else:
                        ins = nc.scalar.activation(xT[:, cols], bank[bk][:, 0:CH], ACT.Identity, bias=lng[:, 3:4],
                                                   scale=lng[:, 2:3])
                    ins.then_inc(A["tr_evac"], 1)
                elif kind == "K":
                    need(a, A["kproj"], NCH * b + c + 1)
                    if L.n == 0:
                        if c == 0:
                            for g in range(4):
                                need(a, A[f"stacked{g}"], STACKED * b)
                        ins = nc.scalar.activation(khi[:, cols], bank[bk][:, 0:CH], ACT.Identity, bias=bk0[:, 0:1])
                    else:
                        ins = nc.scalar.copy(KS[:, par, 0, cols], bank[bk][:, 0:CH])
                    ins.then_inc(A["khi_ready"], 1)
                elif kind == "V":
                    need(a, A["vproj"], NCH * b + c + 1)
                    first = 0 if L.n == 0 else DK1
                    nc.scalar.copy(VS[:, par, c * TPC:c * TPC + TPC, 0:128 - first],
                                   bank[bk][0:KT, :].rearrange("p (t n) -> p t n", t=TPC)[:, :, first:128])\
                        .then_inc(A["v_ready"], 1)

            def normalise(b, par, first, end):
                if first == 0:
                    need(a, A1["shift"], b + 1)
                    need(a, A1["tr_done"], NCH * (b - 1))
                for t_ in range(first, end):
                    nc.scalar.activation(cn[:, par, t_, :], ctxN[:, par, t_, :], ACT.Identity,
                                         bias=st1[0:KT, 6 * par + 4, t_:t_ + 1], scale=st1[0:KT, 6 * par + 5, t_:t_ + 1])\
                        .then_inc(A1["cn_ready"], 1)

            def step(A, L, scale, s, par):
                for k in range(NH2):
                    need(a, A["scores"], NH2 * s + k + 1)
                    old = k // 2 - RING_P // 2
                    if old >= 0:
                        need(a, A["pv"], NT * s + old + 1)
                        need(a, A[f"sum{k % 2}"], (NT - 1) * s + max(old, 1))
                    else:
                        need(a, A["pv"], NT * s + old + 1)
                        need(a, A[f"sum{k % 2}"], (NT - 1) * (s - 1) + NT + old)
                    nc.scalar.activation(P[:, k % RING_P, :], score_bank[k % RING_S][0:KT, 0:HALF], ACT.Exp, scale=scale)\
                        .then_inc(A["exps"], 1)
                    if k >= 1:
                        for kind, c, ahead, bk, _ in L.items(s)[k - 1]:
                            item(A, L, kind, c, bk, s + ahead, (par + ahead) % 2)
                    if L.n == 1 and exists(s, 2) and NORM_AT <= k < NORM_AT + NT // 2:
                        first = 2 * (k - NORM_AT)
                        normalise(s + 2, par, first, first + 2)

            def prepare(A, L, places):
                for items in places:
                    for kind, c, b, bk, _ in items:
                        item(A, L, kind, c, bk, b, b)

            a.wait_ge(k_in, counts["k_in"])
            prepare(A0, L0, L0.before[:QUERIES_AT])
            a.wait_ge(E["tok_tr"], 1)
            done(nc.scalar.copy(zT[:], bank[2][:, 0:TOK]), "zT_ready")
            a.wait_ge(w_in, counts["w_in"])
            a.wait_ge(fill, 2)
            for g in range(4):
                a.wait_ge(E["q0_proj"], g + 1)
                if g >= 2:
                    a.wait_ge(E["q0_stacked"], g - 1)
                done(nc.scalar.activation(q0(g), q0_bank[g][:, 0:TOK], ACT.Identity, bias=bq0[:, g:g + 1]), "q0_hi")
            prepare(A0, L0, L0.before[QUERIES_AT:])
            steps(a, lambda s, par: step(A0, L0, DK0 ** -0.5, s, par))

            a.wait_ge(moe_in, counts["moe_in"])
            done(nc.scalar.activation(tgates[:], gates[:], ACT.Tanh), "tanh_ready")
            a.wait_ge(E["tok_tr"], 2)
            done(nc.scalar.copy(zT[:], bank[2][:, 0:TOK]), "zT_ready")
            a.wait_ge(E["logit_ready"], 1)
            done(nc.scalar.activation(sm[:, 1], sm[:, 0], ACT.Exp), "gate_exp")
            for e in range(NE):
                a.wait_ge(E["xw_tr"], e + 1)
                if e >= 2:
                    a.wait_ge(E["up_done"], FC * (e - 2) + FC)
                done(nc.scalar.copy(xwT[:, e % 2, :], bank[e % 2][:, 0:TOK]), "xwT_ready")
                for c in range(FC):
                    if c == 0 and e >= 2:
                        a.wait_ge(E["expert_out"], e - 1)
                    a.wait_ge(E["up_done"], FC * e + c + 1)
                    done(nc.scalar.activation(hT[:, e % 2, c, :], bank[2 + c][:, 0:TOK], ACT.Relu, bias=b1[:, e, c:c + 1]), "hidden_ready")
            a.wait_ge(E["disp_tr"], 1)
            done(nc.scalar.copy(dispT, bank[7][0:NE, 0:TOK]), "dispT_ready")
            a.wait_ge(bc_in, BC_IN)
            a.wait_ge(E["tok_tr"], 3)
            done(nc.scalar.activation(zT[:], bank[2][:, 0:TOK], ACT.Identity, bias=lng[:, 1:2], scale=lng[:, 0:1]), "zT_ready")
            for h in range(H):
                a.wait_ge(E["q1_proj"], h + 1)
                done(nc.scalar.copy(QS[:, :, h * S:h * S + S], prep_bank[h % 3][:, 0:TOK].rearrange("p (b q) -> p b q", b=B)), "q1_hi")
            for c in range(FC):
                a.wait_ge(E["ff_proj"], c + 1)
                done(nc.scalar.activation(O2[:, c, :], bank[3 + 2 * (c % 2)][:, 0:TOK], ACT.Exp, scale=-1.0), "ff_exp")

            for b in range(2):
                normalise(b, b, 0, NT)
            prepare(A1, L1, L1.before)
            steps(a, lambda s, par: step(A1, L1, DK1 ** -0.5, s, par))

            a.wait_ge(E["tok_tr"], 4)
            done(nc.scalar.copy(zT[:], bank[0][:, 0:TOK]), "zT_ready")
            for c in range(FC):
                a.wait_ge(E["conv_done"], c + 1)
                done(nc.scalar.activation(uT[:, 1, c, :], uT[:, 0, c, :], ACT.Exp, scale=-1.0), "conv_exp")
            for c in range(FC):
                a.wait_ge(E["hq_tr"], c + 1)
                done(nc.scalar.copy(hqT(c), hq_bank(c)), "hqT_ready")

        @block.tensor
        def _(pe):
            def done(ins, key):
                ins.then_inc(E[key], 1)

            def tokens_transposed(src, dst):
                for i in range(NTT):
                    last = nc.tensor.transpose(dst[:, i * RT:i * RT + RT], src[:, i, :], ident[0:RT, 0:RT])
                return last

            def item(A, L, kind, c, bk, after, b, par):
                if after is not None:
                    need(pe, *released(A, after, after[2]))
                elif kind != "M":
                    need(pe, A["sum_rec"], b - 1)
                if kind == "T":
                    if c == 0:
                        if L.n == 0:
                            need(pe, A[f"ctx_in{par}"], ctx_count(b, par))
                        else:
                            need(pe, A["cn_ready"], NT * (b + 1))
                    src = ctxN if L.n == 0 else cn
                    for k in range(TPC):
                        last = nc.tensor.transpose(bank[bk][:, k * KT:k * KT + KT], src[:, par, c * TPC + k, :],
                                                   ident[0:KT, 0:KT])
                    last.then_inc(A["tr_done"], 1)
                elif kind == "K":
                    need(pe, A["tr_evac"], NCH * b + c + 1)
                    nc.tensor.matmul(bank[bk][:, 0:CH], wkT[:] if L.n == 0 else wk1[:].rearrange("p a n -> p (a n)"),
                                     xT[:, c * CH:c * CH + CH], start=True, stop=True).then_inc(A["kproj"], 1)
                elif kind == "V":
                    need(pe, A["klo_ready"], NCH * b + c + 1)
                    for k in range(TPC):
                        kk = (c * TPC + k) * KT
                        last = nc.tensor.matmul(bank[bk][0:KT, k * 128:k * 128 + 128], xT[:, kk:kk + KT],
                                                wvT[:] if L.n == 0 else wv1[:], start=True, stop=True)
                    last.then_inc(A["vproj"], 1)
                elif kind == "M":
                    rt, j = L.max_chunk(c)
                    if c < 2:
                        need(pe, A["max_in_q"], 2 * b)
                    need(pe, A["max_taken"], L.nmax * b + c - 1)
                    if L.n == 1 and rt == 0:
                        need(pe, A["klo_ready"], NCH * b + j + 1)
                    if L.n == 0 and j == 0 and rt % 2 == 0:
                        need(pe, A[f"stacked{rt // 2}"], STACKED * (b + 1))
                    nc.tensor.matmul(bank[c % 2][0:L.rows, 0:CH],
                                     QS[:, bass.ds(b, 1), rt * L.rows:rt * L.rows + L.rows].rearrange("p o n -> p (o n)"),
                                     KS[:, par, rt // 2 if L.n == 0 else 0, j * CH:j * CH + CH],
                                     start=True, stop=True).then_inc(A["max_scores"], 1)
                elif kind == "R":
                    need(pe, A["max_block"], b + 1)
                    for rt in range(L.tiles):
                        half, col = divmod(rt * L.rows, L.split)
                        last = nc.tensor.matmul((bank[7], bank[0])[half][L.spare:L.spare + 32, col:col + L.rows],
                                                MB[0:L.rows, rt, :], identb[0:L.rows, 0:L.rows], start=True, stop=True,
                                                tile_position=(0, L.spare))
                        if col + L.rows == L.split or rt == L.tiles - 1:
                            last.then_inc(A["max_row"], 1)

            def scores(A, L, b, par, k):
                t_, half = divmod(k, 2)
                need(pe, A["exps"], NH2 * b + k + 1 - RING_S)
                if k == 0:
                    need(pe, A["max_in_q"], 2 * (b + 1))
                keys = slice(t_ * KT, t_ * KT + KT)
                dst = score_bank[k % RING_S]
                if L.n == 0:
                    for j in range(2):
                        g = 2 * half + j
                        last = nc.tensor.matmul(dst[0:KT, j * 224:j * 224 + 224], KS[:, par, g, keys],
                                                QS[:, bass.ds(b, 1), g * 224:g * 224 + 224].rearrange("p o n -> p (o n)"),
                                                start=True, stop=True)
                else:
                    cols = slice(half * HALF, half * HALF + HALF)
                    nc.tensor.matmul(dst[0:KT, 0:HALF], KS[:, par, 0, keys],
                                     QS[:, bass.ds(b, 1), cols].rearrange("p o n -> p (o n)"), start=True, stop=False)
                    last = nc.tensor.matmul(dst[0:KT, 0:HALF], KS[:, par, 1, keys],
                                            QB[:, bass.ds(b, 1), cols].rearrange("p o n -> p (o n)"), start=False, stop=True)
                last.then_inc(A["scores"], 1)

            def values(A, L, b, par, t_):
                need(pe, A["exps"], NH2 * b + 2 * t_ + 2)
                if t_ == 0:
                    need(pe, A["v_ready"], NCH * (b + 1))
                    need(pe, A["normed"], b - 1)
                n_ = HS * L.group // 128
                for g in range(128 // L.group):
                    half, col = divmod(g * n_, HALF)
                    first = g * 32 if L.n == 0 else 0
                    last = nc.tensor.matmul(acc_bank[par][L.group * g:L.group * g + L.group, 0:n_],
                                            VS[:, par, t_, first:first + L.group],
                                            P[:, (2 * t_ + half) % RING_P, col:col + n_],
                                            start=(t_ == 0), stop=(t_ == NT - 1), tile_position=(0, L.group * g))
                last.then_inc(A["pv"], 1)

            def sums(A, L, b):
                for half in range(2):
                    need(pe, A[f"sum{half}"], (NT - 1) * (b + 1))
                n_ = HS * L.group // 128
                for g in range(128 // L.group):
                    half, col = divmod(g * n_, HALF)
                    last = nc.tensor.matmul(bank[7][L.group * g:L.group * g + L.group, 0:n_], ones[0:KT, 0:L.group],
                                            SP[:, half, col:col + n_], start=True, stop=True,
                                            tile_position=(0, L.group * g))
                last.then_inc(A["sums_mm"], 1)

            def attend(A, L, s, par):
                scores(A, L, s, par, 0)
                scores(A, L, s, par, 1)
                for p in range(NH2):
                    if p == SUMS_AT and not (isinstance(s, int) and s == 0):
                        sums(A, L, s - 1)
                    if p + 2 < NH2:
                        scores(A, L, s, par, p + 2)
                    for kind, c, ahead, bk, after in L.items(s)[p]:
                        if after is not None:
                            after = (*after[0:2], s + after[2])
                        item(A, L, kind, c, bk, after, s + ahead, (par + ahead) % 2)
                    if p % 2 == 1:
                        values(A, L, s, par, p // 2)

            def prepare(A, L, places):
                for items in places:
                    for kind, c, b, bk, after in items:
                        item(A, L, kind, c, bk, after, b, b)

            pe.wait_ge(x_in, counts["x_in"])
            pe.wait_ge(k_in, counts["k_in"])
            prepare(A0, L0, L0.before[:QUERIES_AT])
            pe.wait_ge(E["z_ready"], 1)
            done(tokens_transposed(z, bank[2]), "tok_tr")
            pe.wait_ge(w_in, counts["w_in"])
            pe.wait_ge(fill, 2)
            pe.wait_ge(E["zT_ready"], 1)
            for g in range(4):
                done(nc.tensor.matmul(q0_bank[g][:, 0:TOK], wq0[:, g].rearrange("p r n -> p (r n)"), zT[:],
                                      start=True, stop=True), "q0_proj")
            pe.wait_ge(E["q0_stacked"], 4)
            pe.wait_ge(fill, 7)
            pe.wait_ge(E["identb_ready"], 1)
            prepare(A0, L0, L0.before[QUERIES_AT:])
            steps(pe, lambda s, par: attend(A0, L0, s, par))
            sums(A0, L0, B - 1)

            pe.wait_ge(E["acc_divided"], 1)
            for i in range(NTT):
                for j in range(4):
                    last = nc.tensor.matmul(bank[2][0:RT, i * 128:i * 128 + 128], O2[:, j, i * RT:i * RT + RT], wo0[:, j, :],
                                            start=(i == 0 and j == 0), stop=(j == 3), skip_group_check=True)
            done(last, "wo0_done")

            pe.wait_ge(E["z_ready"], 2)
            done(tokens_transposed(z, bank[2]), "tok_tr")
            pe.wait_ge(E["zT_ready"], 2)
            for i in range(NTT):
                last = nc.tensor.matmul(bank[3][0:RT, i * NE:i * NE + NE], zT[:, i * RT:i * RT + RT], gate_w[:],
                                        start=True, stop=True)
            done(last, "logits_done")

            def down(e):
                if e >= 1:
                    pe.wait_ge(E["expert_added"], e)
                pe.wait_ge(E["hidden_ready"], FC * e + FC)
                for i in range(NTT):
                    for c in range(FC):
                        last = nc.tensor.matmul(bank[6][0:RT, i * 128:i * 128 + 128], hT[:, e % 2, c, i * RT:i * RT + RT],
                                                w2[:, e, c, :], start=(i == 0 and c == 0), stop=(c == FC - 1),
                                                skip_group_check=True)
                done(last, "expert_out")

            for e in range(NE):
                pe.wait_ge(E["xw_ready"], e + 1)
                if e >= 2:
                    pe.wait_ge(E["xwT_ready"], e - 1)
                done(tokens_transposed(xw[:, e % 2], bank[e % 2]), "xw_tr")
                pe.wait_ge(E["xwT_ready"], e + 1)
                for c in range(FC):
                    if e >= 1:
                        pe.wait_ge(E["hidden_ready"], FC * (e - 1) + c + 1)
                    done(nc.tensor.matmul(bank[2 + c][:, 0:TOK], w1[:, e, c * 128:c * 128 + 128], xwT[:, e % 2, :],
                                          start=True, stop=True), "up_done")
                if e >= 1:
                    down(e - 1)
            for i in range(NTT):
                last = nc.tensor.transpose(bank[7][0:NE, i * RT:i * RT + RT], sm[:, 7, i, :], ident[0:RT, 0:RT])
            done(last, "disp_tr")
            down(NE - 1)
            pe.wait_ge(E["dispT_ready"], 1)
            for i in range(NTT):
                last = nc.tensor.matmul(bank[2][0:RT, i * 128:i * 128 + 128], dispT[:, i * RT:i * RT + RT], b2[:],
                                        start=True, stop=True)
            done(last, "b2_done")

            pe.wait_ge(E["z_ready"], 4)
            done(tokens_transposed(z, bank[2]), "tok_tr")
            pe.wait_ge(bc_in, BC_IN)
            pe.wait_ge(E["zT_ready"], 3)
            for h in range(H):
                if h >= 3:
                    pe.wait_ge(E["q1_lo"], h - 2)
                done(nc.tensor.matmul(prep_bank[h % 3][:, 0:TOK], wq1[:, h].rearrange("p a n -> p (a n)"), zT[:],
                                      start=True, stop=True), "q1_proj")
            for c in range(FC):
                if c >= 2:
                    pe.wait_ge(E["ff_silu"], c - 1)
                nc.tensor.matmul(bank[2 + 2 * (c % 2)][:, 0:TOK], wff1[:, c, :], zT[:], start=True, stop=True)
                done(nc.tensor.matmul(bank[3 + 2 * (c % 2)][:, 0:TOK], wff1[:, FC + c, :], zT[:], start=True, stop=True), "ff_proj")
            pe.wait_ge(E["wabs_ready"], 2)
            done(nc.tensor.matmul(bank[3][:, 0:2], ones[:], wqs[:, 0:2], start=True, stop=True), "wmean_done")

            pe.wait_ge(E["q1_lo"], H)
            pe.wait_ge(fill, 10)
            prepare(A1, L1, L1.before)
            steps(pe, lambda s, par: attend(A1, L1, s, par))
            sums(A1, L1, B - 1)

            pe.wait_ge(A1["normed"], B)
            for i in range(NTT):
                for k in range(H // 2 + FC):
                    lhsT = O2[:, k, i * RT:i * RT + RT] if k < H // 2 else sT(k - H // 2)[:, i * RT:i * RT + RT]
                    rhs = wo1[:, k, :] if k < H // 2 else wff2[:, k - H // 2, :]
                    last = nc.tensor.matmul(bank[2][0:RT, i * 128:i * 128 + 128], lhsT, rhs, start=(i == 0 and k == 0),
                                            stop=(k == H // 2 + FC - 1), skip_group_check=True)
            done(last, "out1_done")

            pe.wait_ge(E["xq_ready"], 1)
            done(tokens_transposed(moe, bank[0]), "tok_tr")
            pe.wait_ge(E["zT_ready"], 4)
            for c in range(FC):
                done(nc.tensor.matmul(bank[2 + c][:, 0:TOK], bw1[:, c * 128:c * 128 + 128], zT[:], start=True, stop=True), "lin1_done")
            pe.wait_ge(E["silu_done"], FC)
            for i in range(NTT):
                for c in range(FC):
                    last = nc.tensor.transpose(bank[2 + i][0:RT, c * 128:c * 128 + 128], sT(c)[:, i * RT:i * RT + RT], ident[:])
                done(last, "back_tr")
            pe.wait_ge(E["hq_ready"], 1)
            q2 = QS[0:RT, 0:3, :].rearrange("p a n -> p (a n)")[:, 0:NTT * FF].rearrange("p (i f) -> p i f", i=NTT)
            for c in range(FC):
                for i in range(NTT):
                    last = nc.tensor.transpose(hq_bank(c)[:, i * RT:i * RT + RT], q2[:, i, c * 128:c * 128 + 128],
                                               identb[0:RT, 0:RT])
                done(last, "hq_tr")
            pe.wait_ge(E["hqT_ready"], FC)
            for i in range(NTT):
                for c in range(FC):
                    last = nc.tensor.matmul(bank[7][0:RT, i * 128:i * 128 + 128], hqT(c)[:, i * RT:i * RT + RT],
                                            bw2t[:, c, :], start=(i == 0 and c == 0), stop=(c == FC - 1), skip_group_check=True)
            done(last, "lin2_done")


def kernel(**inputs):
    import numpy as np
    import concourse.bacc as bacc
    from concourse.bass_utils import run_bass_kernel_spmd

    arrays = {k: np.ascontiguousarray(v) for k, v in inputs.items()}
    for new, old in (("wkT", "L0_xattn_Wk"), ("wvT", "L0_xattn_Wv"), ("wqT", "L0_xattn_Wq"), ("woT", "L0_xattn_Wo"),
                     ("bw1T", "L1_ffn_w1"), ("bw2T", "L1_ffn_w2")):
        arrays[new] = np.ascontiguousarray(arrays.pop(old).T)
    arrays["c_ident"] = np.eye(128, dtype=np.float32)
    p = np.arange(128)
    arrays["c_qmask"] = ((p[:, None] % 32) // DK0 == np.arange(4)).astype(np.float32)
    head = 2 * np.arange(2)[None, :] + np.arange(RT)[:, None] // S
    arrays["c_mmask0"] = -(head[:, :, None] == np.arange(32)).astype(np.float32)
    arrays["c_mmask1"] = -np.tile(np.arange(32) == 0, (128, 1)).astype(np.float32)
    arrays["c_iota8"] = np.tile(np.arange(NE, 0, -1, dtype=np.float32), (RT, NTT, 1))
    arrays["c_iota1"] = np.tile(np.arange(1, NE + 1, dtype=np.float32), (RT, NTT, 1))

    nc = bacc.Bacc("TRN2", target_bir_lowering=False, num_devices=1)
    t = {k: nc.dram_tensor(f"in_{k}", a.shape, mybir.dt.from_np(a.dtype), kind="ExternalInput").ap()
         for k, a in arrays.items()}
    out = nc.dram_tensor("out", (B, S, D), fp32, kind="ExternalOutput").ap()
    build(nc, t, out)
    r = run_bass_kernel_spmd(nc, [{f"in_{k}": a for k, a in arrays.items()}], core_ids=[0])
    return r.results[0]["out"]
```

```python
import concourse.bass as bass
from concourse import mybir
from contextlib import ExitStack

B, S, D = 8, 56, 128
NK = 1500
H = 16
KT, NT = 125, 12
HS = H * S
HALF = HS // 2
RT = 2 * S
TOK = B * S
NTT = TOK // RT
CH, NCH = 500, 3
TPC = CH // KT
NH2 = 2 * NT
DK0, DK1 = 8, 64
NE, FF = 8, 512
FC = FF // 128
EPS = 1e-5
STACKED = 3 * 16
RSTD_TILE = 7
SUMS_AT = (0, 1)
ADD_LAG = 1
NORM_AT = 18
LAG = (0, 2)
QUERIES_AT = 5
OUT_AT = (8, 10, 14)
RING_S, RING_P = 3, 6
OUT_PARTS = 2
ROUND = 12582912.0


class Layer:

    def __init__(self, n, rows, spare, group, banks, before, beside):
        self.n, self.rows, self.spare, self.group = n, rows, spare, group
        self.tiles = HS // rows
        self.nmax = self.tiles * NCH
        self.split = (self.tiles + 1) // 2 * rows
        self.before = self.scheduled(before, banks, 2)
        self.beside = [self.scheduled(beside, (7,), ahead) for ahead in range(3)]

    def scheduled(self, places, banks, most):
        schedule, held, turn = [[] for _ in range(NH2)], {}, 0
        for p, kind, c, ahead in sorted(places):
            if ahead > most:
                continue
            bank = None
            if kind in "TKV":
                bank, turn = banks[turn % len(banks)], turn + 1
            elif kind == "R":
                bank = 7
            schedule[p].append((kind, c, ahead, bank, held.get(bank)))
            if bank is not None:
                held[bank] = (kind, c, ahead)
        return schedule

    def max_banks(self, b):
        return ((0, 1, 2, 3), (0, 1, 6))[self.n] if isinstance(b, int) and b == 0 else (0, 1)

    def max_chunk(self, c, b):
        return divmod(c, NCH) if self.n == 0 or (isinstance(b, int) and b == 0) else divmod(c, self.tiles)[::-1]

    def sums(self, bank, acc_bank, par):
        n = HS * self.group // 128
        return acc_bank[par][:, n:2 * n] if self.n == 0 else bank[7][:, 0:n]

    def context(self, par):
        return par if self.n == 0 else 0

    def items(self, s):
        return self.beside[sum(exists(s, ahead) for ahead in (1, 2))]


def spread(kind, ahead, places, first=0):
    return [(p, kind, first + c, ahead) for c, p in enumerate(places)]


def evenly(lo, hi, n):
    return [lo + i * (hi - lo + 1) // n for i in range(n)]


def placed(*counts):
    return [p for p, n in enumerate(counts) for _ in range(n)]


L0 = Layer(0, 2 * S, 96, 32, (6, 7),
           spread("K", 0, (0, 0, 1)) + spread("V", 0, (1, 2, 2))
           + spread("M", 0, evenly(5, 7, 24)) + spread("K", 1, (20, 21, 22)) + [(14, "R", 0, 0)],
           spread("V", 1, (0, 1, 2)) + spread("K", 2, (11, 13, 15)) + [(21, "R", 0, 1)]
           + spread("M", 1, placed(0, 2, 2, 1, 1, 2, 1, 1, 0, 2, 1, 1, 2, 1, 1, 1, 2, 1, 2, 0, 0, 0, 0, 0)))
L1 = Layer(1, 128, 64, 64, (7, 1),
           spread("T", 0, (0, 0, 0)) + spread("K", 0, (1, 2, 2)) + spread("V", 0, (3, 3, 3)),
           spread("T", 1, (3, 5, 7)) + spread("K", 1, (4, 6, 9)) + spread("V", 1, (10, 12, 14)) + [(21, "R", 0, 1)]
           + spread("M", 1, placed(0, 0, 0, 0, 0, 2, 1, 1, 2, 2, 0, 2, 2, 1, 0, 2, 0, 2, 3, 1, 0, 0, 0, 0)))

fp32 = mybir.dt.float32
bf16 = mybir.dt.bfloat16
ALU = mybir.AluOpType
ACT = mybir.ActivationFunctionType
AX = mybir.AxisListType


def need(eng, sem, value):
    if isinstance(value, int) and value <= 0:
        return
    eng.wait_ge(sem, value)


def steps(eng, step):
    for s in range(2):
        step(s, s)
    with eng.Fori(1, B // 2 - 1) as pair:
        for par in range(2):
            step(2 * pair + par, par)
    for s in range(B - 2, B):
        step(s, s % 2)


def first_queries():
    for h in range(H):
        yield "Q", h
        for rt in range(L1.tiles):
            if min((128 * (rt + 1) - 1) // S + 1, H - 1) == h:
                for c in range(NCH):
                    yield "M", rt * NCH + c
    for c in range(FC):
        yield "F", c


def exists(s, ahead):
    return not isinstance(s, int) or s + ahead < B


def released(A, item, b):
    kind, c = item[0], item[1]
    return {"T": (A["tr_evac"], NCH * b + c + 1), "K": (A["klo_ready"], NCH * b + c + 1),
            "V": (A["v_ready"], NCH * b + c + 1), "R": (A["max_in_q"], 2 * b + 1)}[kind]


def ctx_count(b, par):
    return 8 * (b - par) + 16


def build(nc, t, out):
    ctx = ExitStack()
    with ctx:
        ctx.enter_context(nc.allow_non_contiguous_dma(reason="biases, a few hundred values each"))
        def sb(name, shape, dt=fp32):
            return ctx.enter_context(nc.sbuf_tensor(name, shape, dt))

        def sem(name):
            return ctx.enter_context(nc.semaphore(name))

        bank = [ctx.enter_context(nc.psum_tensor(f"bank{i}", [128, 512], fp32)) for i in range(8)]
        q0_bank = [bank[0], bank[1], bank[3], bank[4]]
        score_bank = [bank[2], bank[3], bank[4]]
        q1_bank = score_bank
        acc_bank = [bank[5], bank[6]]

        ident = sb("ident", [128, 128])
        identb = sb("identb", [128, 128], bf16)
        ones = sb("ones", [128, 128])
        qmask = sb("qmask", [128, 4])
        mmask0 = sb("mmask0", [RT, 2, 32])
        mmask1 = sb("mmask1", [128, 32])
        iota8 = sb("iota8", [RT, NTT, NE])
        iota1 = sb("iota1", [RT, NTT, NE])
        gates = sb("gates", [128, 4])
        tgates = sb("tgates", [128, 4])
        wkT = sb("wkT", [128, 128])
        wvT = sb("wvT", [128, 128])
        wq0 = sb("wq0", [128, 4, 4, 32])
        bq0 = sb("bq0", [128, 4])
        bk0 = sb("bk0", [128, 1])
        bv0 = sb("bv0", [128, 1])
        bo_bc = sb("bo_bc", [128, 128])
        wo0 = sb("wo0", [128, 4, 128])
        woT = sb("woT", [128, 128])
        gate_w = sb("gate_w", [128, NE])
        gb_bc = sb("gb_bc", [128, NE])
        w1 = sb("w1", [128, NE, FF])
        b1 = sb("b1", [128, NE, FC])
        w2 = sb("w2", [128, NE, FC, 128])
        b2 = sb("b2", [NE, 128])
        wk1 = sb("wk1", [128, 2, DK1])
        wv1 = sb("wv1", [128, 128])
        wq1 = sb("wq1", [128, H, 2, DK1])
        wo1 = sb("wo1", [128, H // 2, 128])
        wff1 = sb("wff1", [128, 2 * FC, 128])
        wff2 = sb("wff2", [128, FC, 128])
        lng = sb("lng", [128, 4])
        bw1 = sb("bw1", [128, FF])
        bw2 = sb("bw2", [128, FC, 128])
        bw2t = sb("bw2t", [128, FC, 128], bf16)
        convw = sb("convw", [128, FC, 3])
        convb = sb("convb", [128, FC])
        ctxN = sb("ctxN", [KT, 2, NT, 128])
        xT = sb("xT", [128, 2, NK])
        cn = [sb("cn", [KT, NT, 128])[:],
              w1[0:KT].rearrange("p e f -> p (e f)")[:, 0:NT * 128].rearrange("p (t d) -> p t d", d=128)]
        khi = sb("khi", [128, NK], bf16)
        klo = sb("klo", [128, NK], bf16)
        KS = sb("KS", [128, 2, 4, NK], bf16)
        VS = sb("VS", [KT, 2, NT, 128])
        SP = sb("SP", [KT, 2, HALF])
        powers = sb("powers", [128, 2, NT])
        QS = sb("QS", [128, B, HS], bf16)
        QB = sb("QB", [128, B, HS], bf16)
        P = sb("P", [KT, RING_P, HALF])
        O2 = sb("O2", [128, H // 2, TOK])
        mxc = sb("mxc", [128, L0.nmax])
        mx = sb("mx", [128, L0.tiles])
        MB = sb("MB", [128, L0.tiles, 32], bf16)
        rsum = sb("rsum", [128, HALF])
        st6 = sb("st6", [128, NT, 6])
        st1 = sb("st1", [128, 12, NT])
        x = sb("x", [RT, NTT, 128])
        z = sb("z", [RT, NTT, 128])
        zT = sb("zT", [128, TOK])
        hT = QB[:].rearrange("p b n -> p (b n)").bitcast(fp32).rearrange("p (a c n) -> p a c n", a=2, c=FC)
        xw = P[0:RT].rearrange("p a n -> p (a n)")[:, 0:2 * NTT * 128].rearrange("p (a i d) -> p a i d", a=2, d=128)
        xwT = xT[:, 1, 0:2 * TOK].rearrange("p (a n) -> p a n", a=2)
        uT = w2[:].rearrange("p e c d -> p (e c d)")[:, 0:2 * FC * TOK].rearrange("p (a c n) -> p a c n", a=2, c=FC)

        def q0(g):
            return QB[:, 0, g % 2 * TOK:g % 2 * TOK + TOK]

        def stacked_queries(g, j):
            return QS[:].rearrange("p b (g j q) -> p b g j q", g=4, j=4)[:, :, g, j, :]

        def sT(c):
            free = KS[:, c // 2, 2:4, :].rearrange("p a n -> p (a n)").bitcast(fp32)
            return free[:, c % 2 * TOK:c % 2 * TOK + TOK]

        sm = sb("sm", [RT, 12, NTT, NE])
        sm1 = sb("sm1", [128, 24, NTT])
        dispT = rsum[0:NE, :]
        moe = sb("moe", [RT, NTT, 128])
        wqs = sb("wqs", [128, 8])

        k_in, w_in, moe_in, x_in, bc_in = sem("k_in"), sem("w_in"), sem("moe_in"), sem("x_in"), sem("bc_in")
        fill = sem("fill")
        E = {k: sem(k) for k in """
            acc_divided b2_done back_tr conv_centre conv_done conv_left conv_tanh dispT_ready disp_tr
            expert_added expert_out ff_proj ff_silu ff_tanh final_done gate_exp hidden_ready hqT_even
            hqT_odd hq_clipped hq_ready hq_rounded hq_tr identb_ready lin1_done lin2_done logit_ready
            logits_done out1_done q0_hi q0_lo q0_masked q0_proj q0_stacked q1_hi q1_lo q1_proj
            rstd_ready rstd_step silu_done tanh_ready tok_tr up_done var_ready vector_chain wabs_ready
            winner_ready wmean_done wmean_read wo0_done wo0_ready xq_ready xwT_ready xw_ready xw_tr
            zT_ready z_ready
            """.split()}
        out_done = sem("out_done")

        def attention_sems(n):
            names = ("stats_v", "rstd", "shift", "cn_ready", "tr_done", "tr_evac",
                     "kproj", "khi_ready", "klo_ready", "khi_copied", "vproj", "v_ready", "max_scores", "max_taken",
                     "max_final", "max_block", "max_row", "max_in_q", "scores", "exps", "pv",
                     "sum0", "sum1", "sums_mm", "sum_rec", "normed")
            return {k: sem(f"{k}_{n}") for k in names} \
                | {f"ctx_in{par}": sem(f"ctx_in{par}_{n}") for par in range(2)} \
                | ({f"stacked{g}": sem(f"stacked{g}") for g in range(4)} if n == 0 else {})

        A0, A1 = attention_sems(0), attention_sems(1)

        block = ctx.enter_context(nc.Block())
        ctx_h = t["ctx_1024"].rearrange("b (p t) d -> b p t d", t=NT)
        NCONST, NW, NMOE, NX, NBC = [0], [0], [0], [0], [0]
        counts = {"k_in": 0, "w_in": 0, "moe_in": 0, "x_in": 0}

        def add_tile(unit, eng, A, b, half, t_):
            need(eng, A["exps"], NH2 * b + 2 * t_ + half + 1)
            if t_ == 1:
                need(eng, A["sums_mm"], b)
            else:
                need(eng, A[f"sum{half}"], (NT - 1) * b + t_ - 1)
            a = P[:, (2 * t_ + half) % RING_P, :]
            other = P[:, half, :] if t_ == 1 else SP[:, half, :]
            unit.tensor_tensor(SP[:, half, :], a, other, ALU.add).then_inc(A[f"sum{half}"], 1)

        h2 = O2[0:RT, 0:5, :].rearrange("p a n -> p (a n)")[:, 0:NTT * FF].rearrange("p (i f) -> p i f", i=NTT)
        q2 = QS[0:RT, 0:3, :].rearrange("p a n -> p (a n)")[:, 0:NTT * FF].rearrange("p (i f) -> p i f", i=NTT)

        def hqT(c):
            return QB[:, 0:2, :].rearrange("p a n -> p (a n)")[:, c * TOK:c * TOK + TOK]

        def hq_bank(c):
            return bank[(0, 1, 6, 7)[c]][:].bitcast(bf16)[:, 0:TOK]

        @block.sync
        def _(sp):
            def load(dst, src, s, key):
                sp.dma_start(dst, src).then_inc(s, 16)
                counts[key] += 16

            load(x[:], t["x"].rearrange("(n b) s d -> (b s) n d", b=2), x_in, "x_in")
            load(ident[:], t["c_ident"], x_in, "x_in")
            sp.dma_start(xT[:, 0], t["ctxT"][0]).then_inc(A0["ctx_in0"], 16)
            load(wkT[:], t["wkT"], k_in, "k_in")
            load(wvT[:], t["wvT"], k_in, "k_in")
            load(bk0[:], t["L0_xattn_bk"].rearrange("(p o) -> p o", o=1), k_in, "k_in")
            for r in range(3):
                load(wq0[:, :, r, :], t["wqT"].rearrange("d (g n) -> d g n", g=4), w_in, "w_in")
                load(bq0[32 * r:32 * r + 32, :], t["L0_xattn_bq"].rearrange("(g p) -> p g", p=32), w_in, "w_in")
            load(qmask[:], t["c_qmask"], w_in, "w_in")
            load(mmask0[:], t["c_mmask0"], w_in, "w_in")
            sp.dma_start(xT[:, 1], t["ctxT"][1]).then_inc(A0["ctx_in1"], 16)

            def stack(b, par):
                need(sp, A0["klo_ready"], NCH * (b + 1))
                for g in range(4):
                    rows = slice(32 * g, 32 * g + 32)
                    for r, src in enumerate((khi, khi, klo)):
                        sp.dma_start(KS[32 * r:32 * r + 32, par, g, :], src[rows, :])\
                            .then_inc(A0[f"stacked{g}"], 16)

            def fetch(b, par):
                sp.dma_start(xT[:, par], t["ctxT"][bass.ds(b, 1)].rearrange("o d n -> d (o n)")).then_inc(A0[f"ctx_in{par}"], 16)

            def refill(b, par):
                need(sp, A0["scores"], NH2 * (b - 1))
                if exists(b, 1):
                    fetch(b + 1, 1 - par)
                stack(b, par)

            stack(0, 0)
            sp.wait_ge(A0["vproj"], NCH)
            fetch(2, 0)
            stack(1, 1)
            for dst, src in ((gate_w, t["L0_ffn_gate_w"]), (gb_bc, t["L0_ffn_gate_b"].partition_broadcast(128)),
                             (b2, t["L0_ffn_b2"]), (bo_bc, t["L0_xattn_bo"].partition_broadcast(128))):
                load(dst[:], src, moe_in, "moe_in")
            load(mmask1[:], t["c_mmask1"], moe_in, "moe_in")
            load(iota8[:], t["c_iota8"], moe_in, "moe_in")
            load(iota1[:], t["c_iota1"], moe_in, "moe_in")
            load(bv0[:], t["L0_xattn_bv"].rearrange("(p o) -> p o", o=1), moe_in, "moe_in")
            load(gates[:, 0:2], t["g_xattn"].partition_broadcast(128), moe_in, "moe_in")
            load(gates[:, 2:4], t["g_ffn"].partition_broadcast(128), moe_in, "moe_in")
            load(woT[:], t["woT"], moe_in, "moe_in")
            load(w1[:], t["L0_ffn_w1"].rearrange("e d h -> d e h"), moe_in, "moe_in")
            load(b1[:], t["L0_ffn_b1"].rearrange("e (c p) -> p e c", p=128), moe_in, "moe_in")
            load(w2[:], t["L0_ffn_w2"].rearrange("e (c p) d -> p e c d", p=128), moe_in, "moe_in")
            for b in range(2):
                sp.dma_start(ctxN[:, b], ctx_h[b]).then_inc(A1[f"ctx_in{b}"], 16)
            with sp.Fori(1, B // 2 - 1) as pair:
                for j in range(2):
                    refill(2 * pair + j, j)
            refill(B - 2, 0)
            refill(B - 1, 1)
            for j in range(2):
                sp.dma_start(wk1[:, j, :], t["L1_xattn_Wkv"][:, 0:DK1]).then_inc(bc_in, 16)
                sp.dma_start(wq1[:, :, j, :], t["L1_xattn_Wq"].rearrange("d (h e) -> d h e", h=H)).then_inc(bc_in, 16)
            for a in range(2):
                sp.dma_start(wo1[64 * a:64 * a + 64], t["L1_xattn_Wo"].rearrange("(a k p) d -> a p k d", a=2, k=8)[a])\
                    .then_inc(bc_in, 16)
            for dst, src in ((wv1, t["L1_xattn_Wkv"]),
                             (wff1, t["L1_xattn_Wff1"].rearrange("d (c n) -> d c n", n=128)),
                             (wff2, t["L1_xattn_Wff2"].rearrange("(c p) d -> p c d", p=128)),
                             (bw1, t["bw1T"]), (bw2, t["bw2T"].rearrange("(c p) d -> p c d", p=128)),
                             (convw, t["L1_ffn_conv_w"].rearrange("(c p) o k -> p c (o k)", p=128)),
                             (convb, t["L1_ffn_conv_b"].rearrange("(c p) -> p c", p=128))):
                sp.dma_start(dst[:], src).then_inc(bc_in, 16)
            for j, k in enumerate(("ln_g", "ln_b", "cln_g", "cln_b")):
                sp.dma_start(lng[:, j:j + 1], t["L1_xattn_" + k].rearrange("(p o) -> p o", o=1)).then_inc(bc_in, 16)

            def fetch1(b, par):
                need(sp, A1["cn_ready"], NT * (b - 1))
                sp.dma_start(ctxN[:, par], ctx_h[bass.ds(b, 1)].rearrange("o p t d -> p (o t) d")).then_inc(A1[f"ctx_in{par}"], 16)

            with sp.Fori(1, B // 2) as pair:
                for j in range(2):
                    fetch1(2 * pair + j, j)
            sp.wait_ge(E["final_done"], NTT)
            sp.dma_start(out.rearrange("(n b) s d -> (b s) n d", b=2), x[:]).then_inc(out_done, 16)
            sp.wait_ge(out_done, 16)

        BC_IN = 16 * (2 * 2 + 2 + 7 + 4)

        @block.gpsimd
        def _(pool):
            filled = [0]

            def put(dst, value):
                nc.gpsimd.memset(dst, value).then_inc(fill, 1)
                filled[0] += 1
                pool.wait_ge(fill, filled[0])

            put(wq0[:, :, 3, :], 0.0)
            put(bq0[96:128, :], 0.0)
            put(powers[:, 0], -0.5)
            put(powers[:, 1], 1.5)
            put(ones[:], 1.0)

            def estimate_rstd(var, r, tmp, n, width, done):
                p = slice(0, n)
                def step(ins):
                    ins.then_inc(done[0], 1)
                    done[1] += 1
                    need(pool, done[0], done[1])
                step(nc.gpsimd.tensor_tensor(r, var, powers[p, 0, 0:width], ALU.pow))
                step(nc.gpsimd.tensor_tensor(tmp, var, r, ALU.mult))
                step(nc.gpsimd.tensor_tensor(tmp, tmp, r, ALU.mult))
                step(nc.gpsimd.tensor_tensor(tmp, tmp, powers[p, 0, 0:width], ALU.mult))
                step(nc.gpsimd.tensor_tensor(tmp, tmp, powers[p, 1, 0:width], ALU.add))
                return nc.gpsimd.tensor_tensor(r, r, tmp, ALU.mult)

            token_steps = [E["rstd_step"], 0]

            def token_rstd(k):
                row = [sm1[0:RT, i, :] for i in range(5)]
                pool.wait_ge(E["var_ready"], k + 1)
                estimate_rstd(row[2], row[4], row[3], RT, NTT, token_steps).then_inc(E["rstd_ready"], 1)
                pool.wait_ge(E["rstd_ready"], k + 1)

            def context_rstd(b, par):
                r = [st1[0:KT, 6 * par + k, :] for k in range(6)]
                need(pool, A1["stats_v"], 8 * (b + 1))
                estimate_rstd(r[2], r[5], r[3], KT, NT, [A1["rstd"], 6 * b]).then_inc(A1["rstd"], 1)
                need(pool, A1["rstd"], 6 * (b + 1))
                nc.gpsimd.tensor_tensor(r[4], r[0], r[5], ALU.mult).then_inc(A1["shift"], 1)
                need(pool, A1["shift"], b + 1)

            def sum_tiles(A, s, first=1, end=NT):
                for t_ in range(first, end):
                    add_tile(nc.gpsimd, pool, A, s, 0, t_)
                need(pool, A["sum0"], (NT - 1) * s + end - 1)

            token_rstd(0)
            for par in range(2):
                put(KS[96:128, par], 0.0)
                put(KS[96:100, par], 1.0)
            sum_tiles(A0, 0)
            with pool.Fori(1, B - 1) as s:
                sum_tiles(A0, s)
            sum_tiles(A0, B - 1, 1, RSTD_TILE)
            context_rstd(0, 0)
            sum_tiles(A0, B - 1, RSTD_TILE, NT)
            context_rstd(1, 1)
            token_rstd(1)
            put(KS[64:128, :, 1, :], 0.0)
            put(KS[64:65, :, 1, :], 1.0)
            token_rstd(2)
            pool.wait_ge(E["expert_out"], NE)
            put(QB[64:128], 0.0)

            def step1(s, par):
                sum_tiles(A1, s, 1, RSTD_TILE)
                if exists(s, 2):
                    context_rstd(s + 2, par)
                sum_tiles(A1, s, RSTD_TILE, NT)

            steps(pool, step1)
            token_rstd(3)

        @block.vector
        def _(v):
            count = {}

            def signal(ins, key="vector_chain"):
                count[key] = count.get(key, 0) + 1
                ins.then_inc(E[key], 1)

            def link(ins, key="vector_chain"):
                signal(ins, key)
                v.wait_ge(E[key], count[key])

            def layernorm(src, dst, k, meanwhile=None, twice=False):
                for i in range(NTT):
                    last = nc.vector.bn_stats(st6[0:RT, i, :], src[:, i, :])
                link(last)
                for i in range(NTT):
                    last = nc.vector.bn_aggr(sm1[0:RT, 0:2, i], st6[0:RT, i, :])
                link(last)
                factor, guard = (1.0 + EPS, EPS * EPS) if twice else (1.0, EPS)
                link(nc.vector.tensor_scalar(sm1[0:RT, 2, :], sm1[0:RT, 1, :], factor, guard, ALU.mult, ALU.add), "var_ready")
                if meanwhile:
                    meanwhile()
                v.wait_ge(E["rstd_ready"], k + 1)
                for i in range(NTT):
                    last = nc.vector.tensor_scalar(dst[:, i, :], src[:, i, :], sm1[0:RT, 0, i:i + 1], sm1[0:RT, 4, i:i + 1],
                                                   ALU.subtract, ALU.mult)
                link(last, "z_ready")

            v.wait_ge(x_in, counts["x_in"])
            layernorm(x, z, 0)
            signal(nc.vector.tensor_copy(identb[:], ident[:]), "identb_ready")
            def item(A, L, mask, kind, c, bk, b, par):
                cols = slice(c * CH, c * CH + CH)
                if kind == "K":
                    need(v, A["khi_ready"], NCH * b + c + 1)
                    if L.n == 0:
                        nc.vector.scalar_tensor_tensor(klo[:, cols], bank[bk][:, 0:CH], bk0[:, 0:1], khi[:, cols],
                                                       ALU.add, ALU.subtract).then_inc(A["klo_ready"], 1)
                    else:
                        nc.vector.tensor_copy(KS[0:64, par, 1, cols], KS[0:64, par, 0, cols]).then_inc(A["khi_copied"], 1)
                        nc.vector.tensor_tensor(KS[64:128, par, 0, cols], bank[bk][64:128, 0:CH],
                                                KS[64:128, par, 0, cols], ALU.subtract).then_inc(A["klo_ready"], 1)
                elif kind == "M":
                    need(v, A["max_scores"], L.nmax * b + c + 1)
                    rt, j = L.max_chunk(c, b)
                    banks = L.max_banks(b)
                    nc.vector.tensor_reduce(mxc[0:L.rows, rt * NCH + j:rt * NCH + j + 1], bank[banks[c % len(banks)]][0:L.rows, 0:CH],
                                            AX.X, ALU.max)\
                        .then_inc(A["max_taken"], 1)
                    if c == L.nmax - 1:
                        need(v, A["max_taken"], L.nmax * (b + 1))
                        nc.vector.tensor_reduce(mx[0:L.rows, 0:L.tiles],
                                                mxc[0:L.rows, 0:L.nmax].rearrange("p (r c) -> p r c", c=NCH), AX.X, ALU.max)\
                            .then_inc(A["max_final"], 1)
                        need(v, A["max_final"], b + 1)
                        m, blk = mx[0:L.rows, 0:L.tiles], MB[0:L.rows, 0:L.tiles]
                        if L.n == 0:
                            m, blk = m.rearrange("p (a c) -> p a c", c=2), blk.rearrange("p (a c) n -> p a c n", c=2)
                        nc.vector.tensor_tensor(blk, m[..., None].broadcast_to(list(m.shape) + [32]), mask, ALU.mult)\
                            .then_inc(A["max_block"], 1)
                elif kind == "R":
                    dst = QS if L.n == 0 else QB
                    for half, (lo, hi) in enumerate(((0, L.split), (L.split, HS))):
                        need(v, A["max_row"], 2 * b + half + 1)
                        nc.vector.tensor_copy(dst[L.spare:L.spare + 32, bass.ds(b, 1), lo:hi].rearrange("p o n -> p (o n)"),
                                              (bank[7], bank[0])[half][L.spare:L.spare + 32, 0:hi - lo])\
                            .then_inc(A["max_in_q"], 1)

            def normalise(A, L, b, par, parts=1):
                n_ = HS * L.group // 128 // parts
                need(v, A["sums_mm"], b + 1)
                for part in range(parts):
                    cols = slice(part * n_, part * n_ + n_)
                    nc.vector.reciprocal(rsum[:, cols], L.sums(bank, acc_bank, par)[:, cols]).then_inc(A["sum_rec"], 1)
                    need(v, A["sum_rec"], b + 1 + part)
                    if part == 0:
                        need(v, A["pv"], NT * (b + 1))
                    nc.vector.tensor_tensor(O2[:, part * n_ // S:(part + 1) * n_ // S, bass.ds(b * S, S)],
                                            acc_bank[par][:, cols].rearrange("p (a q) -> p a q", q=S),
                                            rsum[:, cols].rearrange("p (a q) -> p a q", q=S), ALU.mult)\
                        .then_inc(A["normed"], 1)

            def stats1(b, par, k):
                A = A1
                if k < NT:
                    if k == 0:
                        need(v, A[f"ctx_in{par}"], ctx_count(b, par))
                        need(v, A["cn_ready"], NT * (b - 1))
                    ins = nc.vector.bn_stats(st6[0:KT, k, :], ctxN[:, par, k, :])
                    if k == NT - 1:
                        ins.then_inc(A["stats_v"], 1)
                    return
                need(v, A["stats_v"], 8 * b + 1)
                f = [st6[0:KT, :, k] for k in range(6)]
                r = [st1[0:KT, 6 * par + k, :] for k in range(6)]
                steps = [0]

                def step(ins):
                    steps[0] += 1
                    ins.then_inc(A["stats_v"], 1)
                    need(v, A["stats_v"], 8 * b + 1 + steps[0])

                step(nc.vector.tensor_tensor(r[1], f[1], f[4], ALU.subtract))
                step(nc.vector.tensor_tensor(r[0], f[1], f[4], ALU.add))
                step(nc.vector.tensor_scalar(r[0], r[0], -0.5, None, ALU.mult))
                step(nc.vector.tensor_tensor(r[1], r[1], r[1], ALU.mult))
                step(nc.vector.tensor_tensor(r[2], f[2], f[5], ALU.add))
                step(nc.vector.tensor_scalar(r[2], r[2], 1.0 / D, EPS, ALU.mult, ALU.add))
                step(nc.vector.scalar_tensor_tensor(r[2], r[1], 0.25, r[2], ALU.mult, ALU.add))
                assert steps[0] == 7

            def add_bv(first, end):
                signal(nc.vector.tensor_scalar(O2[:, 0:4, first:end], O2[:, 0:4, first:end], bv0[:, 0:1], None, ALU.add),
                       "acc_divided")

            def output_weights():
                v.wait_ge(moe_in, counts["moe_in"])
                for j in range(4):
                    last = nc.vector.tensor_scalar(wo0[:, j, :], woT[:], qmask[:, j:j + 1], None, ALU.mult)
                signal(last, "wo0_ready")
                v.wait_ge(A0["normed"], B - 1)
                add_bv(0, (B - 2) * S)

            def step(A, L, mask, s, par):
                for p in range(NH2):
                    if p == SUMS_AT[L.n] and not (isinstance(s, int) and s == 0):
                        normalise(A, L, s - 1, 1 - par)
                        if L.n == 0 and isinstance(s, int) and s == B - 1:
                            output_weights()
                    for kind, c, ahead, bk, _ in L.items(s)[p]:
                        item(A, L, mask, kind, c, bk, s + ahead, (par + ahead) % 2)
                    if L.n == 1 and exists(s, 2) and p <= NT:
                        stats1(s + 2, par, p)
                    if L.n == 0 and isinstance(s, int) and s == B - 1:
                        parts = [(b, k) for b in range(2) for k in range(NT + 1)]
                        for b, k in parts[p * len(parts) // NH2:(p + 1) * len(parts) // NH2]:
                            stats1(b, b, k)
                    t_, odd = divmod(p - ADD_LAG, 2)
                    if L.n == 1 and odd == 0 and t_ >= 1:
                        add_tile(nc.vector, v, A, s, 1, t_)
                for t_ in range((NH2 - 1 - ADD_LAG) // 2 + 1, NT if L.n == 1 else 0):
                    add_tile(nc.vector, v, A, s, 1, t_)

            mask0 = mmask0[:][:, None, :, :].broadcast_to([L0.rows, L0.tiles // 2, 2, 32])
            mask1 = mmask1[:][:, None, :].broadcast_to([L1.rows, L1.tiles, 32])
            def prepare(A, L, mask, places):
                for items in places:
                    for kind, c, b, bk, _ in items:
                        item(A, L, mask, kind, c, bk, b, b)

            prepare(A0, L0, mask0, L0.before[:QUERIES_AT])
            v.wait_ge(w_in, counts["w_in"])
            for g in range(4):
                v.wait_ge(E["q0_hi"], g + 1)
                link(nc.vector.scalar_tensor_tensor(q0(g)[32:64, :], q0_bank[g][32:64, 0:TOK], bq0[32:64, g:g + 1],
                                                    q0(g)[32:64, :], ALU.add, ALU.subtract), "q0_lo")
                for j in (2, 3):
                    last = nc.vector.tensor_scalar(stacked_queries(g, j), q0(g).rearrange("p (b q) -> p b q", b=B),
                                                   qmask[:, j:j + 1], None, ALU.mult)
                signal(last, "q0_stacked")
            prepare(A0, L0, mask0, L0.before[QUERIES_AT:])
            steps(v, lambda s, par: step(A0, L0, mask0, s, par))
            normalise(A0, L0, B - 1, 1)
            v.wait_ge(A0["normed"], B)
            add_bv((B - 2) * S, B * S)

            v.wait_ge(E["tanh_ready"], 1)
            v.wait_ge(E["wo0_done"], 1)
            ob = moe[:]
            link(nc.vector.tensor_tensor(ob, bank[0][0:RT, :].rearrange("p (i d) -> p i d", i=NTT),
                                         bo_bc[0:RT, None, :].broadcast_to([RT, NTT, 128]), ALU.add))
            link(nc.vector.scalar_tensor_tensor(x[:], ob, tgates[0:RT, 0:1], x[:], ALU.mult, ALU.add))

            layernorm(x, z, 1, lambda: prepare(A1, L1, mask1, L1.before[0:2]))
            prepare(A1, L1, mask1, L1.before[2:QUERIES_AT])
            v.wait_ge(E["logits_done"], 1)
            L, E_, s1, s2, o1, o2, w_, m_, t_ = (sm[:, k] for k in range(9))

            def col(k):
                return sm1[0:RT, 8 + k, :]

            def bc(a):
                return a[:, :, None].broadcast_to([RT, NTT, NE])

            link(nc.vector.tensor_tensor(L, bank[3][0:RT, 0:NTT * NE].rearrange("p (i e) -> p i e", e=NE),
                                         gb_bc[0:RT, None, :].broadcast_to([RT, NTT, NE]), ALU.add))
            link(nc.vector.tensor_reduce(col(0), L, AX.X, ALU.max))
            link(nc.vector.tensor_tensor(L, L, bc(col(0)), ALU.subtract), "logit_ready")
            v.wait_ge(E["gate_exp"], 1)
            link(nc.vector.tensor_reduce(col(1), E_, AX.X, ALU.add))
            link(nc.vector.reciprocal(col(2), col(1)))
            link(nc.vector.tensor_tensor(s1, E_, bc(col(2)), ALU.mult))

            def first_best(s, o):
                link(nc.vector.tensor_reduce(col(3), s, AX.X, ALU.max))
                link(nc.vector.tensor_tensor(t_, s, bc(col(3)), ALU.is_equal))
                link(nc.vector.tensor_tensor(t_, t_, iota8[:], ALU.mult))
                link(nc.vector.tensor_reduce(col(4), t_, AX.X, ALU.max))
                link(nc.vector.tensor_tensor(o, iota8[:], bc(col(4)), ALU.is_equal))

            first_best(s1, o1)
            link(nc.vector.scalar_tensor_tensor(s2, o1, -2.0, s1, ALU.mult, ALU.add))
            first_best(s2, o2)
            link(nc.vector.tensor_tensor(m_, o1, o2, ALU.add))
            link(nc.vector.tensor_tensor(w_, m_, s1, ALU.mult))
            link(nc.vector.scalar_tensor_tensor(t_, w_, 0.0, iota1[:], ALU.is_gt, ALU.mult))
            link(nc.vector.tensor_reduce(col(5), t_, AX.X, ALU.max))
            link(nc.vector.tensor_tensor(m_, iota1[:], bc(col(5)), ALU.is_equal), "winner_ready")

            def add_expert(e):
                v.wait_ge(E["expert_out"], e + 1)
                for i in range(NTT):
                    y = bank[6][0:RT, i * 128:i * 128 + 128]
                    if e == 0:
                        last = nc.vector.tensor_scalar(moe[:, i, :], y, m_[:, i, e:e + 1], None, ALU.mult)
                    else:
                        last = nc.vector.scalar_tensor_tensor(moe[:, i, :], y, m_[:, i, e:e + 1], moe[:, i, :],
                                                              ALU.mult, ALU.add)
                link(last, "expert_added")

            def weigh(e):
                if e >= 2:
                    v.wait_ge(E["xw_tr"], e - 1)
                signal(nc.vector.tensor_tensor(xw[:, e % 2], z[:], w_[:, :, e:e + 1].broadcast_to([RT, NTT, 128]), ALU.mult),
                       "xw_ready")

            def weight_means():
                v.wait_ge(bc_in, BC_IN)
                for k, w in enumerate((bw1[:], bw2[:].rearrange("p c d -> p (c d)"))):
                    signal(nc.vector.tensor_reduce(wqs[:, k:k + 1], w, AX.X, ALU.add, apply_absolute_value=True), "wabs_ready")

            def ternary():
                v.wait_ge(E["wmean_done"], 1)
                link(nc.vector.tensor_scalar(wqs[:, 2:4], bank[7][:, 0:2], 1.0 / (D * FF), EPS, ALU.mult, ALU.max), "wmean_read")
                link(nc.vector.reciprocal(wqs[:, 4:6], wqs[:, 2:4]))
                for k, w in enumerate((bw1[:], bw2[:].rearrange("p c d -> p (c d)"))):
                    link(nc.vector.tensor_scalar(w, w, wqs[:, 4 + k:5 + k], ROUND, ALU.mult, ALU.add))
                    link(nc.vector.tensor_scalar(w, w, ROUND, 1.0, ALU.subtract, ALU.min))
                    if k == 0:
                        link(nc.vector.tensor_scalar(w, w, -1.0, wqs[:, 2:3], ALU.max, ALU.mult))
                    else:
                        link(nc.vector.tensor_scalar(bw2t[:].rearrange("p c d -> p (c d)"), w, -1.0, None, ALU.max))

            weigh(0)
            weigh(1)
            for e in range(NE):
                if e + 2 < NE:
                    weigh(e + 2)
                if e == 1:
                    weight_means()
                elif e == 2:
                    ternary()
                if e < NE - 1:
                    add_expert(e)
                if e == NE - 3:
                    v.wait_ge(E["b2_done"], 1)
                    link(nc.vector.tensor_tensor(moe[:], bank[7][0:RT, :].rearrange("p (i d) -> p i d", i=NTT), moe[:], ALU.add))
            link(nc.vector.tensor_scalar(col(6), m_[:, :, NE - 1], tgates[0:RT, 2:3], None, ALU.mult))
            link(nc.vector.scalar_tensor_tensor(x[:], moe[:], tgates[0:RT, 2:3], x[:], ALU.mult, ALU.add))
            v.wait_ge(E["expert_out"], NE)
            for i in range(NTT):
                last = nc.vector.scalar_tensor_tensor(x[:, i, :], bank[6][0:RT, i * 128:i * 128 + 128], col(6)[:, i:i + 1],
                                                      x[:, i, :], ALU.mult, ALU.add)
            link(last, "expert_added")

            layernorm(x, z, 2, twice=True)
            def query(h):
                v.wait_ge(E["q1_hi"], h + 1)
                q = slice(h * S, h * S + S)
                signal(nc.vector.tensor_tensor(QB[0:64, :, q], q1_bank[h % 3][0:64, 0:TOK].rearrange("p (b q) -> p b q", b=B),
                                               QS[0:64, :, q], ALU.subtract), "q1_lo")

            def gate(c):
                v.wait_ge(E["ff_tanh"], c + 1)
                e1, hb, gb = O2[:, c, :], bank[2 + 2 * (c % 2)][:, 0:TOK], bank[3 + 2 * (c % 2)][:, 0:TOK]
                link(nc.vector.scalar_tensor_tensor(e1, e1, 1.0, gb, ALU.add, ALU.mult))
                link(nc.vector.scalar_tensor_tensor(sT(c), e1, 0.5, hb, ALU.mult, ALU.mult), "ff_silu")

            for kind, c in first_queries():
                if kind == "Q":
                    query(c)
                elif kind == "M":
                    item(A1, L1, mask1, "M", c, None, 0, 0)
                else:
                    gate(c)
            v.wait_ge(fill, 12)
            item(A1, L1, mask1, "R", 0, 7, 0, 0)
            steps(v, lambda s, par: step(A1, L1, mask1, s, par))
            normalise(A1, L1, B - 1, 1, OUT_PARTS)

            v.wait_ge(E["out1_done"], 1)
            link(nc.vector.scalar_tensor_tensor(x[:], bank[0][0:RT, :].rearrange("p (i d) -> p i d", i=NTT), tgates[0:RT, 1:2],
                                                x[:], ALU.mult, ALU.add))
            layernorm(x, z, 3)

            def row_scale(inv):
                link(nc.vector.tensor_scalar(inv, inv, EPS, 1.0 / 127.0, ALU.max, ALU.mult))
                link(nc.vector.reciprocal(sm1[0:RT, 20, :], inv))
                return sm1[0:RT, 20, :]

            inv = sm1[0:RT, 21, :]
            link(nc.vector.tensor_reduce(inv, z[:], AX.X, ALU.max, apply_absolute_value=True))
            sc = row_scale(inv)
            for i in range(NTT):
                last = nc.vector.tensor_scalar(z[:, i], z[:, i], sc[:, i:i + 1], ROUND, ALU.mult, ALU.add)
            link(last)
            link(nc.vector.tensor_scalar(z[:], z[:], ROUND, 127.0, ALU.subtract, ALU.min))
            for i in range(NTT):
                last = nc.vector.tensor_scalar(moe[:, i], z[:, i], -128.0, inv[:, i:i + 1], ALU.max, ALU.mult)
            link(last, "xq_ready")
            for c in range(FC + 1):
                if c < FC:
                    v.wait_ge(E["conv_centre"], c + 1)
                    hb, d = (a.rearrange("p (b q) -> p b q", b=B) for a in (bank[2 + c][:, 0:TOK], uT[:, 0, c, :]))
                    signal(nc.vector.scalar_tensor_tensor(d[:, :, 1:S], hb[:, :, 0:S - 1], convw[:, c, 0:1], d[:, :, 1:S],
                                                          ALU.mult, ALU.add), "conv_left")
                if c > 0:
                    hb, d = (a.rearrange("p (b q) -> p b q", b=B) for a in (bank[1 + c][:, 0:TOK], uT[:, 0, c - 1, :]))
                    v.wait_ge(E["conv_left"], c)
                    signal(nc.vector.scalar_tensor_tensor(d[:, :, 0:S - 1], hb[:, :, 1:S], convw[:, c - 1, 2:3],
                                                          d[:, :, 0:S - 1], ALU.mult, ALU.add), "conv_done")
            for c in range(FC):
                v.wait_ge(E["conv_tanh"], c + 1)
                signal(nc.vector.scalar_tensor_tensor(sT(c), uT[:, 1, c, :], 1.0, uT[:, 0, c, :], ALU.add, ALU.mult),
                       "silu_done")
            link(nc.vector.memset(wqs[:, 7:8], -ROUND))
            inv = sm1[0:RT, 22, :]
            for i in range(NTT):
                v.wait_ge(E["back_tr"], i + 1)
                last = nc.vector.tensor_reduce(inv[:, i:i + 1], bank[2 + i][0:RT, :], AX.X, ALU.max, apply_absolute_value=True)
            link(last)
            link(nc.vector.tensor_scalar(inv, inv, 0.5, None, ALU.mult))
            sc = row_scale(inv)
            link(nc.vector.tensor_scalar(sc, sc, 0.5, None, ALU.mult))
            for i in range(NTT + 1):
                if i < NTT:
                    signal(nc.vector.tensor_scalar(h2[:, i], bank[2 + i][0:RT, :], sc[:, i:i + 1], ROUND, ALU.mult, ALU.add),
                           "hq_rounded")
                if i > 0:
                    v.wait_ge(E["hq_rounded"], i)
                    signal(nc.vector.tensor_scalar(h2[:, i - 1], h2[:, i - 1], ROUND + 127.0, ROUND - 128.0, ALU.min, ALU.max),
                           "hq_clipped")
            link(nc.vector.tensor_scalar(wqs[:, 6:7], wqs[:, 3:4], tgates[:, 3:4], None, ALU.mult))
            link(nc.vector.tensor_scalar(sm1[0:RT, 23, :], sm1[0:RT, 22, :], wqs[0:RT, 6:7], None, ALU.mult))
            for c in range(1, FC, 2):
                v.wait_ge(E["hq_tr"], c + 1)
                signal(nc.vector.tensor_copy(hqT(c), hq_bank(c)), "hqT_odd")
            v.wait_ge(E["lin2_done"], 1)
            for i in range(NTT):
                signal(nc.vector.scalar_tensor_tensor(x[:, i, :], bank[2][0:RT, i * 128:i * 128 + 128], sm1[0:RT, 23, i:i + 1],
                                                      x[:, i, :], ALU.mult, ALU.add), "final_done")

        @block.scalar
        def _(a):
            def done(ins, key):
                ins.then_inc(E[key], 1)

            def item(A, L, kind, c, bk, b, par):
                cols = slice(c * CH, c * CH + CH)
                if kind == "T":
                    need(a, A["tr_done"], NCH * b + c + 1)
                    nc.scalar.activation(xT[:, 0, cols], bank[bk][:, 0:CH], ACT.Identity, bias=lng[:, 3:4],
                                         scale=lng[:, 2:3]).then_inc(A["tr_evac"], 1)
                elif kind == "K":
                    need(a, A["kproj"], NCH * b + c + 1)
                    if L.n == 0:
                        if c == 0:
                            for g in range(4):
                                need(a, A[f"stacked{g}"], STACKED * b)
                        ins = nc.scalar.activation(khi[:, cols], bank[bk][:, 0:CH], ACT.Identity, bias=bk0[:, 0:1])
                    else:
                        ins = nc.scalar.copy(KS[:, par, 0, cols], bank[bk][:, 0:CH])
                    ins.then_inc(A["khi_ready"], 1)
                elif kind == "V":
                    need(a, A["vproj"], NCH * b + c + 1)
                    first = 0 if L.n == 0 else DK1
                    nc.scalar.copy(VS[:, par, c * TPC:c * TPC + TPC, 0:128 - first],
                                   bank[bk][0:KT, :].rearrange("p (t n) -> p t n", t=TPC)[:, :, first:128])\
                        .then_inc(A["v_ready"], 1)

            def normalise(b, par, first, end):
                if first == 0:
                    need(a, A1["shift"], b + 1)
                    need(a, A1["tr_done"], NCH * (b - 1))
                for t_ in range(first, end):
                    nc.scalar.activation(cn[par][:, t_, :], ctxN[:, par, t_, :], ACT.Identity,
                                         bias=st1[0:KT, 6 * par + 4, t_:t_ + 1], scale=st1[0:KT, 6 * par + 5, t_:t_ + 1])\
                        .then_inc(A1["cn_ready"], 1)

            def step(A, L, scale, s, par):
                for k in range(NH2):
                    need(a, A["scores"], NH2 * s + k + 1)
                    old = k // 2 - RING_P // 2
                    need(a, A["pv"], NT * s + old + 1)
                    if L.n == 1 or k % 2 == 0:
                        need(a, A[f"sum{k % 2}"], (NT - 1) * s + (max(old, 1) if old >= 0 else old + 1))
                    nc.scalar.activation(P[:, k % RING_P, :], score_bank[k % RING_S][0:KT, 0:HALF], ACT.Exp, scale=scale)\
                        .then_inc(A["exps"], 1)
                    if k >= 1:
                        for kind, c, ahead, bk, _ in L.items(s)[k - 1]:
                            item(A, L, kind, c, bk, s + ahead, (par + ahead) % 2)
                    if L.n == 0 and isinstance(s, int) and s == B - 1 and k >= NH2 - NT // 2:
                        first = 2 * (k - NH2 + NT // 2)
                        normalise(0, 0, first, first + 2)
                    if L.n == 1 and exists(s, 2) and NORM_AT <= k < NORM_AT + NT // 2:
                        first = 2 * (k - NORM_AT)
                        normalise(s + 2, par, first, first + 2)

            def prepare(A, L, places):
                for items in places:
                    for kind, c, b, bk, _ in items:
                        item(A, L, kind, c, bk, b, b)

            a.wait_ge(k_in, counts["k_in"])
            prepare(A0, L0, L0.before[:QUERIES_AT])
            a.wait_ge(E["tok_tr"], 1)
            done(nc.scalar.copy(zT[:], bank[2][:, 0:TOK]), "zT_ready")
            a.wait_ge(w_in, counts["w_in"])
            a.wait_ge(fill, 2)
            def mask(g):
                a.wait_ge(E["q0_lo"], g + 1)
                for j in range(2):
                    last = nc.scalar.activation(stacked_queries(g, j), q0(g).rearrange("p (b q) -> p b q", b=B), ACT.Identity,
                                                scale=qmask[:, j:j + 1])
                done(last, "q0_masked")

            for g in range(4):
                a.wait_ge(E["q0_proj"], g + 1)
                if g >= 2:
                    a.wait_ge(E["q0_stacked"], g - 1)
                    a.wait_ge(E["q0_masked"], g - 1)
                done(nc.scalar.activation(q0(g), q0_bank[g][:, 0:TOK], ACT.Identity, bias=bq0[:, g:g + 1]), "q0_hi")
                if g >= 1:
                    mask(g - 1)
            mask(3)
            prepare(A0, L0, L0.before[QUERIES_AT:])
            steps(a, lambda s, par: step(A0, L0, DK0 ** -0.5, s, par))

            a.wait_ge(moe_in, counts["moe_in"])
            done(nc.scalar.activation(tgates[:], gates[:], ACT.Tanh), "tanh_ready")
            a.wait_ge(bc_in, BC_IN)
            prepare(A1, L1, L1.before[0:3])
            a.wait_ge(E["tok_tr"], 2)
            done(nc.scalar.copy(zT[:], bank[2][:, 0:TOK]), "zT_ready")
            a.wait_ge(E["logit_ready"], 1)
            done(nc.scalar.activation(sm[:, 1], sm[:, 0], ACT.Exp), "gate_exp")
            prepare(A1, L1, L1.before[3:QUERIES_AT])

            def weighed(e):
                a.wait_ge(E["xw_tr"], e + 1)
                if e >= 2:
                    a.wait_ge(E["up_done"], FC * (e - 2) + FC)
                done(nc.scalar.copy(xwT[:, e % 2, :], bank[e % 2][:, 0:TOK]), "xwT_ready")

            weighed(0)
            for e in range(NE):
                for c in range(FC):
                    if c == 0 and e >= 2:
                        a.wait_ge(E["expert_out"], e - 1)
                    a.wait_ge(E["up_done"], FC * e + c + 1)
                    done(nc.scalar.activation(hT[:, e % 2, c, :], bank[2 + c][:, 0:TOK], ACT.Relu,
                                              bias=b1[:, e, c:c + 1]), "hidden_ready")
                if e + 1 < NE:
                    weighed(e + 1)
                if e == 3:
                    a.wait_ge(E["disp_tr"], 1)
                    done(nc.scalar.copy(dispT, bank[7][0:NE, 0:TOK]), "dispT_ready")
            normalise(1, 1, 0, NT)
            a.wait_ge(E["tok_tr"], 3)
            done(nc.scalar.activation(zT[:], bank[2][:, 0:TOK], ACT.Identity, bias=lng[:, 1:2], scale=lng[:, 0:1]), "zT_ready")
            def query(h):
                a.wait_ge(E["q1_proj"], h + 1)
                done(nc.scalar.copy(QS[:, :, h * S:h * S + S], q1_bank[h % 3][:, 0:TOK].rearrange("p (b q) -> p b q", b=B)),
                     "q1_hi")

            def gate(c):
                a.wait_ge(E["ff_proj"], c + 1)
                done(nc.scalar.activation(O2[:, c, :], bank[3 + 2 * (c % 2)][:, 0:TOK], ACT.Tanh, scale=0.5), "ff_tanh")

            for kind, c in first_queries():
                if kind == "Q":
                    query(c)
                elif kind == "F":
                    gate(c)
            steps(a, lambda s, par: step(A1, L1, DK1 ** -0.5, s, par))

            a.wait_ge(E["tok_tr"], 4)
            done(nc.scalar.copy(zT[:], bank[0][:, 0:TOK]), "zT_ready")
            for c in range(FC):
                a.wait_ge(E["lin1_done"], c + 1)
                done(nc.scalar.activation(uT[:, 0, c, :], bank[2 + c][:, 0:TOK], ACT.Identity, bias=convb[:, c:c + 1],
                                          scale=convw[:, c, 1:2]), "conv_centre")
            for c in range(FC):
                a.wait_ge(E["conv_done"], c + 1)
                done(nc.scalar.activation(uT[:, 1, c, :], uT[:, 0, c, :], ACT.Tanh, scale=0.5), "conv_tanh")
            for i in range(NTT):
                a.wait_ge(E["hq_clipped"], i + 1)
                done(nc.scalar.activation(q2[:, i], h2[:, i], ACT.Identity, bias=wqs[0:RT, 7:8]), "hq_ready")
            for c in range(0, FC, 2):
                a.wait_ge(E["hq_tr"], c + 1)
                done(nc.scalar.copy(hqT(c), hq_bank(c)), "hqT_even")

        @block.tensor
        def _(pe):
            def done(ins, key):
                ins.then_inc(E[key], 1)

            def tokens_transposed(src, dst):
                for i in range(NTT):
                    last = nc.tensor.transpose(dst[:, i * RT:i * RT + RT], src[:, i, :], ident[0:RT, 0:RT])
                return last

            def item(A, L, kind, c, bk, after, b, par):
                if after is not None:
                    need(pe, *released(A, after, after[2]))
                elif kind != "M" and L.n == 1:
                    need(pe, A["sum_rec"], b - 1)
                elif kind == "V":
                    need(pe, A["klo_ready"], NCH * (b + 1))
                if kind == "T":
                    if c == 0:
                        need(pe, A["cn_ready"], NT * (b + 1))
                    for k in range(TPC):
                        last = nc.tensor.transpose(bank[bk][:, k * KT:k * KT + KT], cn[par][:, c * TPC + k, :],
                                                   ident[0:KT, 0:KT])
                    last.then_inc(A["tr_done"], 1)
                elif kind == "K":
                    if L.n == 1:
                        need(pe, A["tr_evac"], NCH * b + c + 1)
                    elif c == 0:
                        need(pe, A[f"ctx_in{par}"], ctx_count(b, par))
                    nc.tensor.matmul(bank[bk][:, 0:CH], wkT[:] if L.n == 0 else wk1[:].rearrange("p a n -> p (a n)"),
                                     xT[:, L.context(par), c * CH:c * CH + CH], start=True, stop=True).then_inc(A["kproj"], 1)
                elif kind == "V":
                    need(pe, A["klo_ready"], NCH * b + c + 1)
                    for k in range(TPC):
                        kk = (c * TPC + k) * KT
                        last = nc.tensor.matmul(bank[bk][0:KT, k * 128:k * 128 + 128], xT[:, L.context(par), kk:kk + KT],
                                                wvT[:] if L.n == 0 else wv1[:], start=True, stop=True)
                    last.then_inc(A["vproj"], 1)
                elif kind == "M":
                    rt, j = L.max_chunk(c, b)
                    if c < 2:
                        need(pe, A["max_in_q"], 2 * b)
                    banks = L.max_banks(b)
                    need(pe, A["max_taken"], L.nmax * b + c + 1 - len(banks))
                    if L.n == 1 and rt == 0:
                        need(pe, A["klo_ready"], NCH * b + j + 1)
                    if L.n == 0 and j == 0 and rt % 2 == 0:
                        need(pe, A[f"stacked{rt // 2}"], STACKED * (b + 1))
                    nc.tensor.matmul(bank[banks[c % len(banks)]][0:L.rows, 0:CH],
                                     QS[:, bass.ds(b, 1), rt * L.rows:rt * L.rows + L.rows].rearrange("p o n -> p (o n)"),
                                     KS[:, par, rt // 2 if L.n == 0 else 0, j * CH:j * CH + CH],
                                     start=True, stop=True).then_inc(A["max_scores"], 1)
                elif kind == "R":
                    need(pe, A["max_block"], b + 1)
                    for rt in range(L.tiles):
                        half, col = divmod(rt * L.rows, L.split)
                        last = nc.tensor.matmul((bank[7], bank[0])[half][L.spare:L.spare + 32, col:col + L.rows],
                                                MB[0:L.rows, rt, :], identb[0:L.rows, 0:L.rows], start=True, stop=True,
                                                tile_position=(0, L.spare))
                        if col + L.rows == L.split or rt == L.tiles - 1:
                            last.then_inc(A["max_row"], 1)

            def scores(A, L, b, par, k):
                t_, half = divmod(k, 2)
                need(pe, A["exps"], NH2 * b + k + 1 - RING_S)
                if k == 0:
                    need(pe, A["max_in_q"], 2 * (b + 1))
                keys = slice(t_ * KT, t_ * KT + KT)
                dst = score_bank[k % RING_S]
                if L.n == 0:
                    for j in range(2):
                        g = 2 * half + j
                        last = nc.tensor.matmul(dst[0:KT, j * 224:j * 224 + 224], KS[:, par, g, keys],
                                                QS[:, bass.ds(b, 1), g * 224:g * 224 + 224].rearrange("p o n -> p (o n)"),
                                                start=True, stop=True)
                else:
                    cols = slice(half * HALF, half * HALF + HALF)
                    nc.tensor.matmul(dst[0:KT, 0:HALF], KS[:, par, 0, keys],
                                     QS[:, bass.ds(b, 1), cols].rearrange("p o n -> p (o n)"), start=True, stop=False)
                    last = nc.tensor.matmul(dst[0:KT, 0:HALF], KS[:, par, 1, keys],
                                            QB[:, bass.ds(b, 1), cols].rearrange("p o n -> p (o n)"), start=False, stop=True)
                last.then_inc(A["scores"], 1)

            def values(A, L, b, par, t_):
                need(pe, A["exps"], NH2 * b + 2 * t_ + 2)
                if t_ == 0:
                    need(pe, A["v_ready"], NCH * (b + 1))
                    need(pe, A["normed"], b - 1)
                n_ = HS * L.group // 128
                for g in range(128 // L.group):
                    half, col = divmod(g * n_, HALF)
                    rows = slice(L.group * g, L.group * g + L.group)
                    first = g * 32 if L.n == 0 else 0
                    p = P[:, (2 * t_ + half) % RING_P, col:col + n_]
                    last = nc.tensor.matmul(acc_bank[par][rows, 0:n_], VS[:, par, t_, first:first + L.group], p,
                                            start=(t_ == 0), stop=(t_ == NT - 1), tile_position=(0, L.group * g),
                                            skip_group_check=True)
                    if L.n == 0 and half == 1:
                        last = nc.tensor.matmul(acc_bank[par][rows, n_:2 * n_], ones[0:KT, 0:L.group], p, start=False,
                                                stop=(t_ == NT - 1), tile_position=(0, L.group * g), skip_group_check=True)
                last.then_inc(A["pv"], 1)

            def sums(A, L, b, par):
                for half in range(2 if L.n == 1 else 1):
                    need(pe, A[f"sum{half}"], (NT - 1) * (b + 1))
                n_ = HS * L.group // 128
                for g in range(128 // L.group if L.n == 1 else 2):
                    half, col = divmod(g * n_, HALF)
                    last = nc.tensor.matmul(L.sums(bank, acc_bank, par)[L.group * g:L.group * g + L.group], ones[0:KT, 0:L.group],
                                            SP[:, half, col:col + n_], start=(L.n == 1), stop=True,
                                            tile_position=(0, L.group * g), skip_group_check=True)
                last.then_inc(A["sums_mm"], 1)

            def attend(A, L, s, par, output):
                scores(A, L, s, par, 0)
                scores(A, L, s, par, 1)
                for p in range(NH2):
                    if p == SUMS_AT[L.n] and not (isinstance(s, int) and s == 0):
                        sums(A, L, s - 1, 1 - par)
                    if p + 2 < NH2:
                        scores(A, L, s, par, p + 2)
                    for kind, c, ahead, bk, after in L.items(s)[p]:
                        if after is not None:
                            after = (*after[0:2], s + after[2])
                        item(A, L, kind, c, bk, after, s + ahead, (par + ahead) % 2)
                    t_, odd = divmod(p - 1 - LAG[L.n], 2)
                    if odd == 0 and t_ >= 0:
                        values(A, L, s, par, t_)
                    elif odd == 0 and not (isinstance(s, int) and s == 0):
                        values(A, L, s - 1, 1 - par, NT + t_)
                    if isinstance(s, int) and s == B - 1 and p in OUT_AT:
                        output(OUT_AT.index(p))
                if not exists(s, 1):
                    for t_ in range((NH2 - 2 - LAG[L.n]) // 2 + 1, NT):
                        values(A, L, s, par, t_)

            def prepare(A, L, places):
                for items in places:
                    for kind, c, b, bk, after in items:
                        item(A, L, kind, c, bk, after, b, b)

            pe.wait_ge(x_in, counts["x_in"])
            pe.wait_ge(k_in, counts["k_in"])
            prepare(A0, L0, L0.before[:QUERIES_AT])
            pe.wait_ge(E["z_ready"], 1)
            done(tokens_transposed(z, bank[2]), "tok_tr")
            pe.wait_ge(w_in, counts["w_in"])
            pe.wait_ge(fill, 2)
            pe.wait_ge(E["zT_ready"], 1)
            for g in range(4):
                done(nc.tensor.matmul(q0_bank[g][:, 0:TOK], wq0[:, g].rearrange("p r n -> p (r n)"), zT[:],
                                      start=True, stop=True), "q0_proj")
            pe.wait_ge(E["q0_stacked"], 4)
            pe.wait_ge(E["q0_masked"], 4)
            pe.wait_ge(fill, 7)
            pe.wait_ge(E["identb_ready"], 1)
            prepare(A0, L0, L0.before[QUERIES_AT:])
            pe.wait_ge(fill, 9)

            def output0(i):
                pe.wait_ge(E["wo0_ready"], 1)
                pe.wait_ge(E["acc_divided"], 1 + i // (NTT - 1))
                for j in range(4):
                    last = nc.tensor.matmul(bank[0][0:RT, i * 128:i * 128 + 128], O2[:, j, i * RT:i * RT + RT], wo0[:, j, :],
                                            start=(i == 0 and j == 0), stop=(j == 3), skip_group_check=True)
                if i == NTT - 1:
                    done(last, "wo0_done")

            steps(pe, lambda s, par: attend(A0, L0, s, par, output0))
            sums(A0, L0, B - 1, 1)

            pe.wait_ge(bc_in, BC_IN)
            prepare(A1, L1, L1.before[0:1])
            output0(NTT - 1)
            prepare(A1, L1, L1.before[1:3])
            pe.wait_ge(E["z_ready"], 2)
            done(tokens_transposed(z, bank[2]), "tok_tr")
            pe.wait_ge(E["zT_ready"], 2)
            for i in range(NTT):
                last = nc.tensor.matmul(bank[3][0:RT, i * NE:i * NE + NE], zT[:, i * RT:i * RT + RT], gate_w[:],
                                        start=True, stop=True)
            done(last, "logits_done")

            def down(e):
                if e >= 1:
                    pe.wait_ge(E["expert_added"], e)
                pe.wait_ge(E["hidden_ready"], FC * e + FC)
                for i in range(NTT):
                    for c in range(FC):
                        last = nc.tensor.matmul(bank[6][0:RT, i * 128:i * 128 + 128], hT[:, e % 2, c, i * RT:i * RT + RT],
                                                w2[:, e, c, :], start=(i == 0 and c == 0), stop=(c == FC - 1),
                                                skip_group_check=True)
                done(last, "expert_out")

            prepare(A1, L1, L1.before[3:QUERIES_AT])
            need(pe, A1["v_ready"], NCH)

            def weighed(e):
                pe.wait_ge(E["xw_ready"], e + 1)
                if e >= 2:
                    pe.wait_ge(E["xwT_ready"], e - 1)
                done(tokens_transposed(xw[:, e % 2], bank[e % 2]), "xw_tr")

            weighed(0)
            for e in range(NE):
                pe.wait_ge(E["xwT_ready"], e + 1)
                for c in range(FC):
                    if e >= 1:
                        pe.wait_ge(E["hidden_ready"], FC * (e - 1) + c + 1)
                    done(nc.tensor.matmul(bank[2 + c][:, 0:TOK], w1[:, e, c * 128:c * 128 + 128], xwT[:, e % 2, :],
                                          start=True, stop=True), "up_done")
                if e + 1 < NE:
                    weighed(e + 1)
                if e == 2:
                    pe.wait_ge(E["wabs_ready"], 2)
                    done(nc.tensor.matmul(bank[7][:, 0:2], ones[:], wqs[:, 0:2], start=True, stop=True), "wmean_done")
                if e >= 1:
                    down(e - 1)
                if e == 3:
                    pe.wait_ge(E["wmean_read"], 1)
                    for i in range(NTT):
                        last = nc.tensor.transpose(bank[7][0:NE, i * RT:i * RT + RT], sm[:, 7, i, :], ident[0:RT, 0:RT])
                    done(last, "disp_tr")
                if e == 4:
                    pe.wait_ge(E["dispT_ready"], 1)
                    for i in range(NTT):
                        last = nc.tensor.matmul(bank[7][0:RT, i * 128:i * 128 + 128], dispT[:, i * RT:i * RT + RT], b2[:],
                                                start=True, stop=True)
                    done(last, "b2_done")
            down(NE - 1)

            pe.wait_ge(E["z_ready"], 3)
            done(tokens_transposed(z, bank[2]), "tok_tr")
            pe.wait_ge(E["zT_ready"], 3)

            def query(h):
                if h >= 3:
                    pe.wait_ge(E["q1_lo"], h - 2)
                done(nc.tensor.matmul(q1_bank[h % 3][:, 0:TOK], wq1[:, h].rearrange("p a n -> p (a n)"), zT[:],
                                      start=True, stop=True), "q1_proj")

            def gate(c):
                pe.wait_ge(E["q1_lo"], H)
                if c >= 2:
                    pe.wait_ge(E["ff_silu"], c - 1)
                nc.tensor.matmul(bank[2 + 2 * (c % 2)][:, 0:TOK], wff1[:, c, :], zT[:], start=True, stop=True)
                done(nc.tensor.matmul(bank[3 + 2 * (c % 2)][:, 0:TOK], wff1[:, FC + c, :], zT[:], start=True, stop=True), "ff_proj")

            for kind, c in first_queries():
                if kind == "Q":
                    query(c)
                elif kind == "M":
                    rt, j = L1.max_chunk(c, 0)
                    if j == 0:
                        pe.wait_ge(E["q1_hi"], (128 * (rt + 1) - 1) // S + 1)
                    item(A1, L1, "M", c, None, None, 0, 0)
                else:
                    gate(c)
            pe.wait_ge(fill, 12)
            item(A1, L1, "R", 0, 7, ("V", 2, 0), 0, 0)
            pe.wait_ge(E["ff_silu"], FC)

            def output1(i):
                for k in (*range(H // 2, H // 2 + FC), *range(H // 2)):
                    if k == 0:
                        pe.wait_ge(A1["normed"], 2 * i + 2)
                    elif i == NTT - 1 and k < H // 2 and k % (H // 2 // OUT_PARTS) == 0:
                        pe.wait_ge(A1["normed"], 2 * i + 2 + k // (H // 2 // OUT_PARTS))
                    lhsT = O2[:, k, i * RT:i * RT + RT] if k < H // 2 else sT(k - H // 2)[:, i * RT:i * RT + RT]
                    rhs = wo1[:, k, :] if k < H // 2 else wff2[:, k - H // 2, :]
                    last = nc.tensor.matmul(bank[0][0:RT, i * 128:i * 128 + 128], lhsT, rhs, start=(i == 0 and k == H // 2),
                                            stop=(k == H // 2 - 1), skip_group_check=True)
                if i == NTT - 1:
                    done(last, "out1_done")

            steps(pe, lambda s, par: attend(A1, L1, s, par, output1))
            sums(A1, L1, B - 1, 1)

            output1(NTT - 1)

            pe.wait_ge(E["xq_ready"], 1)
            done(tokens_transposed(moe, bank[0]), "tok_tr")
            pe.wait_ge(E["zT_ready"], 4)
            for c in range(FC):
                done(nc.tensor.matmul(bank[2 + c][:, 0:TOK], bw1[:, c * 128:c * 128 + 128], zT[:], start=True, stop=True), "lin1_done")
            pe.wait_ge(E["conv_done"], FC)
            for c in range(FC):
                pe.wait_ge(E["silu_done"], c + 1)
                for i in range(NTT):
                    last = nc.tensor.transpose(bank[2 + i][0:RT, c * 128:c * 128 + 128], sT(c)[:, i * RT:i * RT + RT], ident[:])
                    if c == FC - 1:
                        done(last, "back_tr")
            for i in range(NTT):
                pe.wait_ge(E["hq_ready"], i + 1)
                for c in range(FC):
                    last = nc.tensor.transpose(hq_bank(c)[:, i * RT:i * RT + RT], q2[:, i, c * 128:c * 128 + 128],
                                               identb[0:RT, 0:RT])
                    if i == NTT - 1:
                        done(last, "hq_tr")
            for c in range(FC):
                pe.wait_ge(E[("hqT_even", "hqT_odd")[c % 2]], c // 2 + 1)
                for i in range(NTT):
                    last = nc.tensor.matmul(bank[2][0:RT, i * 128:i * 128 + 128], hqT(c)[:, i * RT:i * RT + RT],
                                            bw2t[:, c, :], start=(i == 0 and c == 0), stop=(c == FC - 1), skip_group_check=True)
            done(last, "lin2_done")


def kernel(**inputs):
    import numpy as np
    import concourse.bacc as bacc
    from concourse.bass_utils import run_bass_kernel_spmd

    arrays = {k: np.ascontiguousarray(v) for k, v in inputs.items()}
    for new, old in (("wkT", "L0_xattn_Wk"), ("wvT", "L0_xattn_Wv"), ("wqT", "L0_xattn_Wq"), ("woT", "L0_xattn_Wo"),
                     ("bw1T", "L1_ffn_w1"), ("bw2T", "L1_ffn_w2")):
        arrays[new] = np.ascontiguousarray(arrays.pop(old).T)
    arrays["ctxT"] = np.ascontiguousarray(arrays["ctx_1024"].transpose(0, 2, 1))
    arrays["c_ident"] = np.eye(128, dtype=np.float32)
    p = np.arange(128)
    arrays["c_qmask"] = ((p[:, None] % 32) // DK0 == np.arange(4)).astype(np.float32)
    head = 2 * np.arange(2)[None, :] + np.arange(RT)[:, None] // S
    arrays["c_mmask0"] = -(head[:, :, None] == np.arange(32)).astype(np.float32)
    arrays["c_mmask1"] = -np.tile(np.arange(32) == 0, (128, 1)).astype(np.float32)
    arrays["c_iota8"] = np.tile(np.arange(NE, 0, -1, dtype=np.float32), (RT, NTT, 1))
    arrays["c_iota1"] = np.tile(np.arange(1, NE + 1, dtype=np.float32), (RT, NTT, 1))

    nc = bacc.Bacc("TRN2", target_bir_lowering=False, num_devices=1)
    t = {k: nc.dram_tensor(f"in_{k}", a.shape, mybir.dt.from_np(a.dtype), kind="ExternalInput").ap()
         for k, a in arrays.items()}
    out = nc.dram_tensor("out", (B, S, D), fp32, kind="ExternalOutput").ap()
    build(nc, t, out)
    r = run_bass_kernel_spmd(nc, [{f"in_{k}": a for k, a in arrays.items()}], core_ids=[0])
    return r.results[0]["out"]
```
